# Optimizing a Trainium2 kernel written in Bass

```python
import numpy as np
import jax
import jax.numpy as jnp

def _softmax(x, axis=-1):
    return jax.nn.softmax(x, axis=axis)

def _gelu(x):
    return jax.nn.gelu(x, approximate=True)

def _silu(x):
    return jax.nn.silu(x)

def _sigmoid(x):
    return jax.nn.sigmoid(x)

def _layernorm(x, axis=-1, eps=1e-05):
    m = jnp.mean(x, axis=axis, keepdims=True)
    v = jnp.var(x, axis=axis, keepdims=True)
    return (x - m) / jnp.sqrt(v + eps)

def _scatter_add(tgt, idx, src, axis=0):
    return tgt.at[idx].add(src)

def _segment_sum(src, seg, n):
    return jax.ops.segment_sum(src, seg, n)
kernel_name = 'mk_adj_preln_d4_adj_r2_2b8be6'

def setup_inputs(seed: int=0):
    np.random.seed(seed)
    _w = jnp.asarray

    def _rec_inputs():
        import jax
        import jax.numpy as jnp
        _gk = jax.random.key(seed)
        x = -0.000929 + 1 * jax.random.normal(jax.random.fold_in(_gk, 1), (4096, 128), jnp.float32)
        _a = jax.random.bernoulli(jax.random.fold_in(_gk, 2), 0.000488281, (4096, 4096))
        _a = jnp.logical_or(_a, jnp.eye(4096, dtype=bool))
        _af = _a.astype(jnp.float32)
        _af = _af * jax.random.uniform(jax.random.fold_in(_gk, 3), (4096, 4096), jnp.float32, 0.05, 1)
        adj = _af
        return (x, adj)
    x, adj = _rec_inputs()

    def _L0_gnn_setup():
        import jax, jax.numpy as jnp
        import numpy as np
        N, H, HEADS = (2048, 128, 3)
        ALPHA = 0.2
        NEG_INF = -9000000000000000.0

        def _sign_adj(key, n, density):
            k1, k2 = jax.random.split(key)
            mask = jax.random.uniform(k1, (n, n)) < density
            sign = jnp.where(jax.random.uniform(k2, (n, n)) < 0.5, -1.0, 1.0)
            adj = jnp.where(mask, sign, 0.0).astype(jnp.float32)
            idx = jnp.arange(n)
            return adj.at[idx, idx].set(1.0)

        def _gru_cell(x, hstate, Wih, Whh, bih, bhh):
            gi = x @ Wih.T + bih
            gh = hstate @ Whh.T + bhh
            ir, iz, inn = jnp.split(gi, 3, axis=1)
            hr, hz, hn = jnp.split(gh, 3, axis=1)
            r = jax.nn.sigmoid(ir + hr)
            z = jax.nn.sigmoid(iz + hz)
            n = jnp.tanh(inn + r * hn)
            return (1.0 - z) * n + z * hstate

        def _gat_head(h, node_adj, edge_adj, W, a):
            hW = h @ W
            hp = (node_adj > 0).astype(hW.dtype) @ hW
            hm = (node_adj < 0).astype(hW.dtype) @ hW
            e_plus = jax.nn.leaky_relu(jnp.concatenate([hp, hm], axis=1) @ a, ALPHA)[:, 0]
            e_minus = jax.nn.leaky_relu(jnp.concatenate([hm, hp], axis=1) @ a, ALPHA)[:, 0]
            att = jnp.where(edge_adj > 0, e_plus[None, :], NEG_INF)
            att = jnp.where(edge_adj < 0, e_minus[None, :], att)
            att = jax.nn.softmax(att, axis=1)
            return att * edge_adj @ hW
        key = jax.random.key(seed)
        ks = jax.random.split(key, 16)
        std = 0.01
        gain = 1.414
        return {'h': jax.random.normal(ks[0], (N, H), jnp.float32), 'node_adj': _sign_adj(ks[1], N, 0.005), 'edge_adj': _sign_adj(ks[2], N, 0.005), 'gat_W': jax.random.normal(ks[3], (HEADS, H, H), jnp.float32) * (gain / np.sqrt(H, dtype=np.float32)), 'gat_a': jax.random.normal(ks[4], (HEADS, 2 * H, 1), jnp.float32) * 0.1, 'edge_Wih': jax.random.normal(ks[5], (3 * H, H), jnp.float32) * std, 'edge_Whh': jax.random.normal(ks[6], (3 * H, H), jnp.float32) * std, 'edge_bih': jnp.zeros((3 * H,), jnp.float32), 'edge_bhh': jnp.zeros((3 * H,), jnp.float32), 'node_Wih': jax.random.normal(ks[7], (3 * H, H), jnp.float32) * std, 'node_Whh': jax.random.normal(ks[8], (3 * H, H), jnp.float32) * std, 'node_bih': jnp.zeros((3 * H,), jnp.float32), 'node_bhh': jnp.zeros((3 * H,), jnp.float32)}
    _L0_gnn_all = _L0_gnn_setup()
    _L0_gnn_in = {k: v for k, v in _L0_gnn_all.items() if k in ('gat_W', 'gat_a', 'edge_Wih', 'edge_Whh', 'edge_bih', 'edge_bhh', 'node_Wih', 'node_Whh', 'node_bih', 'node_bhh')}
    del _L0_gnn_all

    def _L1_gnn_setup():
        import jax, jax.numpy as jnp
        import numpy as np
        MIN_NORM = 1e-15
        BALL_EPS = 1e-05
        C_IN = 1.0
        C_OUT = 1.0

        def _artanh(x):
            x = jnp.clip(x, -1.0 + 1e-07, 1.0 - 1e-07)
            return 0.5 * (jnp.log1p(x) - jnp.log1p(-x))

        def _norm(x):
            return jnp.maximum(jnp.linalg.norm(x, axis=-1, keepdims=True), MIN_NORM)

        def proj(x, c):
            norm = _norm(x)
            maxnorm = (1.0 - BALL_EPS) / jnp.sqrt(c)
            return jnp.where(norm > maxnorm, x / norm * maxnorm, x)

        def expmap0(u, c):
            sc = jnp.sqrt(c)
            un = _norm(u)
            return jnp.tanh(sc * un) * u / (sc * un)

        def logmap0(p, c):
            sc = jnp.sqrt(c)
            pn = _norm(p)
            return _artanh(sc * pn) * p / (sc * pn)

        def mobius_matvec(m, x, c):
            sc = jnp.sqrt(c)
            xn = _norm(x)
            mx = x @ m.T
            mxn = _norm(mx)
            res = jnp.tanh(mxn / xn * _artanh(sc * xn)) * mx / (mxn * sc)
            zero_row = jnp.all(mx == 0, axis=-1, keepdims=True)
            return jnp.where(zero_row, jnp.zeros((), dtype=res.dtype), res)

        def mobius_add(x, y, c):
            x2 = jnp.sum(x * x, axis=-1, keepdims=True)
            y2 = jnp.sum(y * y, axis=-1, keepdims=True)
            xy = jnp.sum(x * y, axis=-1, keepdims=True)
            num = (1.0 + 2.0 * c * xy + c * y2) * x + (1.0 - c * x2) * y
            denom = 1.0 + 2.0 * c * xy + c * c * x2 * y2
            return num / jnp.maximum(denom, MIN_NORM)
        key = jax.random.key(seed)
        k1, k2, k3, k4 = jax.random.split(key, 4)
        N, D_IN, D_OUT = (4096, 128, 128)
        x = proj(0.05 * jax.random.normal(k1, (N, D_IN), dtype=jnp.float32), C_IN)
        adj = jax.random.uniform(k2, (N, N), dtype=jnp.float32)
        adj = adj / jnp.sum(adj, axis=1, keepdims=True)
        bound = np.sqrt(2.0) * np.sqrt(6.0 / (D_IN + D_OUT))
        weight = jax.random.uniform(k3, (D_OUT, D_IN), dtype=jnp.float32, minval=-bound, maxval=bound)
        bias = 0.01 * jax.random.normal(k4, (D_OUT,), dtype=jnp.float32)
        return {'x': x, 'adj': adj, 'weight': weight, 'bias': bias}
    _L1_gnn_all = _L1_gnn_setup()
    _L1_gnn_in = {k: v for k, v in _L1_gnn_all.items() if k in ('weight', 'bias')}
    del _L1_gnn_all

    def _L2_gnn_setup():
        import jax, jax.numpy as jnp
        import numpy as np
        N = 4096
        IN_F = 128
        OUT_F = 128
        ALPHA = 0.2
        key = jax.random.key(seed)
        k_x, k_adj, k_w, k_as, k_ad = jax.random.split(key, 5)
        x = jax.random.normal(k_x, (N, IN_F), dtype=jnp.float32)
        adj = (jax.random.uniform(k_adj, (N, N)) < 0.01).astype(jnp.float32)
        lim_w = float(np.sqrt(6.0 / (IN_F + OUT_F)))
        W = jax.random.uniform(k_w, (OUT_F, IN_F), minval=-lim_w, maxval=lim_w, dtype=jnp.float32)
        lim_a = float(np.sqrt(6.0 / (1 + OUT_F)))
        attn_src = jax.random.uniform(k_as, (1, OUT_F), minval=-lim_a, maxval=lim_a, dtype=jnp.float32)
        attn_dst = jax.random.uniform(k_ad, (1, OUT_F), minval=-lim_a, maxval=lim_a, dtype=jnp.float32)
        return {'x': x, 'adj': adj, 'W': W, 'attn_src': attn_src, 'attn_dst': attn_dst}
    _L2_gnn_all = _L2_gnn_setup()
    _L2_gnn_in = {k: v for k, v in _L2_gnn_all.items() if k in ('W', 'attn_src', 'attn_dst')}
    del _L2_gnn_all

    def _L3_gnn_setup():
        import jax, jax.numpy as jnp
        import numpy as np
        N = 4096
        C = 128
        key = jax.random.key(seed)
        k1, k2, k3 = jax.random.split(key, 3)
        x = jax.random.normal(k1, (N, C), dtype=jnp.float32)
        evals = jax.random.uniform(k2, (N,), dtype=jnp.float32)
        evecs = jax.random.normal(k3, (N, N), dtype=jnp.float32)
        t = jnp.ones((1,), dtype=jnp.float32)
        return {'x': x, 'evals': evals, 'evecs': evecs, 't': t}
    _L3_gnn_all = _L3_gnn_setup()
    _L3_gnn_in = {k: v for k, v in _L3_gnn_all.items() if k in ('evals', 't')}
    del _L3_gnn_all
    return {'x': x, 'adj': adj, 'L0_gnn_gat_W': _L0_gnn_in['gat_W'], 'L0_gnn_gat_a': _L0_gnn_in['gat_a'], 'L0_gnn_edge_Wih': _L0_gnn_in['edge_Wih'], 'L0_gnn_edge_Whh': _L0_gnn_in['edge_Whh'], 'L0_gnn_edge_bih': _L0_gnn_in['edge_bih'], 'L0_gnn_edge_bhh': _L0_gnn_in['edge_bhh'], 'L0_gnn_node_Wih': _L0_gnn_in['node_Wih'], 'L0_gnn_node_Whh': _L0_gnn_in['node_Whh'], 'L0_gnn_node_bih': _L0_gnn_in['node_bih'], 'L0_gnn_node_bhh': _L0_gnn_in['node_bhh'], 'L1_gnn_weight': _L1_gnn_in['weight'], 'L1_gnn_bias': _L1_gnn_in['bias'], 'L2_gnn_W': _L2_gnn_in['W'], 'L2_gnn_attn_src': _L2_gnn_in['attn_src'], 'L2_gnn_attn_dst': _L2_gnn_in['attn_dst'], 'L3_gnn_evals': _L3_gnn_in['evals'], 'L3_gnn_t': _L3_gnn_in['t']}

def reference(x, adj, L0_gnn_gat_W, L0_gnn_gat_a, L0_gnn_edge_Wih, L0_gnn_edge_Whh, L0_gnn_edge_bih, L0_gnn_edge_bhh, L0_gnn_node_Wih, L0_gnn_node_Whh, L0_gnn_node_bih, L0_gnn_node_bhh, L1_gnn_weight, L1_gnn_bias, L2_gnn_W, L2_gnn_attn_src, L2_gnn_attn_dst, L3_gnn_evals, L3_gnn_t):
    import jax
    import jax.numpy as jnp

    def _L0_gnn_ref(h, node_adj, edge_adj, gat_W, gat_a, edge_Wih, edge_Whh, edge_bih, edge_bhh, node_Wih, node_Whh, node_bih, node_bhh):
        import jax, jax.numpy as jnp
        import numpy as np
        N, H, HEADS = (2048, 128, 3)
        ALPHA = 0.2
        NEG_INF = -9000000000000000.0

        def _sign_adj(key, n, density):
            k1, k2 = jax.random.split(key)
            mask = jax.random.uniform(k1, (n, n)) < density
            sign = jnp.where(jax.random.uniform(k2, (n, n)) < 0.5, -1.0, 1.0)
            adj = jnp.where(mask, sign, 0.0).astype(jnp.float32)
            idx = jnp.arange(n)
            return adj.at[idx, idx].set(1.0)

        def _gru_cell(x, hstate, Wih, Whh, bih, bhh):
            gi = x @ Wih.T + bih
            gh = hstate @ Whh.T + bhh
            ir, iz, inn = jnp.split(gi, 3, axis=1)
            hr, hz, hn = jnp.split(gh, 3, axis=1)
            r = jax.nn.sigmoid(ir + hr)
            z = jax.nn.sigmoid(iz + hz)
            n = jnp.tanh(inn + r * hn)
            return (1.0 - z) * n + z * hstate

        def _gat_head(h, node_adj, edge_adj, W, a):
            hW = h @ W
            hp = (node_adj > 0).astype(hW.dtype) @ hW
            hm = (node_adj < 0).astype(hW.dtype) @ hW
            e_plus = jax.nn.leaky_relu(jnp.concatenate([hp, hm], axis=1) @ a, ALPHA)[:, 0]
            e_minus = jax.nn.leaky_relu(jnp.concatenate([hm, hp], axis=1) @ a, ALPHA)[:, 0]
            att = jnp.where(edge_adj > 0, e_plus[None, :], NEG_INF)
            att = jnp.where(edge_adj < 0, e_minus[None, :], att)
            att = jax.nn.softmax(att, axis=1)
            return att * edge_adj @ hW
        dn = jnp.diag(node_adj)
        de = jnp.diag(edge_adj)
        idx = jnp.arange(node_adj.shape[0])
        node_adj_norm = node_adj.at[idx, idx].add(-dn)
        edge_adj_norm = edge_adj.at[idx, idx].add(-de)
        node_support = node_adj_norm @ h
        edge_output = _gru_cell(node_support, h, edge_Wih, edge_Whh, edge_bih, edge_bhh)
        edge_support = _gat_head(h, node_adj_norm, edge_adj_norm, gat_W[0], gat_a[0])
        for i in range(1, HEADS):
            edge_support = edge_support + _gat_head(h, node_adj_norm, edge_adj_norm, gat_W[i], gat_a[i])
        edge_support = edge_support / HEADS
        node_output = _gru_cell(edge_support, h, node_Wih, node_Whh, node_bih, node_bhh)
        return de[:, None] * edge_output + dn[:, None] * node_output

    def _L1_gnn_ref(x, adj, weight, bias):
        import jax, jax.numpy as jnp
        import numpy as np
        MIN_NORM = 1e-15
        BALL_EPS = 1e-05
        C_IN = 1.0
        C_OUT = 1.0

        def _artanh(x):
            x = jnp.clip(x, -1.0 + 1e-07, 1.0 - 1e-07)
            return 0.5 * (jnp.log1p(x) - jnp.log1p(-x))

        def _norm(x):
            return jnp.maximum(jnp.linalg.norm(x, axis=-1, keepdims=True), MIN_NORM)

        def proj(x, c):
            norm = _norm(x)
            maxnorm = (1.0 - BALL_EPS) / jnp.sqrt(c)
            return jnp.where(norm > maxnorm, x / norm * maxnorm, x)

        def expmap0(u, c):
            sc = jnp.sqrt(c)
            un = _norm(u)
            return jnp.tanh(sc * un) * u / (sc * un)

        def logmap0(p, c):
            sc = jnp.sqrt(c)
            pn = _norm(p)
            return _artanh(sc * pn) * p / (sc * pn)

        def mobius_matvec(m, x, c):
            sc = jnp.sqrt(c)
            xn = _norm(x)
            mx = x @ m.T
            mxn = _norm(mx)
            res = jnp.tanh(mxn / xn * _artanh(sc * xn)) * mx / (mxn * sc)
            zero_row = jnp.all(mx == 0, axis=-1, keepdims=True)
            return jnp.where(zero_row, jnp.zeros((), dtype=res.dtype), res)

        def mobius_add(x, y, c):
            x2 = jnp.sum(x * x, axis=-1, keepdims=True)
            y2 = jnp.sum(y * y, axis=-1, keepdims=True)
            xy = jnp.sum(x * y, axis=-1, keepdims=True)
            num = (1.0 + 2.0 * c * xy + c * y2) * x + (1.0 - c * x2) * y
            denom = 1.0 + 2.0 * c * xy + c * c * x2 * y2
            return num / jnp.maximum(denom, MIN_NORM)
        h = proj(mobius_matvec(weight, x, C_IN), C_IN)
        hyp_bias = proj(expmap0(bias[None, :], C_IN), C_IN)
        h = proj(mobius_add(h, hyp_bias, C_IN), C_IN)
        x_tangent = logmap0(h, C_IN)
        support_t = adj @ x_tangent
        h = proj(expmap0(support_t, C_IN), C_IN)
        xt = jax.nn.relu(logmap0(h, C_IN))
        return proj(expmap0(xt, C_OUT), C_OUT)

    def _L2_gnn_ref(x, adj, W, attn_src, attn_dst):
        import jax, jax.numpy as jnp
        import numpy as np
        N = 4096
        IN_F = 128
        OUT_F = 128
        ALPHA = 0.2
        h = x @ W.T
        a_src = (h * attn_src).sum(axis=-1)
        a_dst = (h * attn_dst).sum(axis=-1)
        scores = a_src[None, :] + a_dst[:, None]
        mask = (adj > 0).astype(h.dtype)
        s = jnp.where(scores > 0, scores, ALPHA * scores) * mask
        s = s - jnp.max(s, axis=1, keepdims=True)
        e = jnp.exp(s) * mask
        w = e / (jnp.sum(e, axis=1, keepdims=True) + 1e-08)
        out = w @ h
        return jax.nn.elu(out)

    def _L3_gnn_ref(x, evals, evecs, t):
        import jax, jax.numpy as jnp
        import numpy as np
        N = 4096
        C = 128
        t_eff = jnp.clip(t[0], 1e-08, None)
        x_spec = jnp.einsum('nk,nc->kc', evecs, x)
        coefs = jnp.exp(-evals * t_eff)[:, None]
        out = jnp.einsum('nk,kc->nc', evecs, coefs * x_spec)
        return out
    h = jnp.maximum(_layernorm(x, axis=-1), 0.0)
    x = x + _L0_gnn_ref(h, adj, adj, L0_gnn_gat_W, L0_gnn_gat_a, L0_gnn_edge_Wih, L0_gnn_edge_Whh, L0_gnn_edge_bih, L0_gnn_edge_bhh, L0_gnn_node_Wih, L0_gnn_node_Whh, L0_gnn_node_bih, L0_gnn_node_bhh)
    h = jnp.maximum(_layernorm(x, axis=-1), 0.0)
    x = x + _L1_gnn_ref(h, adj, L1_gnn_weight, L1_gnn_bias)
    h = jnp.maximum(_layernorm(x, axis=-1), 0.0)
    x = x + _L2_gnn_ref(h, adj, L2_gnn_W, L2_gnn_attn_src, L2_gnn_attn_dst)
    h = jnp.maximum(_layernorm(x, axis=-1), 0.0)
    x = x + _L3_gnn_ref(h, L3_gnn_evals, adj, L3_gnn_t)
    return x

_drawn_inputs = setup_inputs


def setup_inputs(seed=0):
    import zlib

    import numpy as np

    out = dict(_drawn_inputs(seed))
    spreads = {'L0_gnn_edge_bih': (0.0, 0.306),
     'L0_gnn_edge_bhh': (0.0, 0.586),
     'L0_gnn_node_bih': (0.0, 0.354),
     'L0_gnn_node_bhh': (0.0, 0.534)}
    factors = {'L0_gnn_gat_W': 7.163,
     'L0_gnn_gat_a': 8.0,
     'L0_gnn_edge_Wih': 2.81,
     'L0_gnn_edge_Whh': 5.672,
     'L0_gnn_node_Wih': 7.683,
     'L0_gnn_node_Whh': 5.725,
     'L1_gnn_bias': 8.0}
    for name, (base, spread) in spreads.items():
        noise = np.random.default_rng([zlib.crc32(name.encode()), seed]).standard_normal(out[name].shape)
        drawn = base * np.exp(spread * noise) if base else spread * noise
        out[name] = jnp.asarray(drawn.astype(out[name].dtype))
    for name, factor in factors.items():
        out[name] = (out[name] * factor).astype(out[name].dtype)
    return out
```

```python
from contextlib import ExitStack

import concourse.bass as bass
from concourse import mybir

F32 = mybir.dt.float32
BF16 = mybir.dt.bfloat16
I32 = mybir.dt.int32
ALU = mybir.AluOpType
ACT = mybir.ActivationFunctionType
AX = mybir.AxisListType

P = 128
N = 4096
C = 128
T = N // P
CH = 512
Q = N // CH
B = CH // P
G = T // B
SLOT = B * CH
HALF = N // 2
HEADS = 3
N_LOADS = 24
FAR = 3e38
BIG = 1e30
TINY = 1e-15
MAXNORM = 1.0 - 1e-5
CLIP = 1.0 - 2.0 ** -23
SLOPE = 0.2
VC = 1 + 3 * 2 * HEADS


class Chain:

    def __init__(self, engine, sem):
        self.engine, self.sem, self.at, self.n = engine, sem, 0, 0

    def __call__(self, instruction):
        self.n += 1
        instruction.then_inc(self.sem, 1)
        self.engine.wait_ge(self.sem, self.at + self.n)

    def enter(self, i, per):
        self.kept, self.per = self.at + self.n, per
        self.at, self.n = i * per + self.kept, 0

    def leave(self, times):
        assert self.n == self.per, (self.n, self.per)
        self.at, self.n = self.kept + times * self.per, 0


def s_flat(s, i):
    return s[:, 3 * i:3 * i + 3, :].rearrange("p a t -> p (a t)")


def build(nc, x, adj, adjT, diag, gatW, gatWT, gata, wih, whh, bih, bhh, w1, bias1, w2, att_s, att_d,
          evals, t_in, ident_in, notI_in, sel_in, out):
    PASS_SUPPORT, PASS_MAX, PASS_HEADS, PASS_HYP, PASS_GATMAX, PASS_GAT, PASS_SPEC, PASS_BACK = range(8)

    ctx = ExitStack()
    with ctx:
        def sb(name, shape, dt=F32):
            return ctx.enter_context(nc.sbuf_tensor(name, shape, dt))

        def sem(name):
            return ctx.enter_context(nc.semaphore(name))

        banks = [ctx.enter_context(nc.psum_tensor(f"bank{i}", [P, CH], F32)) for i in range(8)]

        arena = sb("arena", [P, 188 * 256])

        def at(kb, *dims, dt=F32):
            n = 1
            for d in dims:
                n *= d
            words = n if dt == F32 else n // 2
            start = int(kb * 256)
            v = arena[:, start:start + words]
            if dt != F32:
                v = v.bitcast(dt)
            if len(dims) == 1:
                return v
            names = "abcd"[:len(dims)]
            return v.rearrange(f"p ({' '.join(names)}) -> p {' '.join(names)}", **dict(zip(names, dims)))

        ring = [at(8 * s, SLOT) for s in range(G)]
        ring_all = at(0, G * SLOT)
        groups = [r.rearrange("p (b i) -> p b i", b=B) for r in ring]
        X = at(64, T, C)
        R = 80
        H = at(R, T, C)
        HT = at(R + 16, N)
        mask_pos = [at(R + 32 + 4 * i, B, CH, dt=BF16) for i in range(2)]
        mask_neg = [at(R + 40 + 4 * i, B, CH, dt=BF16) for i in range(2)]
        sup_c, pos_c, neg_c, ep, em, dd, scaled, scaled_m = (at(R + 48 + 2 * i, CH) for i in range(8))
        gwT = at(R + 64, HEADS * C)
        V, VR = at(R + 66, T, 2 * HEADS), at(R + 67, T, 2 * HEADS)
        V19 = at(R + 68, T, VC, dt=BF16)
        negmax = at(R + 70, CH)[0:1, :]
        gw = at(R + 104, HEADS * C)
        NM, DEN = at(R + 106, 2, T * HEADS), at(R + 106.75, 2, T * HEADS)
        e_bc = at(R + 32, 2 * HEADS, HALF)
        block_bias = at(R + 80, HALF)
        neg_bias = at(R + 88, HALF)
        logits = [at(R, HALF), at(R + 8, HALF), at(R + 96, HALF)]
        nm_c = at(R, HEADS, CH)
        sup_l, att_c, gr, gz, gn = (at(R + 6 + 2 * i, CH) for i in range(5))
        hW = at(R + 32, T, HEADS * C)
        probs = [at(R + 80 + 8 * i, B, CH) for i in range(3)]
        gt, so = at(R + 104, CH), at(R + 106, CH)
        M1 = at(R + 32, T, C)
        TMP = at(R + 48, T, C)
        ACC = at(R + 64, T, C)
        chunk = at(R + 80, CH)
        src_bc = at(R + 16, N)
        g_bias, g_junk = at(R + 82, HALF), at(R + 90, HALF)
        dst_c = at(R + 82, 2, CH)
        den_c = at(R + 102, CH)[0:1, :]
        gat_p = [at(R + o, B, CH) for o in (16, 24, 86, 94)]

        ident = sb("ident", [P, P])
        not_i = sb("not_i", [P, 15 * P], BF16)
        selp = sb("selp", [VC, 8])
        selm = sb("selm", [VC, 8])
        wx = [sb(f"wih{i}", [P, 3 * C]) for i in range(2)]
        wh = [sb(f"whh{i}", [P, 3 * C]) for i in range(2)]
        ga = sb("ga", [P, 2 * HEADS])
        U = sb("U", [P, 2 * HEADS])
        bi = sb("bi", [P, 2, 3])
        bh = sb("bh", [P, 2, 3])
        bsum = sb("bsum", [P, 2, 3])
        w1s = sb("w1s", [P, C])
        w2s = sb("w2s", [P, C])
        avec = sb("avec", [P, 4, C])
        dg = sb("dg", [P, T])
        ev = sb("ev", [P, T])
        tv = sb("tv", [P, 1])
        ecol = sb("ecol", [P, T, 8])
        flag = sb("flag", [1, 1])
        flag_i = sb("flag_i", [1, 1], I32)
        nmx = sb("nmx", [P, G * HEADS])
        nmf = sb("nmf", [P, 3, HEADS * T])
        rows = sb("rows", [HEADS * T, P])
        s = sb("s", [P, 20, T])
        ones = sb("ones", [P, 1])

        sup_d = nc.dram_tensor("sup_d", (P, N), F32, kind="Internal").ap()
        e_d = nc.dram_tensor("e_d", (2 * HEADS, N), F32, kind="Internal").ap()
        nm_d = nc.dram_tensor("nm_d", (HEADS * T, P), F32, kind="Internal").ap()
        gat_d = nc.dram_tensor("gat_d", (3 * T, P), F32, kind="Internal").ap()

        names = """const_loaded dve_chain neg_chain ln_var ln_sd h_ready tiles_turned turn_copied
            u_ready v_ready v_copied v19_ready masks_ready support_done support_copied support_stored
            edges_summed edges_ready edges_stored edge_cols_turned edge_cols_copied neg_known flag_ready
            e_broadcast logits_ready logits_used row_max_final den_scaled den_ready nm_turned nm_rows_ready
            nm_stored nm_loaded nm_used hw_ready hw_copied probs_ready probs_free heads_ready exponents_ready
            att_copied sup_loaded gates_done gate_r gate_z gate_n_in gate_n gru_out gru_turned x_updated
            mx_done mx_copied norms_ready norms_rooted tanh_in tanh_out log_in log_out
            tangent_ready chunk_evacuated chunk_turned chunk_stored acc_used
            gat_cols_turned gat_rows_ready gat_rows_stored src_broadcast gat_max_done dst_loaded
            dst_used gat_parts node_gru_out gat_slope_ready gat_logit_ready gat_exp_ready gat_w_ready gat_w_free den_out
            den_turned exp_in exp_out coef_ready spec_ready ready_to_store out_stored ones_ready
            pool_settled pe_settled act_settled dve_settled""".split()
        S = {n: sem(n) for n in names}
        loaded = [sem(f"tile_loaded{i}") for i in range(G)]
        freed = [sem(f"tile_freed{i}") for i in range(G)]

        x_v = x.rearrange("(t p) c -> p t c", p=P)
        out_v = out.rearrange("(t p) c -> p t c", p=P)
        natural = adj.rearrange("(r p) j -> p r j", p=P)
        streams = {PASS_SUPPORT: adjT, PASS_HEADS: adjT, PASS_HYP: adjT, PASS_GAT: adjT, PASS_SPEC: adj, PASS_BACK: adjT}

        def settle(engine, name):
            engine.sem_inc(S[name], 1)

        block = ctx.enter_context(nc.Block())

        @block.sync
        def _(sp):
            def load(p, i, g, src):
                sp.wait_ge(freed[g], i + (8 * p + 1))
                dst = ring[g] if p in (PASS_MAX, PASS_GATMAX) else groups[g]
                sp.dma_start(dst, src).then_inc(loaded[g], 16)

            for g in range(G):
                sp.sem_inc(freed[g], 1)
            for p in range(8):
                if p in (PASS_MAX, PASS_GATMAX):
                    for half in range(2):
                        with sp.Fori(0, 4) as i:
                            for g in range(G):
                                load(p, i + 4 * half, g,
                                     natural[:, bass.ds(i * G + g, 1), half * HALF:(half + 1) * HALF]
                                     .rearrange("p r j -> p (r j)"))
                else:
                    v = streams[p].rearrange("(t p) i -> p t i", p=P)
                    with sp.Fori(0, Q) as q:
                        for g in range(G):
                            load(p, q, g, v[:, B * g:B * g + B, bass.ds(q * CH, CH)])

        @block.gpsimd
        def _(pool):
            pool.memset(ones[:], 1.0).then_inc(S["ones_ready"], 1)
            for name, n in (("logits_used", 3), ("probs_free", 3), ("gat_w_free", 4)):
                for _ in range(n):
                    pool.engine_nop().then_inc(S[name], 1)
            loads = [(X, x_v), (ident[:], ident_in), (not_i[:], notI_in), (selp[:], sel_in[0]), (selm[:], sel_in[1]),
                     (gw, gatW), (gwT, gatWT), (ga[:], gata), (w1s[:], w1), (w2s[:], w2),
                     (avec[:, 0, :], bias1), (avec[:, 1, :], att_s), (avec[:, 2, :], att_d),
                     (dg[:], diag), (ev[:], evals), (tv[:], t_in)]
            for i in range(2):
                loads += [(wx[i][:], wih[i]), (wh[i][:], whh[i]), (bi[:, i, :], bih[i]), (bh[:, i, :], bhh[i])]
            assert len(loads) == N_LOADS
            for dst, src in loads:
                pool.dma_start(dst, src).then_inc(S["const_loaded"], 16)

            with pool.Fori(0, Q) as q:
                pool.wait_ge(S["support_copied"], 3 * q + 1)
                settle(pool, "pool_settled")
                pool.dma_start(sup_d[:, bass.ds(q * CH, CH)], sup_c).then_inc(S["support_stored"], 16)
                pool.wait_ge(S["edges_ready"], q + 1)
                settle(pool, "pool_settled")
                pool.dma_start(e_d[0:HEADS, bass.ds(q * CH, CH)], ep[0:HEADS, :]).then_inc(S["edges_stored"], 16)
                pool.dma_start(e_d[HEADS:2 * HEADS, bass.ds(q * CH, CH)], dd[0:HEADS, :]).then_inc(S["edges_stored"], 16)
            pool.wait_ge(S["edges_stored"], 32 * Q)
            pool.wait_ge(S["edge_cols_turned"], Q)
            pool.wait_ge(S["flag_ready"], 1)
            for half in range(2):
                if half:
                    pool.wait_ge(S["logits_ready"], 4 * G * HEADS)
                for r in range(2 * HEADS):
                    pool.dma_start(e_bc[:, r, :], e_d[r, half * HALF:(half + 1) * HALF].partition_broadcast(P))\
                        .then_inc(S["e_broadcast"], 16)
            pool.wait_ge(S["nm_rows_ready"], 1)
            pool.dma_start(nm_d, rows[:]).then_inc(S["nm_stored"], 16)
            pool.wait_ge(S["nm_stored"], 16)
            pool.wait_ge(S["support_stored"], 16 * Q)
            nm_v = nm_d.rearrange("(h t) p -> h (t p)", h=HEADS)

            def load_nm(q):
                for h in range(HEADS):
                    pool.dma_start(nm_c[:, h, :], nm_v[h, bass.ds(q * CH, CH)].partition_broadcast(P))\
                        .then_inc(S["nm_loaded"], 16)

            def load_support(q):
                pool.dma_start(sup_l, sup_d[:, bass.ds(q * CH, CH)]).then_inc(S["sup_loaded"], 16)

            load_nm(0)
            load_support(0)
            with pool.Fori(0, Q - 1) as q:
                pool.wait_ge(S["nm_used"], q + 1)
                settle(pool, "pool_settled")
                load_nm(q + 1)
                pool.wait_ge(S["gru_out"], 2 * q + 1)
                settle(pool, "pool_settled")
                load_support(q + 1)

            pool.wait_ge(S["gat_rows_ready"], 1)
            pool.dma_start(gat_d[0:T, :], rows[0:T, :]).then_inc(S["gat_rows_stored"], 16)
            pool.wait_ge(S["gat_rows_stored"], 16)
            pool.dma_start(src_bc, gat_d[0:T, :].rearrange("t p -> (t p)").partition_broadcast(P))\
                .then_inc(S["src_broadcast"], 16)
            pool.wait_ge(S["gat_rows_ready"], 2)
            pool.dma_start(gat_d[T:3 * T, :], rows[0:2 * T, :]).then_inc(S["gat_rows_stored"], 16)
            pool.wait_ge(S["gat_rows_stored"], 32)
            dst_v = gat_d[T:3 * T, :].rearrange("(h t) p -> h (t p)", h=2)

            def load_dst(q):
                for h in range(2):
                    pool.dma_start(dst_c[:, h, :], dst_v[h, bass.ds(q * CH, CH)].partition_broadcast(P))\
                        .then_inc(S["dst_loaded"], 16)

            load_dst(0)
            with pool.Fori(0, Q - 1) as q:
                pool.wait_ge(S["dst_used"], q + 1)
                settle(pool, "pool_settled")
                load_dst(q + 1)
            pool.wait_ge(S["ready_to_store"], 1)
            pool.dma_start(out_v, X).then_inc(S["out_stored"], 16)
            pool.wait_ge(S["out_stored"], 16)

        @block.tensor
        def _(pe):
            pe.wait_ge(S["const_loaded"], 16 * N_LOADS)
            pe.wait_ge(S["ones_ready"], 1)
            turned = [0]

            def turn(src, n):
                for k in range(n // B):
                    if turned[0] >= 2:
                        pe.wait_ge(S["turn_copied"], turned[0] - 1)
                    for b in range(B):
                        last = pe.transpose(banks[turned[0] % 2][:, b * P:(b + 1) * P], src[:, B * k + b, :], ident[:])
                    last.then_inc(S["tiles_turned"], 1)
                    turned[0] += 1
                pe.wait_ge(S["turn_copied"], turned[0])

            def project(w, u):
                for k in range(G):
                    if k >= 2:
                        pe.wait_ge(S["mx_copied"], G * u + k - 1)
                    for b in range(B):
                        t = B * k + b
                        last = pe.matmul(banks[2 + k % 2][:, b * P:(b + 1) * P], HT[:, t * P:(t + 1) * P], w,
                                         start=True, stop=True)
                    last.then_inc(S["mx_done"], 1)

            def product(p, u, stationary):
                with pe.Fori(0, Q) as q:
                    for g in range(G):
                        pe.wait_ge(loaded[g], q * 16 + 16 * (8 * p + 1))
                        for b in range(B):
                            last = pe.matmul(banks[0][:], stationary[:, B * g + b, :], groups[g][:, b, :],
                                             start=(g == 0 and b == 0), stop=(g == G - 1 and b == B - 1))
                        last.then_inc(freed[g], 1)
                    turn_chunk(q, u)

            def turn_chunk(q, u):
                pe.wait_ge(S["chunk_evacuated"], q + (8 * u + 1))
                for b in range(B):
                    last = pe.transpose(banks[1][:, b * P:(b + 1) * P], chunk[:, b * P:(b + 1) * P], ident[:])
                last.then_inc(S["chunk_turned"], 1)

            for h in range(HEADS):
                last = pe.matmul(banks[4][:, 2 * h:2 * h + 2], gwT[:, h * C:(h + 1) * C], ga[:, 2 * h:2 * h + 2],
                                 start=True, stop=True)
            last.then_inc(S["u_ready"], 1)
            pe.wait_ge(S["h_ready"], 1)
            turn(H, T)
            pe.wait_ge(S["u_ready"], 2)
            for t in range(T):
                last = pe.matmul(banks[5][:, 6 * t:6 * t + 6], HT[:, t * P:(t + 1) * P], U[:], start=True, stop=True)
            last.then_inc(S["v_ready"], 1)
            pe.wait_ge(S["v19_ready"], 1)

            with pe.Fori(0, Q) as q:
                for g in range(G):
                    pe.wait_ge(S["masks_ready"], q * (2 * G) + 2 * (g + 1))
                    for b in range(B):
                        t = B * g + b
                        first, end = t == 0, t == T - 1
                        pe.matmul(banks[2][:], H[:, t, :], groups[g][:, b, :], start=first, stop=end)
                        pe.matmul(banks[3][0:VC, :], V19[:, t, :], mask_pos[g % 2][:, b, :], start=first, stop=end)
                        last = pe.matmul(banks[4][0:VC, :], V19[:, t, :], mask_neg[g % 2][:, b, :], start=first, stop=end)
                    last.then_inc(freed[g], 1)
                pe.wait_ge(S["support_copied"], q * 3 + 3)
                settle(pe, "pe_settled")
                pe.matmul(banks[5][0:4, :], selp[:, 0:4], pos_c[0:VC, :], start=True, stop=False)
                pe.matmul(banks[5][0:4, :], selm[:, 0:4], neg_c[0:VC, :], start=False, stop=True)
                pe.matmul(banks[6][0:3, :], selp[:, 4:7], pos_c[0:VC, :], start=True, stop=False)
                pe.matmul(banks[6][0:3, :], selm[:, 4:7], neg_c[0:VC, :], start=False, stop=True)\
                    .then_inc(S["edges_summed"], 1)
                pe.wait_ge(S["edges_ready"], q + 1)
                settle(pe, "pe_settled")
                for b in range(B):
                    pe.transpose(banks[7][:, 8 * b:8 * b + 4], ep[0:4, b * P:(b + 1) * P], ident[0:4, 0:4])
                    last = pe.transpose(banks[7][:, 8 * b + 4:8 * b + 7], dd[0:3, b * P:(b + 1) * P], ident[0:3, 0:3])
                last.then_inc(S["edge_cols_turned"], 1)

            pe.wait_ge(S["den_ready"], 2)
            pe.transpose(banks[0][0:HEADS * T, 0:P], nmf[:, 2, :], ident[:]).then_inc(S["nm_turned"], 1)
            for t in range(T):
                if t >= 2:
                    pe.wait_ge(S["hw_copied"], t - 1)
                pe.matmul(banks[1 + t % 2][:, 0:HEADS * C], HT[:, t * P:(t + 1) * P], gw, start=True, stop=True)\
                    .then_inc(S["hw_ready"], 1)
            pe.wait_ge(S["hw_copied"], T)

            with pe.Fori(0, Q) as q:
                for g in range(G):
                    for h in range(HEADS):
                        pe.wait_ge(S["heads_ready"], q * (G * HEADS) + (HEADS * g + h + 1))
                        for b in range(B):
                            last = pe.matmul(banks[0][:], hW[:, B * g + b, h * C:(h + 1) * C], probs[h][:, b, :],
                                             start=(g == 0 and h == 0 and b == 0),
                                             stop=(g == G - 1 and h == HEADS - 1 and b == B - 1))
                        last.then_inc(S["probs_free"], 1)
                hT = HT[:, bass.ds(q * CH, CH)]
                for cell, xin in enumerate((sup_l, att_c)):
                    if cell == 0:
                        pe.wait_ge(S["sup_loaded"], q * 16 + 16)
                    else:
                        pe.wait_ge(S["att_copied"], q + 1)
                        pe.wait_ge(S["gru_out"], q * 2 + 1)
                    for gate in range(2):
                        pe.matmul(banks[2 + gate][:], wx[cell][:, gate * C:(gate + 1) * C], xin, start=True, stop=False)
                        pe.matmul(banks[2 + gate][:], wh[cell][:, gate * C:(gate + 1) * C], hT, start=False, stop=True)
                    pe.matmul(banks[4][:], wx[cell][:, 2 * C:], xin, start=True, stop=True)
                    pe.matmul(banks[5][:], wh[cell][:, 2 * C:], hT, start=True, stop=True).then_inc(S["gates_done"], 1)
                pe.wait_ge(S["gru_out"], q * 2 + 2)
                for b in range(B):
                    last = pe.transpose(banks[6][:, b * P:(b + 1) * P], so[:, b * P:(b + 1) * P], ident[:])
                last.then_inc(S["gru_turned"], 1)

            pe.wait_ge(S["h_ready"], 2)
            turn(H, T)
            project(w1s[:], 0)
            pe.wait_ge(S["tangent_ready"], 1)
            product(PASS_HYP, 0, M1)

            pe.wait_ge(S["h_ready"], 3)
            turn(H, T)
            project(w2s[:], 1)
            pe.wait_ge(S["gat_cols_turned"], 1)
            pe.transpose(banks[2][0:T, 0:P], s[:, 0, :], ident[:]).then_inc(S["gat_cols_turned"], 1)
            pe.wait_ge(S["gat_max_done"], 1)
            pe.transpose(banks[2][0:2 * T, 0:P], s[:, 4:6, :].rearrange("p a t -> p (a t)"), ident[:])\
                .then_inc(S["gat_cols_turned"], 1)
            with pe.Fori(0, Q) as q:
                for g in range(G):
                    pe.wait_ge(S["gat_w_ready"], q * G + (g + 1))
                    for b in range(B):
                        first, end = g == 0 and b == 0, g == G - 1 and b == B - 1
                        pe.matmul(banks[3][0:1, :], ones[:], gat_p[g % 4][:, b, :], start=first, stop=end)
                        last = pe.matmul(banks[0][:], M1[:, B * g + b, :], gat_p[g % 4][:, b, :], start=first, stop=end)
                    last.then_inc(S["gat_w_free"], 1)
                turn_chunk(q, 1)
                pe.wait_ge(S["den_out"], q + 1)
                settle(pe, "pe_settled")
                for b in range(B):
                    last = pe.transpose(banks[4][:, b:b + 1], den_c[0:1, b * P:(b + 1) * P], ident[0:1, 0:1])
                last.then_inc(S["den_turned"], 1)

            pe.wait_ge(S["h_ready"], 4)
            product(PASS_SPEC, 2, H)
            pe.wait_ge(S["spec_ready"], 1)
            product(PASS_BACK, 3, M1)

        @block.scalar
        def _(act):
            def root(l):
                act.wait_ge(S["ln_var"], l + 1)
                act.activation(s[:, 2, :], s[:, 1, :], ACT.Sqrt).then_inc(S["ln_sd"], 1)

            turned = [0]

            def turn_copy(n):
                for k in range(n // B):
                    act.wait_ge(S["tiles_turned"], turned[0] + 1)
                    act.activation(HT[:, k * CH:(k + 1) * CH], banks[turned[0] % 2][:], ACT.Copy)\
                        .then_inc(S["turn_copied"], 1)
                    turned[0] += 1

            def project_copy(u):
                for k in range(G):
                    act.wait_ge(S["mx_done"], G * u + k + 1)
                    act.activation(M1[:, B * k:B * k + B, :].rearrange("p b c -> p (b c)"), banks[2 + k % 2][:], ACT.Copy)\
                        .then_inc(S["mx_copied"], 1)

            def evacuate(q, u, done, at_least):
                act.wait_ge(done, at_least)
                act.activation(chunk, banks[0][:], ACT.Copy).then_inc(S["chunk_evacuated"], 1)
                act.wait_ge(S["chunk_turned"], q + (8 * u + 1))
                act.activation(ACC[:, bass.ds(q * B, B), :].rearrange("p b c -> p (b c)"), banks[1][:], ACT.Copy)\
                    .then_inc(S["chunk_stored"], 1)

            def collect(p, u):
                with act.Fori(0, Q) as q:
                    evacuate(q, u, freed[G - 1], q + (8 * p + 2))

            root(0)
            act.wait_ge(S["u_ready"], 1)
            act.activation(U[:], banks[4][:, 0:6], ACT.Copy).then_inc(S["u_ready"], 1)
            turn_copy(T)
            act.wait_ge(S["v_ready"], 1)
            act.activation(V.rearrange("p t v -> p (t v)"), banks[5][:, 0:6 * T], ACT.Copy).then_inc(S["v_copied"], 1)

            with act.Fori(0, Q) as q:
                act.wait_ge(freed[G - 1], q + 2)
                act.activation(sup_c, banks[2][:], ACT.Copy).then_inc(S["support_copied"], 1)
                act.activation(pos_c[0:VC, :], banks[3][0:VC, :], ACT.Copy).then_inc(S["support_copied"], 1)
                act.activation(neg_c[0:VC, :], banks[4][0:VC, :], ACT.Copy).then_inc(S["support_copied"], 1)
                act.wait_ge(S["support_stored"], q * 16 + 16)
                act.wait_ge(S["edges_summed"], q + 1)
                act.wait_ge(S["neg_known"], q + 1)
                settle(act, "act_settled")

            with act.Fori(0, 8) as i:
                for g in range(G):
                    for h in range(HEADS):
                        k = HEADS * g + h
                        act.wait_ge(S["logits_ready"], i * (G * HEADS) + (k + 1))
                        col = DEN.rearrange("p a n -> p (a n)")[:, bass.ds(i * (G * HEADS) + k, 1)]
                        act.activation(logits[k % 3], logits[k % 3], ACT.Exp, bias=nmx[:, k:k + 1], scale=-1.0,
                                       accum_out=col).then_inc(S["logits_used"], 1)
            act.wait_ge(S["row_max_final"], 1)
            act.activation(s_flat(s, 0), s_flat(s, 0), ACT.Exp).then_inc(S["den_scaled"], 1)
            act.activation(s_flat(s, 1), s_flat(s, 1), ACT.Exp).then_inc(S["den_scaled"], 1)
            act.wait_ge(S["den_ready"], 1)
            act.activation(nmf[:, 1, :], nmf[:, 1, :], ACT.Ln).then_inc(S["den_scaled"], 1)
            act.wait_ge(S["nm_turned"], 1)
            act.activation(rows[:], banks[0][0:HEADS * T, 0:P], ACT.Copy).then_inc(S["nm_rows_ready"], 1)
            for t in range(T):
                act.wait_ge(S["hw_ready"], t + 1)
                act.activation(hW[:, t, :], banks[1 + t % 2][:, 0:HEADS * C], ACT.Copy).then_inc(S["hw_copied"], 1)

            with act.Fori(0, Q) as q:
                for k in range(G * HEADS):
                    act.wait_ge(S["exponents_ready"], q * (G * HEADS * B) + B * (k + 1))
                    flat = probs[k % HEADS].rearrange("p b i -> p (b i)")
                    act.activation(flat, flat, ACT.Exp).then_inc(S["probs_ready"], 1)
                act.wait_ge(S["probs_free"], q * (G * HEADS) + (G * HEADS + 3))
                act.activation(att_c, banks[0][:], ACT.Copy, scale=1.0 / HEADS).then_inc(S["att_copied"], 1)
                for cell in range(2):
                    act.wait_ge(S["gates_done"], q * 2 + (cell + 1))
                    act.activation(gr, banks[2][:], ACT.Tanh, bias=bsum[:, cell, 0:1], scale=0.5).then_inc(S["gate_r"], 1)
                    act.activation(gz, banks[3][:], ACT.Tanh, bias=bsum[:, cell, 1:2], scale=0.5).then_inc(S["gate_z"], 1)
                    act.wait_ge(S["gate_n_in"], q * 2 + (cell + 1))
                    act.activation(gn, gt, ACT.Tanh, bias=bi[:, cell, 2:3]).then_inc(S["gate_n"], 1)
                    act.wait_ge(S["gru_out"], q * 2 + (cell + 1))

            hyp = {"root": 0, "tanh": 0, "log": 0}

            def row_root(a, b_):
                hyp["root"] += 1
                act.wait_ge(S["norms_ready"], hyp["root"])
                act.activation(s[:, b_, :], s[:, a, :], ACT.Sqrt).then_inc(S["norms_rooted"], 1)

            def row_tanh(a, b_):
                hyp["tanh"] += 1
                act.wait_ge(S["tanh_in"], hyp["tanh"])
                act.activation(s[:, b_, :], s[:, a, :], ACT.Tanh).then_inc(S["tanh_out"], 1)

            def row_log():
                hyp["log"] += 1
                act.wait_ge(S["log_in"], hyp["log"])
                act.activation(s[:, 11, :], s[:, 11, :], ACT.Ln).then_inc(S["log_out"], 1)

            root(1)
            turn_copy(T)
            project_copy(0)
            row_root(3, 4)
            row_root(5, 6)
            row_log()
            row_tanh(8, 8)
            row_root(13, 13)
            row_tanh(14, 14)
            row_root(3, 4)
            row_log()
            collect(PASS_HYP, 0)
            row_root(3, 4)
            row_root(5, 6)
            row_tanh(8, 8)
            row_log()
            row_tanh(8, 8)

            root(2)
            turn_copy(T)
            project_copy(1)
            for k in range(2):
                act.wait_ge(S["gat_cols_turned"], 2 + k)
                if k:
                    act.wait_ge(S["gat_rows_stored"], 16)
                act.activation(rows[0:(k + 1) * T, :], banks[2][0:(k + 1) * T, 0:P], ACT.Copy).then_inc(S["gat_rows_ready"], 1)
            act.wait_ge(S["gat_w_free"], 4)
            with act.Fori(0, Q) as q:
                act.wait_ge(S["dst_loaded"], q * 32 + 32)
                for g in range(G + 1):
                    if g < G:
                        act.wait_ge(S["gat_w_free"], q * G + (g + 1))
                        for b in range(B):
                            act.activation(gat_p[g % 4][:, b, :], dst_c[:, 1, :], ACT.Identity, scale=1.0,
                                           bias=s[:, 8, B * g + b:B * g + b + 1]).then_inc(S["gat_slope_ready"], 1)
                    if g:
                        act.wait_ge(S["gat_logit_ready"], q * (G * B) + B * g)
                        flat = gat_p[(g - 1) % 4].rearrange("p b i -> p (b i)")
                        act.activation(flat, flat, ACT.Exp).then_inc(S["gat_exp_ready"], 1)
                act.wait_ge(S["gat_w_free"], q * G + (G + 4))
                act.activation(den_c, banks[3][0:1, :], ACT.Copy).then_inc(S["den_out"], 1)
                evacuate(q, 1, S["gat_w_free"], q * G + (G + 4))
                act.wait_ge(S["den_turned"], q + 1)
                act.activation(s[:, 6, :][:, bass.ds(q * B, B)], banks[4][:, 0:B], ACT.Copy).then_inc(S["acc_used"], 1)
            act.wait_ge(S["exp_in"], 1)
            act.activation(TMP.rearrange("p t c -> p (t c)"), TMP.rearrange("p t c -> p (t c)"), ACT.Exp)\
                .then_inc(S["exp_out"], 1)

            root(3)
            act.wait_ge(S["exp_in"], 2)
            act.activation(s[:, 7, :], s[:, 7, :], ACT.Exp).then_inc(S["exp_out"], 1)
            collect(PASS_SPEC, 2)
            act.wait_ge(S["spec_ready"], 1)
            collect(PASS_BACK, 3)

        @block.vector
        def _(dve):
            ch = Chain(dve, S["dve_chain"])
            neg = Chain(dve, S["neg_chain"])
            v = nc.vector

            def wide(col):
                return col.unsqueeze(2).broadcast_to([P, T, C])

            def sc(i):
                return s[:, i, :]

            def ts(o, a, s1, s2, op0, op1=ALU.bypass):
                ch(v.tensor_scalar(o, a, s1, s2, op0, op1) if s2 is not None else v.tensor_scalar(o, a, s1, None, op0))

            def tt(o, a, b_, op):
                ch(v.tensor_tensor(o, a, b_, op))

            def normalise(l):
                ch(v.tensor_reduce(sc(0), X, AX.X, ALU.add))
                ts(sc(0), sc(0), 1.0 / C, None, ALU.mult)
                tt(H, X, wide(sc(0)), ALU.subtract)
                tt(TMP, H, H, ALU.mult)
                ch(v.tensor_reduce(sc(1), TMP, AX.X, ALU.add))
                v.tensor_scalar(sc(1), sc(1), 1.0 / C, 1e-5, ALU.mult, ALU.add).then_inc(S["ln_var"], 1)
                dve.wait_ge(S["ln_sd"], l + 1)
                ch(v.reciprocal(sc(2), sc(2)))
                tt(sc(3), sc(2), sc(2), ALU.mult)
                tt(sc(3), sc(3), sc(1), ALU.mult)
                ts(sc(3), sc(3), -0.5, 1.5, ALU.mult, ALU.add)
                tt(sc(2), sc(2), sc(3), ALU.mult)
                tt(H, H, wide(sc(2)), ALU.mult)
                v.tensor_scalar(H, H, 0.0, None, ALU.max).then_inc(S["h_ready"], 1)
                dve.wait_ge(S["h_ready"], l + 1)

            dve.wait_ge(S["const_loaded"], 16 * N_LOADS)
            normalise(0)
            ch(v.memset(V19, 1.0))
            ch(v.memset(negmax, 0.0))
            tt(bsum[:], bi[:], bh[:], ALU.add)
            ts(bsum[:], bsum[:], 0.5, None, ALU.mult)
            dve.wait_ge(S["v_copied"], 1)
            for part in range(3):
                src = V if part == 0 else VR
                dst = V19[:, :, 1 + 6 * part:7 + 6 * part]
                if part < 2:
                    ch(v.tensor_copy(dst, src))
                    tt(VR, src, dst, ALU.subtract)
                else:
                    v.tensor_copy(dst, src).then_inc(S["v19_ready"], 1)

            def clear_diagonal(q, g):
                diag_ap = diagonal_blocks(g)
                m = not_i[:, bass.ds(q * P + (7 - g) * P, P)].unsqueeze(1).broadcast_to([P, B, P])
                ch(v.tensor_tensor(diag_ap, diag_ap, m, ALU.mult))

            def diagonal_blocks(g):
                step = CH + P
                return arena[:, g * SLOT:g * SLOT + B * step].rearrange("p (b k) -> p b k", k=step)[:, :, 0:P]

            with dve.Fori(0, Q) as q:
                ch.enter(q, G + 5)
                for g in range(G):
                    dve.wait_ge(loaded[g], q * 16 + 16)
                    clear_diagonal(q, g)
                    if g >= 2:
                        dve.wait_ge(freed[g - 2], q + 2)
                    else:
                        dve.wait_ge(freed[g + 6], q + 1)
                    v.tensor_scalar(mask_pos[g % 2], groups[g], 0.0, None, ALU.is_gt).then_inc(S["masks_ready"], 1)
                    v.tensor_scalar(mask_neg[g % 2], groups[g], 0.0, None, ALU.is_lt)\
                        .then_inc(S["masks_ready"], 1)
                dve.wait_ge(S["support_copied"], q * 3 + 3)
                v.tensor_tensor(negmax, negmax, neg_c[0:1, :], ALU.max).then_inc(S["neg_known"], 1)
                dve.wait_ge(S["edges_summed"], q + 1)
                dve.wait_ge(S["neg_known"], q + 1)
                ts(scaled[0:4, :], banks[5][0:4, :], SLOPE, None, ALU.mult)
                tt(ep[0:4, :], scaled[0:4, :], banks[5][0:4, :], ALU.max)
                ts(scaled_m[0:3, :], banks[6][0:3, :], SLOPE, None, ALU.mult)
                tt(em[0:3, :], scaled_m[0:3, :], banks[6][0:3, :], ALU.max)
                v.tensor_tensor(dd[0:3, :], em[0:3, :], ep[0:3, :], ALU.subtract).then_inc(S["edges_ready"], 1)
                dve.wait_ge(S["edge_cols_turned"], q + 1)
                ch(v.tensor_copy(ecol[:, bass.ds(q * B, B), 0:7],
                                 banks[7][:, 0:8 * B].rearrange("p (b k) -> p b k", k=8)[:, :, 0:7]))
                dve.wait_ge(S["edges_stored"], q * 32 + 32)
                settle(dve, "dve_settled")
            ch.leave(Q)
            ch(v.tensor_reduce(flag[:], negmax, AX.X, ALU.max))
            v.tensor_copy(flag_i[:], flag[:]).then_inc(S["flag_ready"], 1)
            dve.wait_ge(S["flag_ready"], 1)
            any_negative = dve.value_load(flag_i[0:1, 0:1], min_val=0, max_val=N)

            dve.wait_ge(S["logits_used"], 3)
            for part in range(4):
                half, on_diagonal = part // 2, part in (0, 3)
                if part % 2 == 0:
                    dve.wait_ge(S["e_broadcast"], 16 * 2 * HEADS * (half + 1))
                with dve.Fori(0, 2) as i:
                    ch.enter(i, G * (1 + on_diagonal) + 1)
                    neg.enter(i, G * (HEADS * 3 - 1))
                    for g in range(G):
                        dve.wait_ge(loaded[g], i * 16 + 16 * (8 + 2 * part + 1))
                        if on_diagonal:
                            d = ring_all[:, bass.ds(i * (G * P) + (g * SLOT + g * P), P)]
                            ch(v.tensor_tensor(d, d, not_i[:, 7 * P:8 * P], ALU.mult))
                        ch(v.tensor_scalar(block_bias, ring[g], 0.0, -BIG, ALU.is_equal, ALU.mult))
                        for h in range(HEADS):
                            k = HEADS * g + h
                            settle(dve, "dve_settled")
                            with dve.If(any_negative):
                                if h:
                                    neg(v.tensor_scalar(block_bias, ring[g], 0.0, -BIG, ALU.is_equal, ALU.mult))
                                neg(v.scalar_tensor_tensor(neg_bias, ring[g], 0.0, e_bc[:, HEADS + h, :],
                                                           ALU.is_lt, ALU.mult))
                                neg(v.tensor_tensor(block_bias, block_bias, neg_bias, ALU.add))
                                settle(dve, "dve_settled")
                            dve.wait_ge(S["logits_used"], i * (G * HEADS) + (2 * part * G * HEADS + k + 1))
                            settle(dve, "dve_settled")
                            v.tensor_tensor_reduce(logits[k % 3], block_bias, e_bc[:, h, :], -1.0, FAR,
                                                   ALU.add, ALU.min, nmx[:, k:k + 1]).then_inc(S["logits_ready"], 1)
                        dve.wait_ge(S["logits_ready"], i * (G * HEADS) + (2 * part * G * HEADS + HEADS * g + HEADS))
                        v.sem_inc(freed[g], 1)
                    col = NM.rearrange("p a n -> p (a n)")[:, bass.ds(i * (G * HEADS) + 2 * part * G * HEADS, G * HEADS)]
                    ch(v.tensor_copy(col, nmx[:]))
                ch.leave(2)
                neg.leave(2)
            rt = "p (t h) -> p h t"
            by_head = nmf[:].rearrange("p a (h t) -> p a h t", h=HEADS)
            tt(by_head[:, 0], NM[:, 0, :].rearrange(rt, h=HEADS), NM[:, 1, :].rearrange(rt, h=HEADS), ALU.min)
            f0, f1 = s_flat(s, 0), s_flat(s, 1)
            tt(f0.rearrange("p (h t) -> p h t", h=HEADS), by_head[:, 0], NM[:, 0, :].rearrange(rt, h=HEADS), ALU.subtract)
            v.tensor_tensor(f1.rearrange("p (h t) -> p h t", h=HEADS), by_head[:, 0], NM[:, 1, :].rearrange(rt, h=HEADS),
                            ALU.subtract).then_inc(S["row_max_final"], 1)
            dve.wait_ge(S["den_scaled"], 2)
            tt(f0.rearrange("p (h t) -> p h t", h=HEADS), f0.rearrange("p (h t) -> p h t", h=HEADS),
               DEN[:, 0, :].rearrange(rt, h=HEADS), ALU.mult)
            tt(f1.rearrange("p (h t) -> p h t", h=HEADS), f1.rearrange("p (h t) -> p h t", h=HEADS),
               DEN[:, 1, :].rearrange(rt, h=HEADS), ALU.mult)
            v.tensor_tensor(nmf[:, 1, :], f0, f1, ALU.add).then_inc(S["den_ready"], 1)
            dve.wait_ge(S["den_scaled"], 3)
            v.tensor_tensor(nmf[:, 2, :], nmf[:, 0, :], nmf[:, 1, :], ALU.subtract).then_inc(S["den_ready"], 1)

            dve.wait_ge(S["probs_free"], 3)
            with dve.Fori(0, Q) as q:
                ch.enter(q, G + 2 * 5 + 2)
                neg.enter(q, G * HEADS * (B + 1))
                dve.wait_ge(S["nm_loaded"], q * (16 * HEADS) + 16 * HEADS)
                for k in range(G * HEADS + 1):
                    g, h = k // HEADS, k % HEADS
                    if k < G * HEADS:
                        if h == 0:
                            dve.wait_ge(loaded[g], q * 16 + 16 * (8 * PASS_HEADS + 1))
                            clear_diagonal(q, g)
                        dve.wait_ge(S["probs_free"], q * (G * HEADS) + (k + 1))
                        settle(dve, "dve_settled")
                        with dve.If(any_negative):
                            for b in range(B):
                                neg(v.tensor_scalar(probs[h][:, b, :], groups[g][:, b, :], 0.0,
                                                    ecol[:, B * g + b, 4 + h:5 + h], ALU.is_lt, ALU.mult))
                            neg(v.tensor_tensor(probs[h], probs[h], nm_c[:, h, :].unsqueeze(1).broadcast_to([P, B, CH]),
                                                ALU.add))
                            for b in range(B):
                                v.tensor_scalar(probs[h][:, b, :], probs[h][:, b, :], ecol[:, B * g + b, h:h + 1], 0.0,
                                                ALU.add, ALU.min).then_inc(S["exponents_ready"], 1)
                        with dve.Else():
                            for b in range(B):
                                v.tensor_scalar(probs[h][:, b, :], nm_c[:, h, :], ecol[:, B * g + b, h:h + 1], 0.0,
                                                ALU.add, ALU.min).then_inc(S["exponents_ready"], 1)
                    if k:
                        g, h = (k - 1) // HEADS, (k - 1) % HEADS
                        dve.wait_ge(S["probs_ready"], q * (G * HEADS) + k)
                        v.tensor_tensor(probs[h], probs[h], groups[g], ALU.mult).then_inc(S["heads_ready"], 1)
                        if h == HEADS - 1:
                            dve.wait_ge(S["heads_ready"], q * (G * HEADS) + k)
                            v.sem_inc(freed[g], 1)
                dve.wait_ge(S["exponents_ready"], q * (G * HEADS * B) + G * HEADS * B)
                v.sem_inc(S["nm_used"], 1)
                hT = HT[:, bass.ds(q * CH, CH)]
                for cell in range(2):
                    dve.wait_ge(S["gate_r"], q * 2 + (cell + 1))
                    dve.wait_ge(S["gate_z"], q * 2 + (cell + 1))
                    ts(gr, gr, 0.5, 0.5, ALU.mult, ALU.add)
                    ts(gz, gz, 0.5, 0.5, ALU.mult, ALU.add)
                    ch(v.scalar_tensor_tensor(gt, banks[5][:], bh[:, cell, 2:3], gr, ALU.add, ALU.mult))
                    v.tensor_tensor(gt, gt, banks[4][:], ALU.add).then_inc(S["gate_n_in"], 1)
                    dve.wait_ge(S["gate_n"], q * 2 + (cell + 1))
                    tt(gt, hT, gn, ALU.subtract)
                    tt(gt, gt, gz, ALU.mult)
                    if cell == 0:
                        v.tensor_tensor(so, gt, gn, ALU.add).then_inc(S["gru_out"], 1)
                        dve.wait_ge(S["gru_out"], q * 2 + 1)
                    else:
                        v.tensor_tensor(gt, gt, gn, ALU.add).then_inc(S["node_gru_out"], 1)
                        dve.wait_ge(S["node_gru_out"], q + 1)
                        v.tensor_tensor(so, so, gt, ALU.add).then_inc(S["gru_out"], 1)
                dve.wait_ge(S["gru_turned"], q + 1)
                xq = X[:, bass.ds(q * B, B), :]
                d = dg[:, bass.ds(q * B, B)].unsqueeze(2).broadcast_to([P, B, C])
                turned = gt.rearrange("p (b c) -> p b c", b=B)
                ch(v.tensor_tensor(turned, banks[6][:].rearrange("p (b c) -> p b c", b=B), d, ALU.mult))
                ch(v.tensor_tensor(xq, xq, turned, ALU.add))
            ch.leave(Q)
            neg.leave(Q)

            hyp = {"root": 0, "tanh": 0, "log": 0}

            def rooted(ins):
                hyp["root"] += 1
                ins.then_inc(S["norms_ready"], 1)
                dve.wait_ge(S["norms_rooted"], hyp["root"])

            def tanhed(ins):
                hyp["tanh"] += 1
                ins.then_inc(S["tanh_in"], 1)
                dve.wait_ge(S["tanh_out"], hyp["tanh"])

            def squares(o, a):
                tt(TMP, a, a, ALU.mult)
                rooted(v.tensor_reduce(o, TMP, AX.X, ALU.add))

            def artanh(x_, o):
                ts(sc(9), x_, CLIP, None, ALU.min)
                tt(sc(10), sc(9), sc(9), ALU.mult)
                ts(sc(12), sc(10), 1.0 / 17, 1.0 / 15, ALU.mult, ALU.add)
                for odd in (13, 11, 9, 7, 5, 3, 1):
                    tt(sc(12), sc(12), sc(10), ALU.mult)
                    ts(sc(12), sc(12), 1.0 / odd, None, ALU.add)
                tt(sc(12), sc(12), sc(9), ALU.mult)
                ts(sc(11), sc(9), -1.0, 1.0, ALU.mult, ALU.add)
                ch(v.reciprocal(sc(11), sc(11)))
                ts(sc(10), sc(9), 1.0, None, ALU.add)
                hyp["log"] += 1
                v.tensor_tensor(sc(11), sc(11), sc(10), ALU.mult).then_inc(S["log_in"], 1)
                dve.wait_ge(S["log_out"], hyp["log"])
                ts(sc(10), sc(9), 0.25, 0.5, ALU.is_ge, ALU.mult)
                tt(sc(11), sc(11), sc(10), ALU.mult)
                ts(sc(10), sc(9), 0.25, None, ALU.is_lt)
                tt(sc(12), sc(12), sc(10), ALU.mult)
                tt(o, sc(11), sc(12), ALU.add)

            def over(o, a, b_):
                ch(v.reciprocal(sc(12), b_))
                tt(o, a, sc(12), ALU.mult)

            normalise(1)
            squares(sc(3), H)
            dve.wait_ge(S["mx_copied"], G)
            squares(sc(5), M1)
            ts(sc(4), sc(4), TINY, None, ALU.max)
            ts(sc(6), sc(6), TINY, None, ALU.max)
            artanh(sc(4), sc(7))
            over(sc(8), sc(6), sc(4))
            tanhed(v.tensor_tensor(sc(8), sc(8), sc(7), ALU.mult))
            ts(sc(8), sc(8), MAXNORM, None, ALU.min)
            over(sc(7), sc(8), sc(6))
            ch(v.tensor_tensor(avec[:, 3, :], avec[:, 0, :], avec[:, 0, :], ALU.mult))
            ch(v.memset(sc(13), 0.0))
            rooted(v.tensor_reduce(s[:, 13, 0:1], avec[:, 3, :], AX.X, ALU.add))
            ts(s[:, 13, :], s[:, 13, :], TINY, None, ALU.max)
            tanhed(v.tensor_copy(sc(14), sc(13)))
            ts(sc(14), sc(14), MAXNORM, None, ALU.min)
            over(sc(15), sc(14), sc(13))
            ch(v.tensor_scalar(avec[:, 3, :], avec[:, 0, :], s[:, 15, 0:1], None, ALU.mult))
            y = avec[:, 3, :].unsqueeze(1).broadcast_to([P, T, C])
            tt(sc(16), sc(14), sc(14), ALU.mult)
            y2 = s[:, 16, 0:1]
            tt(TMP, M1, y, ALU.mult)
            ch(v.tensor_reduce(sc(9), TMP, AX.X, ALU.add))
            tt(sc(9), sc(9), sc(7), ALU.mult)
            ts(sc(9), sc(9), 2.0, 1.0, ALU.mult, ALU.add)
            tt(sc(10), sc(8), sc(8), ALU.mult)
            ts(sc(11), sc(9), y2, None, ALU.add)
            tt(sc(11), sc(11), sc(7), ALU.mult)
            ts(sc(13), sc(10), y2, None, ALU.mult)
            tt(sc(13), sc(13), sc(9), ALU.add)
            ts(sc(13), sc(13), TINY, None, ALU.max)
            ts(sc(10), sc(10), -1.0, 1.0, ALU.mult, ALU.add)
            over(sc(11), sc(11), sc(13))
            over(sc(10), sc(10), sc(13))
            tt(M1, M1, wide(sc(11)), ALU.mult)
            tt(TMP, y, wide(sc(10)), ALU.mult)
            tt(M1, M1, TMP, ALU.add)
            squares(sc(3), M1)
            ts(sc(4), sc(4), TINY, None, ALU.max)
            ts(sc(5), sc(4), MAXNORM, None, ALU.min)
            artanh(sc(5), sc(7))
            over(sc(7), sc(7), sc(4))
            v.tensor_tensor(M1, M1, wide(sc(7)), ALU.mult).then_inc(S["tangent_ready"], 1)
            dve.wait_ge(S["chunk_stored"], 8)
            squares(sc(3), ACC)
            ts(ACC, ACC, 0.0, None, ALU.max)
            squares(sc(5), ACC)
            ts(sc(4), sc(4), TINY, None, ALU.max)
            tanhed(v.tensor_copy(sc(8), sc(4)))
            ts(sc(8), sc(8), MAXNORM, TINY, ALU.min, ALU.max)
            artanh(sc(8), sc(7))
            over(sc(7), sc(7), sc(4))
            tt(sc(5), sc(7), sc(6), ALU.mult)
            ts(sc(5), sc(5), TINY, None, ALU.max)
            tanhed(v.tensor_copy(sc(8), sc(5)))
            ts(sc(8), sc(8), MAXNORM, None, ALU.min)
            over(sc(8), sc(8), sc(5))
            tt(sc(8), sc(8), sc(7), ALU.mult)
            tt(ACC, ACC, wide(sc(8)), ALU.mult)
            tt(X, X, ACC, ALU.add)

            normalise(2)
            dve.wait_ge(S["mx_copied"], 2 * G)
            tt(TMP, M1, avec[:, 1, :].unsqueeze(1).broadcast_to([P, T, C]), ALU.mult)
            ch(v.tensor_reduce(sc(0), TMP, AX.X, ALU.add))
            tt(TMP, M1, avec[:, 2, :].unsqueeze(1).broadcast_to([P, T, C]), ALU.mult)
            ch(v.tensor_reduce(sc(1), TMP, AX.X, ALU.add))
            v.tensor_scalar(sc(8), sc(0), SLOPE, None, ALU.mult).then_inc(S["gat_cols_turned"], 1)
            dve.wait_ge(S["src_broadcast"], 16)
            for half in range(2):
                with dve.Fori(0, 4) as i:
                    ch.enter(i, 2 * G + 1)
                    for g in range(G):
                        dve.wait_ge(loaded[g], i * 16 + 16 * (8 * PASS_GATMAX + 4 * half + 1))
                        ch(v.tensor_scalar(g_bias, ring[g], 0.0, -BIG, ALU.is_le, ALU.mult))
                        settle(dve, "dve_settled")
                        ch(v.tensor_tensor_reduce(g_junk, g_bias, src_bc[:, half * HALF:(half + 1) * HALF], -1.0, FAR,
                                                  ALU.add, ALU.min, nmx[:, g:g + 1]))
                        v.sem_inc(freed[g], 1)
                    ch(v.tensor_copy(s[:, 2 + half, :][:, bass.ds(i * G, G)], nmx[:, 0:G]))
                ch.leave(4)
            tt(sc(2), sc(2), sc(3), ALU.min)
            tt(sc(2), sc(1), sc(2), ALU.subtract)
            ts(sc(3), sc(2), SLOPE, None, ALU.mult)
            tt(sc(2), sc(2), sc(3), ALU.max)
            ts(sc(3), dg[:], 0.0, None, ALU.is_gt)
            tt(sc(3), sc(3), ecol[:, :, 3], ALU.add)
            ts(sc(3), sc(3), float(N) - 0.5, -BIG, ALU.is_gt, ALU.mult)
            tt(sc(2), sc(2), sc(3), ALU.max)
            tt(sc(4), sc(1), sc(2), ALU.subtract)
            ts(sc(5), sc(1), SLOPE, None, ALU.mult)
            v.tensor_tensor(sc(5), sc(5), sc(2), ALU.subtract).then_inc(S["gat_max_done"], 1)
            with dve.Fori(0, Q) as q:
                for g in range(G + 1):
                    if g < G:
                        dve.wait_ge(S["gat_slope_ready"], q * (G * B) + B * (g + 1))
                        buf = gat_p[g % 4]
                        for b in range(B):
                            v.scalar_tensor_tensor(buf[:, b, :], dst_c[:, 0, :], s[:, 0, B * g + b:B * g + b + 1],
                                                   buf[:, b, :], ALU.add, ALU.max).then_inc(S["gat_logit_ready"], 1)
                    if g == G - 1:
                        dve.wait_ge(S["gat_logit_ready"], q * (G * B) + G * B)
                        v.sem_inc(S["dst_used"], 1)
                    if g:
                        buf = gat_p[(g - 1) % 4]
                        dve.wait_ge(loaded[g - 1], q * 16 + 16 * (8 * PASS_GAT + 1))
                        dve.wait_ge(S["gat_exp_ready"], q * G + g)
                        v.scalar_tensor_tensor(buf, groups[g - 1], 0.0, buf, ALU.is_gt, ALU.min)\
                            .then_inc(S["gat_w_ready"], 1)
                        dve.wait_ge(S["gat_w_ready"], q * G + g)
                        v.sem_inc(freed[g - 1], 1)
            dve.wait_ge(S["acc_used"], Q)
            dve.wait_ge(S["chunk_stored"], 16)
            ts(sc(6), sc(6), 1e-8, None, ALU.add)
            ch(v.reciprocal(sc(6), sc(6)))
            tt(ACC, ACC, wide(sc(6)), ALU.mult)
            v.tensor_scalar(TMP, ACC, 0.0, None, ALU.min).then_inc(S["exp_in"], 1)
            dve.wait_ge(S["exp_out"], 1)
            ts(TMP, TMP, -1.0, None, ALU.add)
            ts(ACC, ACC, 0.0, None, ALU.max)
            tt(ACC, ACC, TMP, ALU.add)
            tt(X, X, ACC, ALU.add)

            normalise(3)
            ts(tv[:], tv[:], 1e-8, -1.0, ALU.max, ALU.mult)
            v.tensor_scalar(sc(7), ev[:], tv[:, 0:1], None, ALU.mult).then_inc(S["exp_in"], 1)
            dve.wait_ge(S["exp_out"], 2)
            dve.wait_ge(S["chunk_stored"], 24)
            v.tensor_tensor(M1, ACC, wide(sc(7)), ALU.mult).then_inc(S["spec_ready"], 1)
            dve.wait_ge(S["chunk_stored"], 32)
            v.tensor_tensor(X, X, ACC, ALU.add).then_inc(S["ready_to_store"], 1)


def kernel(**inputs):
    import numpy as np
    import ml_dtypes
    import concourse.bacc as bacc
    from concourse.bass_utils import run_bass_kernel_spmd as run

    f = {k: np.asarray(v) for k, v in inputs.items()}

    def cols(a, n):
        return np.ascontiguousarray(a.reshape(n, P).T)

    def row(a):
        return np.ascontiguousarray(np.broadcast_to(a.reshape(1, C), (P, C)))

    not_i = np.ones((P, 15 * P), ml_dtypes.bfloat16)
    not_i[:, 7 * P:8 * P] = 1 - np.eye(P)
    sel = np.zeros((2, VC, 8), np.float32)
    sel[0, 0, 3] = 1
    for part in range(3):
        for h in range(HEADS):
            a1, a2 = 1 + 6 * part + 2 * h, 2 + 6 * part + 2 * h
            sel[0, a1, h] = sel[0, a2, 4 + h] = 1
            sel[1, a2, h] = sel[1, a1, 4 + h] = 1
    e, n = "L0_gnn_edge_", "L0_gnn_node_"
    arrays = {
        "x": f["x"], "adj": f["adj"], "adjT": np.ascontiguousarray(f["adj"].T),
        "diag": cols(np.diagonal(f["adj"]), T),
        "gatW": np.ascontiguousarray(f["L0_gnn_gat_W"].transpose(1, 0, 2)).reshape(C, HEADS * C),
        "gatWT": np.ascontiguousarray(f["L0_gnn_gat_W"].transpose(2, 0, 1)).reshape(C, HEADS * C),
        "gata": np.ascontiguousarray(f["L0_gnn_gat_a"].reshape(HEADS, 2, C).transpose(2, 0, 1)).reshape(C, 2 * HEADS),
        "wih": np.stack([f[e + "Wih"].T, f[n + "Wih"].T]), "whh": np.stack([f[e + "Whh"].T, f[n + "Whh"].T]),
        "bih": np.stack([cols(f[e + "bih"], 3), cols(f[n + "bih"], 3)]),
        "bhh": np.stack([cols(f[e + "bhh"], 3), cols(f[n + "bhh"], 3)]),
        "w1": np.ascontiguousarray(f["L1_gnn_weight"].T), "bias1": row(f["L1_gnn_bias"]),
        "w2": np.ascontiguousarray(f["L2_gnn_W"].T), "att_s": row(f["L2_gnn_attn_src"]),
        "att_d": row(f["L2_gnn_attn_dst"]),
        "evals": cols(f["L3_gnn_evals"], T), "t_in": np.ascontiguousarray(np.broadcast_to(f["L3_gnn_t"].reshape(1, 1), (P, 1))),
        "ident": np.eye(P, dtype=np.float32), "not_i": not_i, "sel": sel,
    }
    nc = bacc.Bacc("TRN2", target_bir_lowering=False, num_devices=1)
    aps = [nc.dram_tensor(f"in_{k}", a.shape, mybir.dt.from_np(a.dtype), kind="ExternalInput").ap() for k, a in arrays.items()]
    out = nc.dram_tensor("out_x", (N, C), F32, kind="ExternalOutput").ap()
    build(nc, *aps, out)
    r = run(nc, [{f"in_{k}": a for k, a in arrays.items()}], core_ids=[0])
    return r.results[0]["out_x"]
```

```python
from contextlib import ExitStack, nullcontext

import concourse.bass as bass
from concourse import mybir

F32 = mybir.dt.float32
BF16 = mybir.dt.bfloat16
I32 = mybir.dt.int32
ALU = mybir.AluOpType
ACT = mybir.ActivationFunctionType
AX = mybir.AxisListType

P = 128
N = 4096
C = 128
T = N // P
CH = 512
Q = N // CH
B = CH // P
G = T // B
SLOT = B * CH
HALF = N // 2
HEADS = 3
N_LOADS = 23
FAR = 3e38
BIG = 1e30
FAR_UNIT = 2.0 ** 64
STEEP = 2.0 ** 126
NEAR_UNIT = 2.0 ** -64
TINY = 1e-15
MAXNORM = 1.0 - 1e-5
CLIP = 1.0 - 2.0 ** -23
SLOPE = 0.2
NEG0 = 32
VC = 1 + 3 * 2 * HEADS


class Chain:

    def __init__(self, engine, sem):
        self.engine, self.sem, self.at, self.n = engine, sem, 0, 0

    def __call__(self, instruction):
        self.n += 1
        instruction.then_inc(self.sem, 1)
        self.engine.wait_ge(self.sem, self.at + self.n)

    def enter(self, i, per):
        self.kept, self.per = self.at + self.n, per
        self.at, self.n = i * per + self.kept, 0

    def leave(self, times):
        assert self.n == self.per, (self.n, self.per)
        self.at, self.n = self.kept + times * self.per, 0


def s_flat(s, i):
    return s[:, 3 * i:3 * i + 3, :].rearrange("p a t -> p (a t)")


def build(nc, x, adj, adjT, diag, gatW, gatWT, gata, wih, whh, bih, bhh, w1, bias1, w2, att_s, att_d,
          evals, t_in, ident_in, notI_in, sel_in, out):
    PASS_SUPPORT, PASS_MAX, PASS_HEADS, PASS_HYP, PASS_GATMAX, PASS_GAT, PASS_SPEC, PASS_BACK = range(8)

    ctx = ExitStack()
    with ctx:
        def sb(name, shape, dt=F32):
            return ctx.enter_context(nc.sbuf_tensor(name, shape, dt))

        def sem(name):
            return ctx.enter_context(nc.semaphore(name))

        banks = [ctx.enter_context(nc.psum_tensor(f"bank{i}", [P, CH], F32)) for i in range(8)]

        arena = sb("arena", [P, 188 * 256])

        def at(kb, *dims, dt=F32):
            n = 1
            for d in dims:
                n *= d
            words = n if dt == F32 else n // 2
            start = int(kb * 256)
            v = arena[:, start:start + words]
            if dt != F32:
                v = v.bitcast(dt)
            if len(dims) == 1:
                return v
            names = "abcd"[:len(dims)]
            return v.rearrange(f"p ({' '.join(names)}) -> p {' '.join(names)}", **dict(zip(names, dims)))

        ring = [at(8 * s, SLOT) for s in range(G)]
        ring_all = at(0, G * SLOT)
        groups = [r.rearrange("p (b i) -> p b i", b=B) for r in ring]
        X = at(64, T, C)
        R = 80
        H = at(R, T, C)
        HT = at(R + 16, N)
        mask_pos = [at(R + 32 + 4 * i, B, CH, dt=BF16) for i in range(2)]
        mask_neg = [at(R + 40 + 4 * i, B, CH, dt=BF16) for i in range(2)]
        sup_c = at(R + 48, CH)
        ep, dd = at(R + 32, N)[0:4, :], at(R + 50, N)[0:HEADS, :]
        slope_p, slope_m, em = (at(R + 66 + 2 * i, CH) for i in range(3))
        sums = at(R + 72, N)
        gwT = at(R + 88, HEADS * C)
        V, VR = at(R + 90, T, 2 * HEADS), at(R + 91, T, 2 * HEADS)
        V19 = at(R + 92, T, VC, dt=BF16)
        gw = at(R + 104, HEADS * C)
        NM, DEN = at(R + 106, 2, T * HEADS), at(R + 106.75, 2, T * HEADS)
        e_bc = at(R + 32, 2 * HEADS, HALF)
        no_edge, not_positive_edge = (at(R + 80 + 4 * i, HALF, dt=BF16) for i in range(2))
        signed_e = at(R + 88, HALF)
        logits = [at(R, HALF), at(R + 8, HALF), at(R + 96, HALF)]
        hW = at(R + 32, T, HEADS * C)
        probs = [at(R + o, B, CH) for o in (80, 88, 96, 0)]
        nm_c = [at(R + 16 + 6 * i, HEADS, CH) for i in range(2)]
        att_c = at(R + 28, CH)
        supT, attT = at(R + 32, N), at(R + 48, N)
        gr, gz, gn, gt = ([at(R + 64 + 8 * cell + 2 * i, CH) for cell in range(2)] for i in range(4))
        so = [at(R + 80 + 2 * i, CH) for i in range(2)]
        M1 = at(R + 32, T, C)
        TMP = at(R + 48, T, C)
        ACC = at(R + 64, T, C)
        chunk = at(R + 80, CH)
        src_bc = at(R + 16, N)
        not_positive = [at(R + 82 + 4 * i, HALF, dt=BF16) for i in range(2)]
        masked_src = at(R + 90, HALF)
        dst_all = [at(R + 48, N), at(R, N)]
        w_sum = at(R + 98, B, CH)
        den_c = at(R + 106, CH)[0:1, :]
        gat_p = [at(R + o, B, CH) for o in (16, 24, 82, 90)]

        ident = sb("ident", [P, P])
        not_i = sb("not_i", [P, 15 * P], BF16)
        sel = sb("sel", [P, 8])
        wx = [sb(f"wih{i}", [P, 3 * C]) for i in range(2)]
        wh = [sb(f"whh{i}", [P, 3 * C]) for i in range(2)]
        ga = sb("ga", [P, 2 * HEADS])
        U = sb("U", [P, 2 * HEADS])
        bi = sb("bi", [P, 2, 3])
        bh = sb("bh", [P, 2, 3])
        bsum = sb("bsum", [P, 2, 3])
        w1s = sb("w1s", [P, C])
        w2s = sb("w2s", [P, C])
        avec = sb("avec", [P, 4, C])
        dg = sb("dg", [P, T])
        ev = sb("ev", [P, T])
        tv = sb("tv", [P, 1])
        ecol = sb("ecol", [P, T, 8])
        flag = sb("flag", [NEG0 + 1, 1])
        flag_i = sb("flag_i", [NEG0 + 1, 1], I32)
        nmx = sb("nmx", [P, G * HEADS])
        nmf = sb("nmf", [P, 3, HEADS * T])
        rows = sb("rows", [HEADS * T, P])
        s = sb("s", [P, 20, T])
        ones = sb("ones", [P, 1])

        sup_d = nc.dram_tensor("sup_d", (P, N), F32, kind="Internal").ap()
        attT_d = nc.dram_tensor("attT_d", (P, CH + N), F32, kind="Internal").ap()
        hT_d = nc.dram_tensor("hT_d", (P, N), F32, kind="Internal").ap()
        e_d = nc.dram_tensor("e_d", (2 * HEADS, N), F32, kind="Internal").ap()
        nm_d = nc.dram_tensor("nm_d", (HEADS * T, P), F32, kind="Internal").ap()
        gat_d = nc.dram_tensor("gat_d", (3 * T, P), F32, kind="Internal").ap()

        names = """const_loaded dve_chain neg_chain edges_scaled blocks_cleared edge_cols_copied ln_var ln_sd h_ready tiles_turned turn_copied u_ready v_ready v_copied
            v19_ready masks_ready support_copied support_stored edges_summed edges_ready edges_stored
            edge_cols_turned flag_ready e_broadcast logits_ready logits_used row_max_final den_scaled
            den_ready nm_turned nm_rows_ready nm_stored nm_used hw_ready hw_copied probs_ready probs_free
            heads_ready exponents_ready att_copied gates_done gate_r gate_z gate_n_in gate_n gru_out
            gru_turned x_updated mx_done mx_copied norms_ready norms_rooted tanh_in tanh_out log_in log_out
            tangent_ready chunk_evacuated chunk_turned chunk_stored acc_used gat_cols_turned gat_rows_ready
            gat_rows_stored src_broadcast gat_max_done dst_loaded gat_slope_ready gat_logit_ready
            gat_exp_ready gat_w_ready gat_w_free signs_ready signs_used den_out den_turned exp_in exp_out spec_ready ready_to_store
            out_stored ones_ready hT_stored att_stored diagonal_clear last_head_ready gat_summed no_edge_ready
                       den_summed sums_cleared pool_settled pe_settled act_settled dve_settled""".split()
        S = {n: sem(n) for n in names}
        loaded = [sem(f"tile_loaded{i}") for i in range(G)]
        nm_loaded = [sem(f"nm_loaded{i}") for i in range(2)]
        cells_loaded = [sem(f"cells_loaded{i}") for i in range(2)]
        freed = [sem(f"tile_freed{i}") for i in range(G)]

        x_v = x.rearrange("(t p) c -> p t c", p=P)
        out_v = out.rearrange("(t p) c -> p t c", p=P)
        natural = adj.rearrange("(r p) j -> p r j", p=P)
        streams = {PASS_SUPPORT: adjT, PASS_HEADS: adjT, PASS_HYP: adjT, PASS_GAT: adjT, PASS_SPEC: adj, PASS_BACK: adjT}

        def settle(engine, name):
            engine.sem_inc(S[name], 1)

        block = ctx.enter_context(nc.Block())

        @block.sync
        def _(sp):
            def load(p, i, g, src):
                sp.wait_ge(freed[g], i + (8 * p + 1))
                dst = ring[g] if p in (PASS_MAX, PASS_GATMAX) else groups[g]
                sp.dma_start(dst, src).then_inc(loaded[g], 16)

            for g in range(G):
                sp.sem_inc(freed[g], 1)
            for p in range(8):
                if p in (PASS_MAX, PASS_GATMAX):
                    for half in range(2):
                        with sp.Fori(0, 4) as i:
                            for g in range(G):
                                load(p, i + 4 * half, g,
                                     natural[:, bass.ds(i * G + g, 1), half * HALF:(half + 1) * HALF]
                                     .rearrange("p r j -> p (r j)"))
                else:
                    v = streams[p].rearrange("(t p) i -> p t i", p=P)
                    with sp.Fori(0, Q) as q:
                        for g in range(G):
                            load(p, q, g, v[:, B * g:B * g + B, bass.ds(q * CH, CH)])

        @block.gpsimd
        def _(pool):
            pool.memset(ones[:], 1.0).then_inc(S["ones_ready"], 1)
            for name, n in (("logits_used", 3), ("probs_free", 4)):
                for _ in range(n):
                    pool.engine_nop().then_inc(S[name], 1)
            loads = [(X, x_v), (ident[:], ident_in), (not_i[:], notI_in), (sel[:], sel_in),
                     (gw, gatW), (gwT, gatWT), (ga[:], gata), (w1s[:], w1), (w2s[:], w2),
                     (avec[:, 0, :], bias1), (avec[:, 1, :], att_s), (avec[:, 2, :], att_d),
                     (dg[:], diag), (ev[:], evals), (tv[:], t_in)]
            for i in range(2):
                loads += [(wx[i][:], wih[i]), (wh[i][:], whh[i]), (bi[:, i, :], bih[i]), (bh[:, i, :], bhh[i])]
            assert len(loads) == N_LOADS
            for dst, src in loads:
                pool.dma_start(dst, src).then_inc(S["const_loaded"], 16)

            pool.wait_ge(S["turn_copied"], G)
            pool.dma_start(hT_d, HT).then_inc(S["hT_stored"], 16)
            with pool.Fori(0, Q) as q:
                pool.wait_ge(S["support_copied"], 3 * q + 1)
                settle(pool, "pool_settled")
                pool.dma_start(sup_d[:, bass.ds(q * CH, CH)], sup_c).then_inc(S["support_stored"], 16)
            pool.wait_ge(S["edges_scaled"], 2)
            pool.dma_start(e_d[0:HEADS, :], ep[0:HEADS, :]).then_inc(S["edges_stored"], 16)
            pool.dma_start(e_d[HEADS:2 * HEADS, :], dd).then_inc(S["edges_stored"], 16)
            pool.wait_ge(S["edges_stored"], 32)
            pool.wait_ge(S["flag_ready"], 1)
            for half in range(2):
                if half:
                    pool.wait_ge(S["logits_ready"], 4 * G * HEADS)
                for r in range(2 * HEADS):
                    pool.dma_start(e_bc[:, r, :], e_d[r, half * HALF:(half + 1) * HALF].partition_broadcast(P))\
                        .then_inc(S["e_broadcast"], 16)
                with pool.Fori(0, 2) as i:
                    for g in range(G):
                        pool.wait_ge(loaded[g], i * 16 + 16 * (8 + 6 * half + 1))
                        settle(pool, "pool_settled")
                        d = ring_all[:, bass.ds(i * (G * P) + (g * SLOT + g * P), P)]
                        pool.tensor_tensor(d, d, not_i[:, 7 * P:8 * P], ALU.mult).then_inc(S["blocks_cleared"], 1)
            pool.wait_ge(S["nm_rows_ready"], 1)
            pool.dma_start(nm_d, rows[:]).then_inc(S["nm_stored"], 16)
            pool.wait_ge(S["nm_stored"], 16)
            pool.wait_ge(S["hT_stored"], 16)
            pool.wait_ge(S["hw_copied"], T)
            nm_v = nm_d.rearrange("(h t) p -> h (t p)", h=HEADS)

            def load_nm(q, i):
                for h in range(HEADS):
                    pool.dma_start(nm_c[i][:, h, :], nm_v[h, bass.ds(q * CH, CH)].partition_broadcast(P))\
                        .then_inc(nm_loaded[i], 16)

            def weigh(q, g):
                k = HEADS * g + HEADS - 1
                pool.wait_ge(S["probs_ready"], q * (G * HEADS) + (k + 1))
                pool.wait_ge(S["diagonal_clear"], q * G + (g + 1))
                settle(pool, "pool_settled")
                pool.tensor_tensor(probs[k % 4], probs[k % 4], groups[g], ALU.mult).then_inc(S["last_head_ready"], 1)

            load_nm(0, 0)
            load_nm(1, 1)

            def weigh_pair(qq, more):
                for i in range(2):
                    q = qq * 2 + i
                    for g in range(G):
                        if g == 2:
                            with pool.If(qq) if i == 0 else nullcontext():
                                pool.wait_ge(S["att_copied"], q + 2)
                                settle(pool, "pool_settled")
                                pool.dma_start(attT_d[:, bass.ds(q * CH, CH)], att_c).then_inc(S["att_stored"], 16)
                        weigh(q, g)
                    if more:
                        pool.wait_ge(S["nm_used"], q + 1)
                        settle(pool, "pool_settled")
                        load_nm(q + 2, i)

            with pool.Fori(0, Q // 2 - 1) as qq:
                weigh_pair(qq, True)
            with pool.Fori(Q // 2 - 1, Q // 2) as qq:
                weigh_pair(qq, False)
            pool.wait_ge(S["att_copied"], Q + 2)
            pool.dma_start(attT_d[:, Q * CH:], att_c).then_inc(S["att_stored"], 16)
            pool.wait_ge(S["att_stored"], 16 * Q)
            pool.wait_ge(S["support_stored"], 16 * Q)
            pool.wait_ge(S["nm_used"], Q)
            for i in range(2):
                half = slice(i * HALF, (i + 1) * HALF)
                for dst, src in ((HT, hT_d), (supT, sup_d), (attT, attT_d[:, CH:])):
                    pool.dma_start(dst[:, half], src[:, half]).then_inc(cells_loaded[i], 16)

            pool.wait_ge(S["gat_rows_ready"], 1)
            pool.dma_start(gat_d[0:T, :], rows[0:T, :]).then_inc(S["gat_rows_stored"], 16)
            pool.wait_ge(S["gat_rows_stored"], 16)
            pool.dma_start(src_bc, gat_d[0:T, :].rearrange("t p -> (t p)").partition_broadcast(P))\
                .then_inc(S["src_broadcast"], 16)
            pool.wait_ge(S["gat_rows_ready"], 2)
            pool.dma_start(gat_d[T:3 * T, :], rows[0:2 * T, :]).then_inc(S["gat_rows_stored"], 16)
            pool.wait_ge(S["gat_rows_stored"], 32)
            dst_v = gat_d[T:3 * T, :].rearrange("(h t) p -> h (t p)", h=2)
            for h in range(2):
                pool.dma_start(dst_all[h], dst_v[h, :].partition_broadcast(P)).then_inc(S["dst_loaded"], 16)
            def sum_weights(q, first):
                for g in range(1, G):
                    pool.wait_ge(S["gat_w_ready"], q * G + (g + 1))
                    if g > 1:
                        pool.wait_ge(S["gat_summed"], q * (G - 1) + (g - 1))
                    elif not first:
                        pool.wait_ge(S["den_summed"], q)
                    settle(pool, "pool_settled")
                    pool.tensor_tensor(w_sum, gat_p[0] if g == 1 else w_sum, gat_p[g % 4], ALU.add)\
                        .then_inc(S["gat_summed"], 1)

            sum_weights(0, True)
            with pool.Fori(1, Q) as q:
                sum_weights(q, False)
            pool.wait_ge(S["ready_to_store"], 1)
            pool.dma_start(out_v, X).then_inc(S["out_stored"], 16)
            pool.wait_ge(S["out_stored"], 16)

        @block.tensor
        def _(pe):
            pe.wait_ge(S["const_loaded"], 16 * N_LOADS)
            pe.wait_ge(S["ones_ready"], 1)
            turned = [0]

            def turn(src, n):
                for k in range(n // B):
                    if turned[0] >= 2:
                        pe.wait_ge(S["turn_copied"], turned[0] - 1)
                    for b in range(B):
                        last = pe.transpose(banks[turned[0] % 2][:, b * P:(b + 1) * P], src[:, B * k + b, :], ident[:])
                    last.then_inc(S["tiles_turned"], 1)
                    turned[0] += 1
                pe.wait_ge(S["turn_copied"], turned[0])

            def project(w, u):
                for k in range(G):
                    if k >= 2:
                        pe.wait_ge(S["mx_copied"], G * u + k - 1)
                    for b in range(B):
                        t = B * k + b
                        last = pe.matmul(banks[2 + k % 2][:, b * P:(b + 1) * P], HT[:, t * P:(t + 1) * P], w,
                                         start=True, stop=True)
                    last.then_inc(S["mx_done"], 1)

            def product(p, u, stationary):
                with pe.Fori(0, Q) as q:
                    for g in range(G):
                        pe.wait_ge(loaded[g], q * 16 + 16 * (8 * p + 1))
                        for b in range(B):
                            last = pe.matmul(banks[0][:], stationary[:, B * g + b, :], groups[g][:, b, :],
                                             start=(g == 0 and b == 0), stop=(g == G - 1 and b == B - 1))
                        last.then_inc(freed[g], 1)
                    turn_chunk(q, u)

            def turn_chunk(q, u):
                pe.wait_ge(S["chunk_evacuated"], q + (8 * u + 1))
                for b in range(B):
                    last = pe.transpose(banks[1][:, b * P:(b + 1) * P], chunk[:, b * P:(b + 1) * P], ident[:])
                last.then_inc(S["chunk_turned"], 1)

            for h in range(HEADS):
                last = pe.matmul(banks[4][:, 2 * h:2 * h + 2], gwT[:, h * C:(h + 1) * C], ga[:, 2 * h:2 * h + 2],
                                 start=True, stop=True)
            last.then_inc(S["u_ready"], 1)
            pe.wait_ge(S["h_ready"], 1)
            turn(H, T)
            pe.wait_ge(S["u_ready"], 2)
            for t in range(T):
                last = pe.matmul(banks[5][:, 6 * t:6 * t + 6], HT[:, t * P:(t + 1) * P], U[:], start=True, stop=True)
            last.then_inc(S["v_ready"], 1)
            pe.wait_ge(S["v19_ready"], 1)

            with pe.Fori(0, Q) as q:
                for g in range(G):
                    pe.wait_ge(S["masks_ready"], q * (2 * G) + 2 * (g + 1))
                    for b in range(B):
                        t = B * g + b
                        first, end = t == 0, t == T - 1
                        pe.matmul(banks[2][:], H[:, t, :], groups[g][:, b, :], start=first, stop=end)
                        pe.matmul(banks[3][0:VC, :], V19[:, t, :], mask_pos[g % 2][:, b, :], start=first, stop=end)
                        last = pe.matmul(banks[4][NEG0:NEG0 + VC, :], V19[:, t, :], mask_neg[g % 2][:, b, :],
                                         start=first, stop=end)
                    last.then_inc(freed[g], 1)
                pe.wait_ge(S["support_copied"], q * 3 + 3)
            def add_parts(q, i):
                part = sums[:, bass.ds(q * CH, CH)]
                pe.matmul(banks[2 * i][0:4, :], sel[:, 0:4], part, start=True, stop=True)
                pe.matmul(banks[2 * i + 1][0:3, :], sel[:, 4:7], part, start=True, stop=True).then_inc(S["edges_summed"], 1)

            add_parts(0, 0)
            for q in range(Q):
                if q + 1 < Q:
                    if q:
                        pe.wait_ge(S["edges_ready"], q)
                    add_parts(q + 1, (q + 1) % 2)
                pe.wait_ge(S["edges_ready"], q + 1)
                if q >= 2:
                    pe.wait_ge(S["edge_cols_copied"], q - 1)
                for b in range(B):
                    cols = slice(q * CH + b * P, q * CH + (b + 1) * P)
                    pe.transpose(banks[6 + q % 2][:, 8 * b:8 * b + 4], ep[0:4, cols], ident[0:4, 0:4])
                    last = pe.transpose(banks[6 + q % 2][:, 8 * b + 4:8 * b + 7], dd[0:3, cols], ident[0:3, 0:3])
                last.then_inc(S["edge_cols_turned"], 1)

            pe.wait_ge(S["den_ready"], 2)
            pe.transpose(banks[0][0:HEADS * T, 0:P], nmf[:, 2, :], ident[:]).then_inc(S["nm_turned"], 1)
            for t in range(T):
                if t >= 2:
                    pe.wait_ge(S["hw_copied"], t - 1)
                pe.matmul(banks[1 + t % 2][:, 0:HEADS * C], HT[:, t * P:(t + 1) * P], gw, start=True, stop=True)\
                    .then_inc(S["hw_ready"], 1)
            pe.wait_ge(S["hw_copied"], T)

            for _ in range(2):
                pe.sem_inc(S["att_copied"], 1)
            with pe.Fori(0, Q // 2) as qq:
                for i in range(2):
                    q = qq * 2 + i
                    pe.wait_ge(S["att_copied"], q + 1)
                    for k in range(G * HEADS):
                        g, h = k // HEADS, k % HEADS
                        if h < HEADS - 1:
                            pe.wait_ge(S["heads_ready"], q * (G * (HEADS - 1)) + ((HEADS - 1) * g + h + 1))
                        else:
                            pe.wait_ge(S["last_head_ready"], q * G + (g + 1))
                        for b in range(B):
                            last = pe.matmul(banks[i][:], hW[:, B * g + b, h * C:(h + 1) * C], probs[k % 4][:, b, :],
                                             start=(k == 0 and b == 0), stop=(k == G * HEADS - 1 and b == B - 1))
                        last.then_inc(S["probs_free"], 1)

            def gates(q, cell):
                n = 2 * q + cell
                if q:
                    pe.wait_ge(S["gru_out"], n - 1)
                    if cell == 1:
                        pe.wait_ge(S["x_updated"], q)
                bank, chunk_q = banks[4 * cell:4 * cell + 4], slice(q * CH, (q + 1) * CH)
                xin = (supT, attT)[cell][:, chunk_q]
                for gate in range(2):
                    pe.matmul(bank[gate][:], wx[cell][:, gate * C:(gate + 1) * C], xin, start=True, stop=False)
                    pe.matmul(bank[gate][:], wh[cell][:, gate * C:(gate + 1) * C], HT[:, chunk_q], start=False, stop=True)
                pe.matmul(bank[2][:], wx[cell][:, 2 * C:], xin, start=True, stop=True)
                pe.matmul(bank[3][:], wh[cell][:, 2 * C:], HT[:, chunk_q], start=True, stop=True).then_inc(S["gates_done"], 1)

            def turn_gru(q):
                pe.wait_ge(S["gru_out"], 2 * q + 2)
                for b in range(B):
                    last = pe.transpose(banks[7][:, b * P:(b + 1) * P], so[q % 2][:, b * P:(b + 1) * P], ident[:])
                last.then_inc(S["gru_turned"], 1)

            for q in range(Q):
                if q % 4 == 0:
                    pe.wait_ge(cells_loaded[q // 4], 48)
                gates(q, 0)
                if q:
                    turn_gru(q - 1)
                gates(q, 1)
            turn_gru(Q - 1)

            pe.wait_ge(S["h_ready"], 2)
            turn(H, T)
            project(w1s[:], 0)
            pe.wait_ge(S["tangent_ready"], 1)
            product(PASS_HYP, 0, M1)

            pe.wait_ge(S["h_ready"], 3)
            turn(H, T)
            project(w2s[:], 1)
            pe.wait_ge(S["gat_cols_turned"], 1)
            pe.transpose(banks[2][0:T, 0:P], s[:, 9, :], ident[:]).then_inc(S["gat_cols_turned"], 1)
            pe.wait_ge(S["gat_max_done"], 1)
            pe.transpose(banks[2][0:2 * T, 0:P], s[:, 4:6, :].rearrange("p a t -> p (a t)"), ident[:])\
                .then_inc(S["gat_cols_turned"], 1)

            def attend(q, first):
                if not first:
                    pe.wait_ge(S["chunk_evacuated"], q + 8)
                for g in range(G):
                    pe.wait_ge(S["gat_w_ready"], q * G + (g + 1))
                    if g == 3 and not first:
                        finish(q - 1)
                    for b in range(B):
                        last = pe.matmul(banks[0][:], M1[:, B * g + b, :], gat_p[g % 4][:, b, :],
                                         start=(g == 0 and b == 0), stop=(g == G - 1 and b == B - 1))
                    last.then_inc(S["gat_w_free"], 1)
                if not first:
                    pe.wait_ge(S["den_out"], q)
                pe.wait_ge(S["gat_summed"], q * (G - 1) + (G - 1))
                for b in range(B):
                    last = pe.matmul(banks[3][0:1, :], ones[:], w_sum[:, b, :], start=(b == 0), stop=(b == B - 1))
                last.then_inc(S["den_summed"], 1)

            def finish(q):
                turn_chunk(q, 1)
                pe.wait_ge(S["den_out"], q + 1)
                settle(pe, "pe_settled")
                for b in range(B):
                    last = pe.transpose(banks[4][:, b:b + 1], den_c[0:1, b * P:(b + 1) * P], ident[0:1, 0:1])
                last.then_inc(S["den_turned"], 1)

            attend(0, True)
            with pe.Fori(1, Q) as q:
                attend(q, False)
            finish(Q - 1)

            pe.wait_ge(S["h_ready"], 4)
            product(PASS_SPEC, 2, H)
            pe.wait_ge(S["spec_ready"], 1)
            product(PASS_BACK, 3, M1)

        @block.scalar
        def _(act):
            def root(l):
                act.wait_ge(S["ln_var"], l + 1)
                act.activation(s[:, 2, :], s[:, 1, :], ACT.Sqrt).then_inc(S["ln_sd"], 1)

            turned = [0]

            def turn_copy(n):
                for k in range(n // B):
                    act.wait_ge(S["tiles_turned"], turned[0] + 1)
                    act.activation(HT[:, k * CH:(k + 1) * CH], banks[turned[0] % 2][:], ACT.Copy)\
                        .then_inc(S["turn_copied"], 1)
                    turned[0] += 1

            def project_copy(u):
                for k in range(G):
                    act.wait_ge(S["mx_done"], G * u + k + 1)
                    act.activation(M1[:, B * k:B * k + B, :].rearrange("p b c -> p (b c)"), banks[2 + k % 2][:], ACT.Copy)\
                        .then_inc(S["mx_copied"], 1)

            def evacuate(q, u, done, at_least):
                act.wait_ge(done, at_least)
                act.activation(chunk, banks[0][:], ACT.Copy).then_inc(S["chunk_evacuated"], 1)
                act.wait_ge(S["chunk_turned"], q + (8 * u + 1))
                act.activation(ACC[:, bass.ds(q * B, B), :].rearrange("p b c -> p (b c)"), banks[1][:], ACT.Copy)\
                    .then_inc(S["chunk_stored"], 1)

            def collect(p, u):
                with act.Fori(0, Q) as q:
                    evacuate(q, u, freed[G - 1], q + (8 * p + 2))

            root(0)
            act.wait_ge(S["u_ready"], 1)
            act.activation(U[:], banks[4][:, 0:6], ACT.Copy).then_inc(S["u_ready"], 1)
            turn_copy(T)
            act.wait_ge(S["v_ready"], 1)
            act.activation(V.rearrange("p t v -> p (t v)"), banks[5][:, 0:6 * T], ACT.Copy).then_inc(S["v_copied"], 1)

            act.wait_ge(S["sums_cleared"], 1)
            with act.Fori(0, Q) as q:
                act.wait_ge(freed[G - 1], q + 2)
                act.activation(sup_c, banks[2][:], ACT.Copy).then_inc(S["support_copied"], 1)
                act.activation(sums[0:VC, bass.ds(q * CH, CH)], banks[3][0:VC, :], ACT.Copy).then_inc(S["support_copied"], 1)
                act.activation(sums[NEG0:NEG0 + VC, bass.ds(q * CH, CH)], banks[4][NEG0:NEG0 + VC, :], ACT.Copy)\
                    .then_inc(S["support_copied"], 1)
                act.wait_ge(S["support_stored"], q * 16 + 16)
                settle(act, "act_settled")

            for part in range(4):
                with act.Fori(0, 2) as i:
                    for g in range(G):
                        if g % 2 == 0:
                            act.wait_ge(loaded[g + 1], i * 16 + 16 * (8 + 2 * part + 1))
                            if part in (0, 3):
                                act.wait_ge(S["blocks_cleared"], i * G + (2 * G * (part // 3) + g + 2))
                            settle(act, "act_settled")
                            act.activation(not_positive_edge, ring[g + 1], ACT.Relu, bias=ones[:], scale=-STEEP)\
                                .then_inc(S["no_edge_ready"], 1)
                        for h in range(HEADS):
                            k = HEADS * g + h
                            act.wait_ge(S["logits_ready"], i * (G * HEADS) + (2 * part * G * HEADS + k + 1))
                            col = DEN.rearrange("p a n -> p (a n)")[:, bass.ds(i * (G * HEADS) + (2 * part * G * HEADS + k), 1)]
                            act.activation(logits[k % 3], logits[k % 3], ACT.Exp, bias=nmx[:, k:k + 1], scale=-1.0,
                                           accum_out=col).then_inc(S["logits_used"], 1)
            act.wait_ge(S["row_max_final"], 1)
            act.activation(s_flat(s, 0), s_flat(s, 0), ACT.Exp).then_inc(S["den_scaled"], 1)
            act.activation(s_flat(s, 1), s_flat(s, 1), ACT.Exp).then_inc(S["den_scaled"], 1)
            act.wait_ge(S["den_ready"], 1)
            act.activation(nmf[:, 1, :], nmf[:, 1, :], ACT.Ln).then_inc(S["den_scaled"], 1)
            act.wait_ge(S["nm_turned"], 1)
            act.activation(rows[:], banks[0][0:HEADS * T, 0:P], ACT.Copy).then_inc(S["nm_rows_ready"], 1)
            for t in range(T):
                act.wait_ge(S["hw_ready"], t + 1)
                act.activation(hW[:, t, :], banks[1 + t % 2][:, 0:HEADS * C], ACT.Copy).then_inc(S["hw_copied"], 1)

            with act.Fori(0, Q // 2) as qq:
                for i in range(2):
                    q = qq * 2 + i
                    for k in range(G * HEADS):
                        act.wait_ge(S["exponents_ready"], q * (G * HEADS * B) + B * (k + 1))
                        flat = probs[k % 4].rearrange("p b i -> p (b i)")
                        act.activation(flat, flat, ACT.Exp).then_inc(S["probs_ready"], 1)
                        if k == 4:
                            with act.If(qq) if i == 0 else nullcontext():
                                act.wait_ge(S["probs_free"], q * (G * HEADS) + 4)
                                act.activation(att_c, banks[1 - i][:], ACT.Copy, scale=1.0 / HEADS)\
                                    .then_inc(S["att_copied"], 1)
                        if k == 16:
                            with act.If(qq) if i == 0 else nullcontext():
                                act.wait_ge(S["att_stored"], q * 16)
                                settle(act, "act_settled")
            act.wait_ge(S["probs_free"], Q * G * HEADS + 4)
            act.activation(att_c, banks[1][:], ACT.Copy, scale=1.0 / HEADS).then_inc(S["att_copied"], 1)

            for q in range(Q):
                for cell in range(2):
                    n, bank = 2 * q + cell, banks[4 * cell:4 * cell + 4]
                    act.wait_ge(S["gates_done"], n + 1)
                    if q:
                        act.wait_ge(S["gru_out"], n - 1)
                    act.activation(gr[cell], bank[0][:], ACT.Tanh, bias=bsum[:, cell, 0:1], scale=0.5).then_inc(S["gate_r"], 1)
                    act.activation(gz[cell], bank[1][:], ACT.Tanh, bias=bsum[:, cell, 1:2], scale=0.5).then_inc(S["gate_z"], 1)
                    act.wait_ge(S["gate_n_in"], n + 1)
                    act.activation(gn[cell], gt[cell], ACT.Tanh, bias=bi[:, cell, 2:3]).then_inc(S["gate_n"], 1)

            hyp = {"root": 0, "tanh": 0, "log": 0}

            def row_root(a, b_):
                hyp["root"] += 1
                act.wait_ge(S["norms_ready"], hyp["root"])
                act.activation(s[:, b_, :], s[:, a, :], ACT.Sqrt).then_inc(S["norms_rooted"], 1)

            def row_tanh(a, b_):
                hyp["tanh"] += 1
                act.wait_ge(S["tanh_in"], hyp["tanh"])
                act.activation(s[:, b_, :], s[:, a, :], ACT.Tanh).then_inc(S["tanh_out"], 1)

            def row_log():
                hyp["log"] += 1
                act.wait_ge(S["log_in"], hyp["log"])
                act.activation(s[:, 11, :], s[:, 11, :], ACT.Ln).then_inc(S["log_out"], 1)

            root(1)
            turn_copy(T)
            project_copy(0)
            row_root(3, 4)
            row_root(5, 6)
            row_log()
            row_tanh(8, 8)
            row_root(13, 13)
            row_tanh(14, 14)
            row_root(3, 4)
            row_log()
            collect(PASS_HYP, 0)
            row_root(3, 4)
            row_root(5, 6)
            row_tanh(8, 8)
            row_log()
            row_tanh(8, 8)

            root(2)
            turn_copy(T)
            project_copy(1)
            act.wait_ge(S["gat_cols_turned"], 2)
            act.activation(rows[0:T, :], banks[2][0:T, 0:P], ACT.Copy).then_inc(S["gat_rows_ready"], 1)
            for _ in range(2):
                act.sem_inc(S["signs_used"], 1)
            for half in range(2):
                with act.Fori(0, 4) as i:
                    for g in range(G):
                        act.wait_ge(loaded[g], i * 16 + 16 * (8 * PASS_GATMAX + 4 * half + 1))
                        act.wait_ge(S["signs_used"], i * G + (4 * G * half + g + 1))
                        settle(act, "act_settled")
                        act.activation(not_positive[g % 2], ring[g], ACT.Relu, bias=ones[:], scale=-STEEP)\
                            .then_inc(S["signs_ready"], 1)
                        act.wait_ge(S["signs_ready"], i * G + (4 * G * half + g + 1))
                        act.sem_inc(freed[g], 1)
            act.wait_ge(S["gat_cols_turned"], 3)
            act.wait_ge(S["gat_rows_stored"], 16)
            act.activation(rows[0:2 * T, :], banks[2][0:2 * T, 0:P], ACT.Copy).then_inc(S["gat_rows_ready"], 1)
            act.wait_ge(S["dst_loaded"], 32)

            def slopes(q, g, first):
                if g >= 4 or not first:
                    act.wait_ge(S["gat_w_free"], q * G + (g - 3))
                    act.wait_ge(S["gat_summed"], q * (G - 1) + (max(g - 4, 1) if g >= 4 else g - 3))
                    settle(act, "act_settled")
                for b in range(B):
                    act.activation(gat_p[g % 4][:, b, :], dst_all[1][:, bass.ds(q * CH, CH)], ACT.Identity, scale=1.0,
                                   bias=s[:, 8, B * g + b:B * g + b + 1]).then_inc(S["gat_slope_ready"], 1)

            def copy_chunk(q):
                act.wait_ge(S["gat_w_free"], q * G + G)
                act.activation(chunk, banks[0][:], ACT.Copy).then_inc(S["chunk_evacuated"], 1)

            def copy_denominators(q):
                act.wait_ge(S["den_summed"], q + 1)
                act.activation(den_c, banks[3][0:1, :], ACT.Copy).then_inc(S["den_out"], 1)

            def store_chunk(q):
                act.wait_ge(S["chunk_turned"], q + (8 + 1))
                act.activation(ACC[:, bass.ds(q * B, B), :].rearrange("p b c -> p (b c)"), banks[1][:], ACT.Copy)\
                    .then_inc(S["chunk_stored"], 1)
                act.wait_ge(S["den_turned"], q + 1)
                act.activation(s[:, 6, :][:, bass.ds(q * B, B)], banks[4][:, 0:B], ACT.Copy).then_inc(S["acc_used"], 1)

            def attention(q, first, more):
                for g in range(G):
                    if g < G - 1:
                        slopes(q, g + 1, first)
                    elif more:
                        slopes(q + 1, 0, False)
                    act.wait_ge(S["gat_logit_ready"], q * (G * B) + B * (g + 1))
                    flat = gat_p[g % 4].rearrange("p b i -> p (b i)")
                    act.activation(flat, flat, ACT.Exp).then_inc(S["gat_exp_ready"], 1)
                    if not first:
                        if g == 2:
                            copy_chunk(q - 1)
                        if g == 3:
                            copy_denominators(q - 1)
                        if g == 6:
                            store_chunk(q - 1)

            slopes(0, 0, True)
            attention(0, True, True)
            with act.Fori(1, Q - 1) as q:
                attention(q, False, True)
            attention(Q - 1, False, False)
            copy_chunk(Q - 1)
            copy_denominators(Q - 1)
            store_chunk(Q - 1)
            act.wait_ge(S["exp_in"], 1)
            act.activation(TMP.rearrange("p t c -> p (t c)"), TMP.rearrange("p t c -> p (t c)"), ACT.Exp)\
                .then_inc(S["exp_out"], 1)

            root(3)
            act.wait_ge(S["exp_in"], 2)
            act.activation(s[:, 7, :], s[:, 7, :], ACT.Exp).then_inc(S["exp_out"], 1)
            collect(PASS_SPEC, 2)
            act.wait_ge(S["spec_ready"], 1)
            collect(PASS_BACK, 3)

        @block.vector
        def _(dve):
            ch = Chain(dve, S["dve_chain"])
            neg = Chain(dve, S["neg_chain"])
            v = nc.vector

            def wide(col):
                return col.unsqueeze(2).broadcast_to([P, T, C])

            def sc(i):
                return s[:, i, :]

            def ts(o, a, s1, s2, op0, op1=ALU.bypass):
                ch(v.tensor_scalar(o, a, s1, s2, op0, op1) if s2 is not None else v.tensor_scalar(o, a, s1, None, op0))

            def tt(o, a, b_, op):
                ch(v.tensor_tensor(o, a, b_, op))

            def normalise(l):
                ch(v.tensor_reduce(sc(0), X, AX.X, ALU.add))
                ts(sc(0), sc(0), 1.0 / C, None, ALU.mult)
                tt(H, X, wide(sc(0)), ALU.subtract)
                tt(TMP, H, H, ALU.mult)
                ch(v.tensor_reduce(sc(1), TMP, AX.X, ALU.add))
                v.tensor_scalar(sc(1), sc(1), 1.0 / C, 1e-5, ALU.mult, ALU.add).then_inc(S["ln_var"], 1)
                dve.wait_ge(S["ln_sd"], l + 1)
                ch(v.reciprocal(sc(2), sc(2)))
                tt(sc(3), sc(2), sc(2), ALU.mult)
                tt(sc(3), sc(3), sc(1), ALU.mult)
                ts(sc(3), sc(3), -0.5, 1.5, ALU.mult, ALU.add)
                tt(sc(2), sc(2), sc(3), ALU.mult)
                tt(H, H, wide(sc(2)), ALU.mult)
                v.tensor_scalar(H, H, 0.0, None, ALU.max).then_inc(S["h_ready"], 1)
                dve.wait_ge(S["h_ready"], l + 1)

            dve.wait_ge(S["const_loaded"], 16 * N_LOADS)
            normalise(0)
            ch(v.memset(V19, 1.0))
            v.memset(sums, 0.0).then_inc(S["sums_cleared"], 1)
            tt(bsum[:], bi[:], bh[:], ALU.add)
            ts(bsum[:], bsum[:], 0.5, None, ALU.mult)
            dve.wait_ge(S["v_copied"], 1)
            for part in range(3):
                src = V if part == 0 else VR
                dst = V19[:, :, 1 + 6 * part:7 + 6 * part]
                if part < 2:
                    ch(v.tensor_copy(dst, src))
                    tt(VR, src, dst, ALU.subtract)
                else:
                    v.tensor_copy(dst, src).then_inc(S["v19_ready"], 1)

            def clear_diagonal(q, g):
                diag_ap = diagonal_blocks(g)
                m = not_i[:, bass.ds(q * P + (7 - g) * P, P)].unsqueeze(1).broadcast_to([P, B, P])
                ch(v.tensor_tensor(diag_ap, diag_ap, m, ALU.mult))

            def diagonal_blocks(g):
                step = CH + P
                return arena[:, g * SLOT:g * SLOT + B * step].rearrange("p (b k) -> p b k", k=step)[:, :, 0:P]

            with dve.Fori(0, Q) as q:
                ch.enter(q, G)
                for g in range(G):
                    dve.wait_ge(loaded[g], q * 16 + 16)
                    clear_diagonal(q, g)
                    if g >= 2:
                        dve.wait_ge(freed[g - 2], q + 2)
                    else:
                        dve.wait_ge(freed[g + 6], q + 1)
                    v.tensor_scalar(mask_pos[g % 2], groups[g], 0.0, None, ALU.is_gt).then_inc(S["masks_ready"], 1)
                    v.tensor_scalar(mask_neg[g % 2], groups[g], 0.0, None, ALU.is_lt)\
                        .then_inc(S["masks_ready"], 1)
            ch.leave(Q)
            dve.wait_ge(S["support_stored"], 16 * Q)
            dve.wait_ge(freed[G - 1], Q + 1)

            def copy_cols(q):
                dve.wait_ge(S["edge_cols_turned"], q + 1)
                v.tensor_copy(ecol[:, B * q:B * q + B, 0:7],
                              banks[6 + q % 2][:, 0:8 * B].rearrange("p (b k) -> p b k", k=8)[:, :, 0:7])\
                    .then_inc(S["edge_cols_copied"], 1)

            for q in range(Q):
                cols, plus, minus = slice(q * CH, (q + 1) * CH), banks[2 * (q % 2)], banks[2 * (q % 2) + 1]
                dve.wait_ge(S["edges_summed"], q + 1)
                ts(slope_p[0:4, :], plus[0:4, :], SLOPE, None, ALU.mult)
                ts(slope_m[0:3, :], minus[0:3, :], SLOPE, None, ALU.mult)
                tt(ep[:, cols], slope_p[0:4, :], plus[0:4, :], ALU.max)
                tt(em[0:3, :], slope_m[0:3, :], minus[0:3, :], ALU.max)
                v.tensor_tensor(dd[:, cols], em[0:3, :], ep[0:3, cols], ALU.subtract).then_inc(S["edges_ready"], 1)
                if q:
                    copy_cols(q - 1)
            copy_cols(Q - 1)
            dve.wait_ge(S["edge_cols_copied"], Q)
            v.tensor_scalar(ep[0:3, :], ep[0:3, :], -NEAR_UNIT, None, ALU.mult).then_inc(S["edges_scaled"], 1)
            v.tensor_scalar(dd, dd, -NEAR_UNIT, None, ALU.mult).then_inc(S["edges_scaled"], 1)
            at_count = slice(NEG0, NEG0 + 1)
            ch(v.tensor_reduce(flag[at_count, :], sums[at_count, :], AX.X, ALU.max))
            v.tensor_copy(flag_i[at_count, :], flag[at_count, :]).then_inc(S["flag_ready"], 1)
            dve.wait_ge(S["flag_ready"], 1)
            any_negative = dve.value_load(flag_i[NEG0:NEG0 + 1, 0:1], min_val=0, max_val=N)

            dve.wait_ge(S["logits_used"], 3)
            for part in range(4):
                half, on_diagonal = part // 2, part in (0, 3)
                if part % 2 == 0:
                    dve.wait_ge(S["e_broadcast"], 16 * 2 * HEADS * (half + 1))
                with dve.Fori(0, 2) as i:
                    ch.enter(i, G // 2 + 1)
                    neg.enter(i, G // 2 + G * HEADS * 2)
                    for g in range(G):
                        dve.wait_ge(loaded[g], i * 16 + 16 * (8 + 2 * part + 1))
                        if on_diagonal:
                            dve.wait_ge(S["blocks_cleared"], i * G + (2 * G * half + g + 1))
                        if g % 2 == 0:
                            ch(v.tensor_scalar(no_edge, ring[g], 0.0, None, ALU.is_equal))
                        else:
                            dve.wait_ge(S["no_edge_ready"], i * (G // 2) + (G * part + (g + 1) // 2))

                        def masked_logits(h, mask, e_row):
                            k = HEADS * g + h
                            dve.wait_ge(S["logits_used"], i * (G * HEADS) + (2 * part * G * HEADS + k + 1))
                            settle(dve, "dve_settled")
                            v.tensor_tensor_reduce(logits[k % 3], mask, e_row, FAR_UNIT, FAR,
                                                   ALU.add, ALU.min, nmx[:, k:k + 1]).then_inc(S["logits_ready"], 1)

                        settle(dve, "dve_settled")
                        with dve.If(any_negative):
                            if g % 2:
                                neg(v.tensor_scalar(no_edge, ring[g], 0.0, None, ALU.is_equal))
                            for h in range(HEADS):
                                if h:
                                    dve.wait_ge(S["logits_ready"], i * (G * HEADS) + (2 * part * G * HEADS + HEADS * g + h))
                                neg(v.scalar_tensor_tensor(signed_e, ring[g], 0.0, e_bc[:, HEADS + h, :],
                                                           ALU.is_lt, ALU.mult))
                                neg(v.tensor_tensor(signed_e, signed_e, e_bc[:, h, :], ALU.add))
                                masked_logits(h, no_edge, signed_e)
                        with dve.Else():
                            for h in range(HEADS):
                                masked_logits(h, not_positive_edge if g % 2 else no_edge, e_bc[:, h, :])
                        dve.wait_ge(S["logits_ready"], i * (G * HEADS) + (2 * part * G * HEADS + HEADS * g + HEADS))
                        v.sem_inc(freed[g], 1)
                    col = NM.rearrange("p a n -> p (a n)")[:, bass.ds(i * (G * HEADS) + 2 * part * G * HEADS, G * HEADS)]
                    ch(v.tensor_copy(col, nmx[:]))
                ch.leave(2)
                neg.leave(2)
            rt = "p (t h) -> p h t"
            by_head = nmf[:].rearrange("p a (h t) -> p a h t", h=HEADS)
            tt(by_head[:, 0], NM[:, 0, :].rearrange(rt, h=HEADS), NM[:, 1, :].rearrange(rt, h=HEADS), ALU.min)
            f0, f1 = s_flat(s, 0), s_flat(s, 1)
            tt(f0.rearrange("p (h t) -> p h t", h=HEADS), by_head[:, 0], NM[:, 0, :].rearrange(rt, h=HEADS), ALU.subtract)
            v.tensor_tensor(f1.rearrange("p (h t) -> p h t", h=HEADS), by_head[:, 0], NM[:, 1, :].rearrange(rt, h=HEADS),
                            ALU.subtract).then_inc(S["row_max_final"], 1)
            dve.wait_ge(S["den_scaled"], 2)
            tt(f0.rearrange("p (h t) -> p h t", h=HEADS), f0.rearrange("p (h t) -> p h t", h=HEADS),
               DEN[:, 0, :].rearrange(rt, h=HEADS), ALU.mult)
            tt(f1.rearrange("p (h t) -> p h t", h=HEADS), f1.rearrange("p (h t) -> p h t", h=HEADS),
               DEN[:, 1, :].rearrange(rt, h=HEADS), ALU.mult)
            v.tensor_tensor(nmf[:, 1, :], f0, f1, ALU.add).then_inc(S["den_ready"], 1)
            dve.wait_ge(S["den_scaled"], 3)
            v.tensor_tensor(nmf[:, 2, :], nmf[:, 0, :], nmf[:, 1, :], ALU.subtract).then_inc(S["den_ready"], 1)

            dve.wait_ge(S["probs_free"], 4)

            def heads_chunk(q, qq, i):
                nm = nm_c[i]
                dve.wait_ge(nm_loaded[i], qq * (16 * HEADS) + 16 * HEADS)
                last = G * HEADS

                def exponents(k):
                    g, h = k // HEADS, k % HEADS
                    if h == 0:
                        dve.wait_ge(loaded[g], q * 16 + 16 * (8 * PASS_HEADS + 1))
                        clear_diagonal(q, g)
                        v.sem_inc(S["diagonal_clear"], 1)
                    dve.wait_ge(S["probs_free"], q * (G * HEADS) + (k + 1))
                    settle(dve, "dve_settled")
                    buf = probs[k % 4]
                    with dve.If(any_negative):
                        for b in range(B):
                            neg(v.tensor_scalar(buf[:, b, :], groups[g][:, b, :], 0.0,
                                                ecol[:, B * g + b, 4 + h:5 + h], ALU.is_lt, ALU.mult))
                        neg(v.tensor_tensor(buf, buf, nm[:, h, :].unsqueeze(1).broadcast_to([P, B, CH]), ALU.add))
                        for b in range(B):
                            v.tensor_scalar(buf[:, b, :], buf[:, b, :], ecol[:, B * g + b, h:h + 1], 0.0,
                                            ALU.add, ALU.min).then_inc(S["exponents_ready"], 1)
                    with dve.Else():
                        for b in range(B):
                            v.tensor_scalar(buf[:, b, :], nm[:, h, :], ecol[:, B * g + b, h:h + 1], 0.0,
                                            ALU.add, ALU.min).then_inc(S["exponents_ready"], 1)

                def weigh(k):
                    g, h = k // HEADS, k % HEADS
                    if h < HEADS - 1:
                        dve.wait_ge(S["probs_ready"], q * last + (k + 1))
                        v.tensor_tensor(probs[k % 4], probs[k % 4], groups[g], ALU.mult).then_inc(S["heads_ready"], 1)
                    else:
                        dve.wait_ge(S["heads_ready"], q * (G * (HEADS - 1)) + (HEADS - 1) * (g + 1))
                        if g:
                            dve.wait_ge(S["last_head_ready"], q * G + g)
                            v.sem_inc(freed[g - 1], 1)

                for k in range(last + 2):
                    if k >= 2:
                        weigh(k - 2)
                    if k < last:
                        exponents(k)
                dve.wait_ge(S["last_head_ready"], q * G + G)
                v.sem_inc(freed[G - 1], 1)
                dve.wait_ge(S["exponents_ready"], q * (last * B) + last * B)
                v.sem_inc(S["nm_used"], 1)

            with dve.Fori(0, Q // 2) as qq:
                ch.enter(qq, 2 * G)
                neg.enter(qq, 2 * G * HEADS * (B + 1))
                for i in range(2):
                    heads_chunk(qq * 2 + i, qq, i)
            ch.leave(Q // 2)
            neg.leave(Q // 2)

            for q in range(Q):
                for cell in range(2):
                    n, bank = 2 * q + cell, banks[4 * cell:4 * cell + 4]
                    r, z, t_, h_new = gr[cell], gz[cell], gt[cell], gn[cell]
                    dve.wait_ge(S["gate_r"], n + 1)
                    ts(r, r, 0.5, 0.5, ALU.mult, ALU.add)
                    ch(v.scalar_tensor_tensor(t_, bank[3][:], bh[:, cell, 2:3], r, ALU.add, ALU.mult))
                    v.tensor_tensor(t_, t_, bank[2][:], ALU.add).then_inc(S["gate_n_in"], 1)
                    dve.wait_ge(S["gate_z"], n + 1)
                    ts(z, z, 0.5, 0.5, ALU.mult, ALU.add)
                    dve.wait_ge(S["gate_n"], n + 1)
                    tt(t_, HT[:, q * CH:(q + 1) * CH], h_new, ALU.subtract)
                    tt(t_, t_, z, ALU.mult)
                    if cell == 0:
                        if q >= 2:
                            dve.wait_ge(S["gru_turned"], q - 1)
                        v.tensor_tensor(so[q % 2], t_, h_new, ALU.add).then_inc(S["gru_out"], 1)
                        dve.wait_ge(S["gru_out"], n + 1)
                    else:
                        tt(t_, t_, h_new, ALU.add)
                        v.tensor_tensor(so[q % 2], so[q % 2], t_, ALU.add).then_inc(S["gru_out"], 1)
                dve.wait_ge(S["gru_turned"], q + 1)
                d = dg[:, B * q:B * q + B].unsqueeze(2).broadcast_to([P, B, C])
                turned = gt[0].rearrange("p (b c) -> p b c", b=B)
                ch(v.tensor_tensor(turned, banks[7][:].rearrange("p (b c) -> p b c", b=B), d, ALU.mult))
                v.tensor_tensor(X[:, B * q:B * q + B, :], X[:, B * q:B * q + B, :], turned, ALU.add).then_inc(S["x_updated"], 1)
            dve.wait_ge(S["x_updated"], Q)

            hyp = {"root": 0, "tanh": 0, "log": 0}

            def rooted(ins):
                hyp["root"] += 1
                ins.then_inc(S["norms_ready"], 1)
                dve.wait_ge(S["norms_rooted"], hyp["root"])

            def tanhed(ins):
                hyp["tanh"] += 1
                ins.then_inc(S["tanh_in"], 1)
                dve.wait_ge(S["tanh_out"], hyp["tanh"])

            def squares(o, a):
                tt(TMP, a, a, ALU.mult)
                rooted(v.tensor_reduce(o, TMP, AX.X, ALU.add))

            def artanh(x_, o):
                ts(sc(9), x_, CLIP, None, ALU.min)
                tt(sc(10), sc(9), sc(9), ALU.mult)
                ts(sc(12), sc(10), 1.0 / 17, 1.0 / 15, ALU.mult, ALU.add)
                for odd in (13, 11, 9, 7, 5, 3, 1):
                    tt(sc(12), sc(12), sc(10), ALU.mult)
                    ts(sc(12), sc(12), 1.0 / odd, None, ALU.add)
                tt(sc(12), sc(12), sc(9), ALU.mult)
                ts(sc(11), sc(9), -1.0, 1.0, ALU.mult, ALU.add)
                ch(v.reciprocal(sc(11), sc(11)))
                ts(sc(10), sc(9), 1.0, None, ALU.add)
                hyp["log"] += 1
                v.tensor_tensor(sc(11), sc(11), sc(10), ALU.mult).then_inc(S["log_in"], 1)
                dve.wait_ge(S["log_out"], hyp["log"])
                ts(sc(10), sc(9), 0.25, 0.5, ALU.is_ge, ALU.mult)
                tt(sc(11), sc(11), sc(10), ALU.mult)
                ts(sc(10), sc(9), 0.25, None, ALU.is_lt)
                tt(sc(12), sc(12), sc(10), ALU.mult)
                tt(o, sc(11), sc(12), ALU.add)

            def over(o, a, b_):
                ch(v.reciprocal(sc(12), b_))
                tt(o, a, sc(12), ALU.mult)

            normalise(1)
            squares(sc(3), H)
            dve.wait_ge(S["mx_copied"], G)
            squares(sc(5), M1)
            ts(sc(4), sc(4), TINY, None, ALU.max)
            ts(sc(6), sc(6), TINY, None, ALU.max)
            artanh(sc(4), sc(7))
            over(sc(8), sc(6), sc(4))
            tanhed(v.tensor_tensor(sc(8), sc(8), sc(7), ALU.mult))
            ts(sc(8), sc(8), MAXNORM, None, ALU.min)
            over(sc(7), sc(8), sc(6))
            ch(v.tensor_tensor(avec[:, 3, :], avec[:, 0, :], avec[:, 0, :], ALU.mult))
            ch(v.memset(sc(13), 0.0))
            rooted(v.tensor_reduce(s[:, 13, 0:1], avec[:, 3, :], AX.X, ALU.add))
            ts(s[:, 13, :], s[:, 13, :], TINY, None, ALU.max)
            tanhed(v.tensor_copy(sc(14), sc(13)))
            ts(sc(14), sc(14), MAXNORM, None, ALU.min)
            over(sc(15), sc(14), sc(13))
            ch(v.tensor_scalar(avec[:, 3, :], avec[:, 0, :], s[:, 15, 0:1], None, ALU.mult))
            y = avec[:, 3, :].unsqueeze(1).broadcast_to([P, T, C])
            tt(sc(16), sc(14), sc(14), ALU.mult)
            y2 = s[:, 16, 0:1]
            tt(TMP, M1, y, ALU.mult)
            ch(v.tensor_reduce(sc(9), TMP, AX.X, ALU.add))
            tt(sc(9), sc(9), sc(7), ALU.mult)
            ts(sc(9), sc(9), 2.0, 1.0, ALU.mult, ALU.add)
            tt(sc(10), sc(8), sc(8), ALU.mult)
            ts(sc(11), sc(9), y2, None, ALU.add)
            tt(sc(11), sc(11), sc(7), ALU.mult)
            ts(sc(13), sc(10), y2, None, ALU.mult)
            tt(sc(13), sc(13), sc(9), ALU.add)
            ts(sc(13), sc(13), TINY, None, ALU.max)
            ts(sc(10), sc(10), -1.0, 1.0, ALU.mult, ALU.add)
            over(sc(11), sc(11), sc(13))
            over(sc(10), sc(10), sc(13))
            tt(M1, M1, wide(sc(11)), ALU.mult)
            tt(TMP, y, wide(sc(10)), ALU.mult)
            tt(M1, M1, TMP, ALU.add)
            squares(sc(3), M1)
            ts(sc(4), sc(4), TINY, None, ALU.max)
            ts(sc(5), sc(4), MAXNORM, None, ALU.min)
            artanh(sc(5), sc(7))
            over(sc(7), sc(7), sc(4))
            v.tensor_tensor(M1, M1, wide(sc(7)), ALU.mult).then_inc(S["tangent_ready"], 1)
            dve.wait_ge(S["chunk_stored"], 8)
            squares(sc(3), ACC)
            ts(ACC, ACC, 0.0, None, ALU.max)
            squares(sc(5), ACC)
            ts(sc(4), sc(4), TINY, None, ALU.max)
            tanhed(v.tensor_copy(sc(8), sc(4)))
            ts(sc(8), sc(8), MAXNORM, TINY, ALU.min, ALU.max)
            artanh(sc(8), sc(7))
            over(sc(7), sc(7), sc(4))
            tt(sc(5), sc(7), sc(6), ALU.mult)
            ts(sc(5), sc(5), TINY, None, ALU.max)
            tanhed(v.tensor_copy(sc(8), sc(5)))
            ts(sc(8), sc(8), MAXNORM, None, ALU.min)
            over(sc(8), sc(8), sc(5))
            tt(sc(8), sc(8), sc(7), ALU.mult)
            tt(ACC, ACC, wide(sc(8)), ALU.mult)
            tt(X, X, ACC, ALU.add)

            normalise(2)
            dve.wait_ge(S["mx_copied"], 2 * G)
            tt(TMP, M1, avec[:, 1, :].unsqueeze(1).broadcast_to([P, T, C]), ALU.mult)
            ch(v.tensor_reduce(sc(0), TMP, AX.X, ALU.add))
            tt(TMP, M1, avec[:, 2, :].unsqueeze(1).broadcast_to([P, T, C]), ALU.mult)
            ch(v.tensor_reduce(sc(1), TMP, AX.X, ALU.add))
            ts(sc(9), sc(0), -NEAR_UNIT, None, ALU.mult)
            v.tensor_scalar(sc(8), sc(0), SLOPE, None, ALU.mult).then_inc(S["gat_cols_turned"], 1)
            dve.wait_ge(S["src_broadcast"], 16)
            for half in range(2):
                with dve.Fori(0, 4) as i:
                    ch.enter(i, G + 1)
                    for g in range(G):
                        dve.wait_ge(S["signs_ready"], i * G + (4 * G * half + g + 1))
                        settle(dve, "dve_settled")
                        ch(v.tensor_tensor_reduce(masked_src, not_positive[g % 2], src_bc[:, half * HALF:(half + 1) * HALF],
                                                  FAR_UNIT, FAR, ALU.add, ALU.min, nmx[:, g:g + 1]))
                        v.sem_inc(S["signs_used"], 1)
                    ch(v.tensor_copy(s[:, 2 + half, :][:, bass.ds(i * G, G)], nmx[:, 0:G]))
                ch.leave(4)
            tt(sc(2), sc(2), sc(3), ALU.min)
            tt(sc(2), sc(1), sc(2), ALU.subtract)
            ts(sc(3), sc(2), SLOPE, None, ALU.mult)
            tt(sc(2), sc(2), sc(3), ALU.max)
            ts(sc(3), dg[:], 0.0, None, ALU.is_gt)
            tt(sc(3), sc(3), ecol[:, :, 3], ALU.add)
            ts(sc(3), sc(3), float(N) - 0.5, -BIG, ALU.is_gt, ALU.mult)
            tt(sc(2), sc(2), sc(3), ALU.max)
            tt(sc(4), sc(1), sc(2), ALU.subtract)
            ts(sc(5), sc(1), SLOPE, None, ALU.mult)
            v.tensor_tensor(sc(5), sc(5), sc(2), ALU.subtract).then_inc(S["gat_max_done"], 1)
            dve.wait_ge(S["dst_loaded"], 32)

            def scores(q, g):
                buf = gat_p[g % 4]
                for b in range(B):
                    dve.wait_ge(S["gat_slope_ready"], q * (G * B) + (B * g + b + 1))
                    v.scalar_tensor_tensor(buf[:, b, :], dst_all[0][:, bass.ds(q * CH, CH)], s[:, 0, B * g + b:B * g + b + 1],
                                           buf[:, b, :], ALU.add, ALU.max).then_inc(S["gat_logit_ready"], 1)

            def weights(q, g):
                dve.wait_ge(loaded[g], q * 16 + 16 * (8 * PASS_GAT + 1))
                dve.wait_ge(S["gat_exp_ready"], q * G + (g + 1))
                settle(dve, "dve_settled")
                v.scalar_tensor_tensor(gat_p[g % 4], groups[g], 0.0, gat_p[g % 4], ALU.is_gt, ALU.min)\
                    .then_inc(S["gat_w_ready"], 1)
                if g:
                    dve.wait_ge(S["gat_w_ready"], q * G + g)
                    v.sem_inc(freed[g - 1], 1)

            def attention(q, more):
                for g in range(G):
                    if g < G - 1:
                        scores(q, g + 1)
                    elif more:
                        scores(q + 1, 0)
                    weights(q, g)
                dve.wait_ge(S["gat_w_ready"], q * G + G)
                v.sem_inc(freed[G - 1], 1)

            scores(0, 0)
            with dve.Fori(0, Q - 1) as q:
                attention(q, True)
            attention(Q - 1, False)
            dve.wait_ge(S["acc_used"], Q)
            dve.wait_ge(S["chunk_stored"], 16)
            ts(sc(6), sc(6), 1e-8, None, ALU.add)
            ch(v.reciprocal(sc(6), sc(6)))
            tt(ACC, ACC, wide(sc(6)), ALU.mult)
            v.tensor_scalar(TMP, ACC, 0.0, None, ALU.min).then_inc(S["exp_in"], 1)
            dve.wait_ge(S["exp_out"], 1)
            ts(TMP, TMP, -1.0, None, ALU.add)
            ts(ACC, ACC, 0.0, None, ALU.max)
            tt(ACC, ACC, TMP, ALU.add)
            tt(X, X, ACC, ALU.add)

            normalise(3)
            ts(tv[:], tv[:], 1e-8, -1.0, ALU.max, ALU.mult)
            v.tensor_scalar(sc(7), ev[:], tv[:, 0:1], None, ALU.mult).then_inc(S["exp_in"], 1)
            dve.wait_ge(S["exp_out"], 2)
            dve.wait_ge(S["chunk_stored"], 24)
            v.tensor_tensor(M1, ACC, wide(sc(7)), ALU.mult).then_inc(S["spec_ready"], 1)
            dve.wait_ge(S["chunk_stored"], 32)
            v.tensor_tensor(X, X, ACC, ALU.add).then_inc(S["ready_to_store"], 1)


def kernel(**inputs):
    import numpy as np
    import ml_dtypes
    import concourse.bacc as bacc
    from concourse.bass_utils import run_bass_kernel_spmd as run

    f = {k: np.asarray(v) for k, v in inputs.items()}

    def cols(a, n):
        return np.ascontiguousarray(a.reshape(n, P).T)

    def row(a):
        return np.ascontiguousarray(np.broadcast_to(a.reshape(1, C), (P, C)))

    not_i = np.ones((P, 15 * P), ml_dtypes.bfloat16)
    not_i[:, 7 * P:8 * P] = 1 - np.eye(P)
    sel = np.zeros((P, 8), np.float32)
    sel[0, 3] = 1
    for part in range(3):
        for h in range(HEADS):
            a1, a2 = 1 + 6 * part + 2 * h, 2 + 6 * part + 2 * h
            sel[a1, h] = sel[a2, 4 + h] = 1
            sel[NEG0 + a2, h] = sel[NEG0 + a1, 4 + h] = 1
    e, n = "L0_gnn_edge_", "L0_gnn_node_"
    arrays = {
        "x": f["x"], "adj": f["adj"], "adjT": np.ascontiguousarray(f["adj"].T),
        "diag": cols(np.diagonal(f["adj"]), T),
        "gatW": np.ascontiguousarray(f["L0_gnn_gat_W"].transpose(1, 0, 2)).reshape(C, HEADS * C),
        "gatWT": np.ascontiguousarray(f["L0_gnn_gat_W"].transpose(2, 0, 1)).reshape(C, HEADS * C),
        "gata": np.ascontiguousarray(f["L0_gnn_gat_a"].reshape(HEADS, 2, C).transpose(2, 0, 1)).reshape(C, 2 * HEADS),
        "wih": np.stack([f[e + "Wih"].T, f[n + "Wih"].T]), "whh": np.stack([f[e + "Whh"].T, f[n + "Whh"].T]),
        "bih": np.stack([cols(f[e + "bih"], 3), cols(f[n + "bih"], 3)]),
        "bhh": np.stack([cols(f[e + "bhh"], 3), cols(f[n + "bhh"], 3)]),
        "w1": np.ascontiguousarray(f["L1_gnn_weight"].T), "bias1": row(f["L1_gnn_bias"]),
        "w2": np.ascontiguousarray(f["L2_gnn_W"].T), "att_s": row(f["L2_gnn_attn_src"]),
        "att_d": row(f["L2_gnn_attn_dst"]),
        "evals": cols(f["L3_gnn_evals"], T), "t_in": np.ascontiguousarray(np.broadcast_to(f["L3_gnn_t"].reshape(1, 1), (P, 1))),
        "ident": np.eye(P, dtype=np.float32), "not_i": not_i, "sel": sel,
    }
    nc = bacc.Bacc("TRN2", target_bir_lowering=False, num_devices=1)
    aps = [nc.dram_tensor(f"in_{k}", a.shape, mybir.dt.from_np(a.dtype), kind="ExternalInput").ap() for k, a in arrays.items()]
    out = nc.dram_tensor("out_x", (N, C), F32, kind="ExternalOutput").ap()
    build(nc, *aps, out)
    r = run(nc, [{f"in_{k}": a for k, a in arrays.items()}], core_ids=[0])
    return r.results[0]["out_x"]
```

```python
from contextlib import ExitStack, nullcontext

import concourse.bass as bass
from concourse import mybir

F32 = mybir.dt.float32
BF16 = mybir.dt.bfloat16
I32 = mybir.dt.int32
ALU = mybir.AluOpType
ACT = mybir.ActivationFunctionType
AX = mybir.AxisListType

P = 128
N = 4096
C = 128
T = N // P
CH = 512
Q = N // CH
B = CH // P
G = T // B
SLOT = B * CH
HALF = N // 2
HEADS = 3
N_LOADS = 18
FAR = 3e38
BIG = 1e30
FAR_UNIT = 2.0 ** 64
STEEP = 2.0 ** 126
NEAR_UNIT = 2.0 ** -64
TINY = 1e-15
MAXNORM = 1.0 - 1e-5
CLIP = 1.0 - 2.0 ** -23
SLOPE = 0.2
LINKS_3, LINKS_5 = 54, 13
NEG0 = 32
VC = 1 + 3 * 2 * HEADS


class Chain:

    def __init__(self, engine, sem):
        self.engine, self.sem, self.at, self.n = engine, sem, 0, 0

    def __call__(self, instruction):
        self.n += 1
        instruction.then_inc(self.sem, 1)
        self.engine.wait_ge(self.sem, self.at + self.n)

    def also(self, instruction):
        self.n += 1
        instruction.then_inc(self.sem, 1)

    def enter(self, i, per):
        self.kept, self.per = self.at + self.n, per
        self.at, self.n = i * per + self.kept, 0

    def leave(self, times):
        assert self.n == self.per, (self.n, self.per)
        self.at, self.n = self.kept + times * self.per, 0


class Count:

    def __init__(self):
        self.at, self.n = 0, 0

    def __call__(self):
        self.n += 1
        return self.at + self.n

    def enter(self, i, per):
        self.kept, self.per = self.at + self.n, per
        self.at, self.n = i * per + self.kept, 0

    def leave(self, times):
        assert self.n == self.per, (self.n, self.per)
        self.at, self.n = self.kept + times * self.per, 0


def s_flat(s, i):
    return s[:, 3 * i:3 * i + 3, :].rearrange("p a t -> p (a t)")


def build(nc, x, adj, adjT, diag, gatW, gatWT, gata, wih, whh, bih, bhh, w1, bias1, w2, att_s, att_d,
          evals, t_in, ident_in, notI_in, sel_in, out):
    PASS_EDGES, PASS_MAX, PASS_HEADS, PASS_HYP, PASS_GATMAX, PASS_GAT, PASS_SPEC, PASS_BACK = range(8)

    used = [8 * p + 8 * (p > PASS_MAX) for p in range(8)]

    ctx = ExitStack()
    with ctx:
        def sb(name, shape, dt=F32):
            return ctx.enter_context(nc.sbuf_tensor(name, shape, dt))

        def sem(name):
            return ctx.enter_context(nc.semaphore(name))

        banks = [ctx.enter_context(nc.psum_tensor(f"bank{i}", [P, CH], F32)) for i in range(8)]

        arena = sb("arena", [P, 189 * 256])

        def at(kb, *dims, dt=F32):
            n = 1
            for d in dims:
                n *= d
            words = n if dt == F32 else n // 2
            start = int(kb * 256)
            v = arena[:, start:start + words]
            if dt != F32:
                v = v.bitcast(dt)
            if len(dims) == 1:
                return v
            names = "abcd"[:len(dims)]
            return v.rearrange(f"p ({' '.join(names)}) -> p {' '.join(names)}", **dict(zip(names, dims)))

        ring = [at(8 * s, SLOT) for s in range(G)]
        ring_all = at(0, G * SLOT)
        groups = [r.rearrange("p (b i) -> p b i", b=B) for r in ring]
        X = at(64, T, C)
        R = 80
        H = at(R, T, C)
        HT = at(R + 16, N)
        mask_pos = [at(R + 32 + 4 * i, B, CH, dt=BF16) for i in range(2)]
        mask_neg = [at(R + 40 + 4 * i, B, CH, dt=BF16) for i in range(2)]
        ep, dd = at(R + 32, N)[0:4, :], at(R + 50, N)[0:HEADS, :]
        em = at(R + 70, CH)
        slope_p, slope_m = [at(R + 66, CH), at(R + 98, CH)], [at(R + 68, CH), at(R + 100, CH)]
        sums = at(R + 72, N)
        gwT = at(R + 88, HEADS * C)
        V, VR = at(R + 90, T, 2 * HEADS), at(R + 91, T, 2 * HEADS)
        V19 = at(R + 92, T, VC, dt=BF16)
        gw = at(R + 104, HEADS * C)
        NM, DEN = at(R + 105.5, 2, T * HEADS), at(R + 106.25, 2, T * HEADS)
        sup_c = at(R + 107, CH)
        rows = at(R + 80, P)[0:HEADS * T, :]
        e_bc = at(R + 32, 2 * HEADS, HALF)
        no_edge, not_positive_edge = (at(R + 80 + 4 * i, HALF, dt=BF16) for i in range(2))
        signed_e = at(R + 88, HALF)
        logits = [at(R + 16, HALF), at(R + 24, HALF), at(R + 96, HALF)]
        hW = at(R + 32, T, HEADS * C)
        hT_pair = [at(R + 30, CH), at(R + 102, CH)]
        probs = [at(R + o, B, CH) for o in (80, 88, 96, 0)]
        nm_c = [at(R + 16 + 6 * i, HEADS, CH) for i in range(2)]
        att_c = at(R + 28, CH)
        supT, attT = at(R + 32, N), at(R + 48, N)
        gr, gz, gn, gt = ([at(R + 64 + 8 * cell + 2 * i, CH) for cell in range(2)] for i in range(4))
        so = [at(R + 80 + 2 * i, CH) for i in range(2)]
        x_add = at(R + 84, CH)
        junk = at(R + 86, B, C)
        M1 = at(R + 32, T, C)
        TMP = at(R + 48, T, C)
        ACC = at(R + 64, T, C)
        chunk = at(R + 80, CH)
        src_bc = at(R + 16, N)
        M2 = at(R, T, C)
        acc4, tmp4, h4 = (at(R + 48 + 2 * i, B, C) for i in range(3))
        hT4 = at(R + 54, CH)
        not_positive = [at(R + 82 + 4 * i, HALF, dt=BF16) for i in range(2)]
        masked_src = at(R + 90, HALF)
        dst_all = [at(R + 48, N), at(R + 32, N)]
        w_sum = at(R + 98, B, CH)
        den_c = at(R + 106, CH)[0:1, :]
        gat_p = [at(R + o, B, CH) for o in (16, 24, 82, 90)]

        ident = sb("ident", [P, P])
        not_i = sb("not_i", [P, 15 * P], BF16)
        sel = sb("sel", [P, 8])
        wx = [sb(f"wih{i}", [P, 3 * C]) for i in range(2)]
        wh = [sb(f"whh{i}", [P, 3 * C]) for i in range(2)]
        ga = sb("ga", [P, 2 * HEADS])
        U = sb("U", [P, 2 * HEADS])
        bi = sb("bi", [P, 2, 3])
        bh = sb("bh", [P, 2, 3])
        bsum = sb("bsum", [P, 2, 3])
        w1s = sb("w1s", [P, C])
        w2s = sb("w2s", [P, C])
        avec = sb("avec", [P, 4, C])
        dg = sb("dg", [P, T])
        ev = sb("ev", [P, T])
        tv = sb("tv", [P, 1])
        ecol = sb("ecol", [P, T, 8])
        flag = sb("flag", [NEG0 + 1, 1])
        flag_i = sb("flag_i", [NEG0 + 1, 1], I32)
        nmx = sb("nmx", [P, G * HEADS])
        nmf = sb("nmf", [P, 3, HEADS * T])
        s = sb("s", [P, 19, T])
        s4 = sb("s4", [P, 13, B])
        bn, mv = sb("bn", [P, B, 6]), sb("mv", [P, B, 2])
        ln = sb("ln", [P, 4, B])
        ones = sb("ones", [P, 1])

        sup_d = nc.dram_tensor("sup_d", (P, CH + N), F32, kind="Internal").ap()
        attT_d = nc.dram_tensor("attT_d", (P, CH + N), F32, kind="Internal").ap()
        hT_d = nc.dram_tensor("hT_d", (P, N), F32, kind="Internal").ap()
        e_d = nc.dram_tensor("e_d", (2 * HEADS, N), F32, kind="Internal").ap()
        nm_d = nc.dram_tensor("nm_d", (HEADS * T, P), F32, kind="Internal").ap()
        gat_d = nc.dram_tensor("gat_d", (3 * T, P), F32, kind="Internal").ap()

        names = """const_loaded edges_sloped src_second_broadcast hw_turned hw_turn_copied sums_copied
            support_group_ready first_dst_loaded first_loaded second_broadcast x_added gru_scaled ln_factors
            squares_ready dve_chain signed_chain plain_chain edges_scaled blocks_cleared edge_cols_copied
            ln_var ln_sd h_ready tiles_turned turn_copied u_ready v_ready v_copied v19_ready masks_ready
            support_copied support_stored edges_summed edges_ready edges_stored edge_cols_turned flag_ready
            e_broadcast logits_ready logits_used row_max_final den_scaled den_ready nm_turned nm_rows_ready
            nm_stored nm_used hw_ready hw_copied probs_ready probs_free heads_ready exponents_ready att_copied
            gates_done gate_r gate_z gate_n_in gate_n gru_out gru_turned mx_done mx_copied norms_ready
            norms_rooted tanh_in tanh_out log_in log_out tangent_ready chunk_evacuated chunk_turned
            chunk_stored acc_used gat_cols_turned gat_rows_ready gat_rows_stored src_broadcast gat_max_done
            dst_loaded gat_slope_ready gat_logit_ready gat_exp_ready gat_w_ready gat_w_free signs_ready
            signs_used den_out den_turned exp_in exp_out ready_to_store out_stored ones_ready hT_stored
            att_stored diagonal_clear last_head_ready gat_summed no_edge_ready den_summed sums_cleared
            pool_settled pe_settled act_settled dve_settled""".split()
        S = {n: sem(n) for n in names}
        loaded = [sem(f"tile_loaded{i}") for i in range(G)]
        nm_loaded = [sem(f"nm_loaded{i}") for i in range(2)]
        cells_loaded = [sem(f"cells_loaded{i}") for i in range(Q // 2)]
        x_loaded = [sem(f"x_loaded{i}") for i in range(4)]
        freed = [sem(f"tile_freed{i}") for i in range(G)]

        x_v = x.rearrange("(t p) c -> p t c", p=P)
        out_v = out.rearrange("(t p) c -> p t c", p=P)
        natural = adj.rearrange("(r p) j -> p r j", p=P)
        streams = {PASS_EDGES: adjT, PASS_HEADS: adjT, PASS_HYP: adjT, PASS_GAT: adjT, PASS_SPEC: adj, PASS_BACK: adjT}

        def diagonal_blocks(slot):
            step = CH + P
            return arena[:, slot * SLOT:slot * SLOT + B * step].rearrange("p (b k) -> p b k", k=step)[:, :, 0:P]

        def settle(engine, name):
            engine.sem_inc(S[name], 1)

        block = ctx.enter_context(nc.Block())

        @block.sync
        def _(sp):
            def load(p, i, g, src):
                sp.wait_ge(freed[g], i + (used[p] + 1))
                dst = ring[g] if p == PASS_GATMAX else groups[g]
                sp.dma_start(dst, src).then_inc(loaded[g], 16)

            for k in range(4):
                sp.dma_start(X[:, G * k:G * k + G, :], x_v[:, G * k:G * k + G, :]).then_inc(x_loaded[k], 16)
            for dst, src in ((ident[:], ident_in), (gwT, gatWT), (ga[:], gata), (not_i[:], notI_in)):
                sp.dma_start(dst, src).then_inc(S["first_loaded"], 16)
            for g in range(G):
                sp.sem_inc(freed[g], 1)
            for p in range(8):
                if p == PASS_MAX:
                    v = adjT.rearrange("(t p) i -> p t i", p=P)
                    for half in range(2):
                        with sp.Fori(0, 4) as i:
                            for g in range(G):
                                n = used[p] + half * 8 + g // 4 + 1
                                for slot, dst, src in (
                                        (g % 4, ring[g % 4], natural[:, bass.ds(i * G + g, 1), half * HALF:(half + 1) * HALF]
                                         .rearrange("p r j -> p (r j)")),
                                        (4 + g % 4, groups[4 + g % 4], v[:, B * g:B * g + B, bass.ds(i * CH + half * 4 * CH, CH)])):
                                    sp.wait_ge(freed[slot], i * 2 + n)
                                    sp.dma_start(dst, src).then_inc(loaded[slot], 16)
                elif p == PASS_GATMAX:
                    for half in range(2):
                        with sp.Fori(0, 4) as i:
                            for g in range(G):
                                load(p, i + 4 * half, g,
                                     natural[:, bass.ds(i * G + g, 1), half * HALF:(half + 1) * HALF]
                                     .rearrange("p r j -> p (r j)"))
                else:
                    v = streams[p].rearrange("(t p) i -> p t i", p=P)
                    with sp.Fori(0, Q) as q:
                        for g in range(G):
                            load(p, q, g, v[:, B * g:B * g + B, bass.ds(q * CH, CH)])

        @block.gpsimd
        def _(pool):
            pool.memset(ones[:], 1.0).then_inc(S["ones_ready"], 1)
            for name, n in (("logits_used", 3), ("probs_free", 4)):
                for _ in range(n):
                    pool.engine_nop().then_inc(S[name], 1)
            loads = [(sel[:], sel_in), (gw, gatW), (w1s[:], w1), (w2s[:], w2),
                     (avec[:, 0, :], bias1), (avec[:, 1, :], att_s), (avec[:, 2, :], att_d),
                     (dg[:], diag), (ev[:], evals), (tv[:], t_in)]
            for i in range(2):
                loads += [(wx[i][:], wih[i]), (wh[i][:], whh[i]), (bi[:, i, :], bih[i]), (bh[:, i, :], bhh[i])]
            assert len(loads) == N_LOADS
            for dst, src in loads:
                pool.dma_start(dst, src).then_inc(S["const_loaded"], 16)

            pool.wait_ge(S["turn_copied"], G)
            pool.dma_start(hT_d, HT).then_inc(S["hT_stored"], 16)
            pool.wait_ge(S["edges_scaled"], 2)
            pool.dma_start(e_d[0:HEADS, :], ep[0:HEADS, :]).then_inc(S["edges_stored"], 16)
            pool.dma_start(e_d[HEADS:2 * HEADS, :], dd).then_inc(S["edges_stored"], 16)
            pool.wait_ge(S["edges_stored"], 32)
            pool.wait_ge(S["flag_ready"], 1)
            any_negative = pool.value_load(flag_i[NEG0:NEG0 + 1, 0:1], min_val=0, max_val=N)

            def broadcast(first_row, half, place, signal):
                for h in range(HEADS):
                    pool.dma_start(e_bc[:, place * HEADS + h, :],
                                   e_d[first_row + h, half * HALF:(half + 1) * HALF].partition_broadcast(P))\
                        .then_inc(S[signal], 16)

            broadcast(0, 0, 0, "e_broadcast")
            with pool.If(any_negative):
                broadcast(HEADS, 0, 1, "second_broadcast")
            with pool.Else():
                broadcast(0, 1, 1, "second_broadcast")
            for half in range(2):
                if half:
                    with pool.If(any_negative):
                        pool.wait_ge(S["logits_ready"], 4 * G * HEADS)
                        broadcast(0, 1, 0, "e_broadcast")
                        broadcast(HEADS, 1, 1, "second_broadcast")
                for part in (2 * half, 2 * half + 1):
                    with pool.Fori(0, 2) as i:
                        for g in range(G):
                            n = 16 * (used[PASS_MAX] + 4 * part + g // 4 + 1)
                            if part in (0, 3):
                                pool.wait_ge(loaded[g % 4], i * 32 + n)
                                settle(pool, "pool_settled")
                                d = ring_all[:, bass.ds(i * (G * P) + (g % 4 * SLOT + g * P), P)]
                                pool.tensor_tensor(d, d, not_i[:, 7 * P:8 * P], ALU.mult).then_inc(S["blocks_cleared"], 1)
                            pool.wait_ge(loaded[4 + g % 4], i * 32 + n)
                            settle(pool, "pool_settled")
                            d = diagonal_blocks(4 + g % 4)
                            m = not_i[:, bass.ds(i * P + (2 * part + 7 - g) * P, P)].unsqueeze(1).broadcast_to([P, B, P])
                            pool.tensor_tensor(d, d, m, ALU.mult).then_inc(S["support_group_ready"], 1)
                            if g == 4:
                                with pool.If(i) if part == 0 else nullcontext():
                                    pool.wait_ge(S["support_copied"], i + (2 * part + 1))
                                    settle(pool, "pool_settled")
                                    pool.dma_start(sup_d[:, bass.ds(i * CH + 2 * part * CH, CH)], sup_c)\
                                        .then_inc(S["support_stored"], 16)
            pool.wait_ge(S["support_copied"], Q + 1)
            pool.dma_start(sup_d[:, Q * CH:], sup_c).then_inc(S["support_stored"], 16)
            pool.wait_ge(S["nm_rows_ready"], 1)
            pool.dma_start(nm_d, rows[:]).then_inc(S["nm_stored"], 16)
            pool.wait_ge(S["nm_stored"], 16)
            pool.wait_ge(S["logits_used"], 2 * T * HEADS + 3)
            nm_v = nm_d.rearrange("(h t) p -> h (t p)", h=HEADS)

            def load_nm(q, i):
                for h in range(HEADS):
                    pool.dma_start(nm_c[i][:, h, :], nm_v[h, bass.ds(q * CH, CH)].partition_broadcast(P))\
                        .then_inc(nm_loaded[i], 16)

            def weigh(q, g):
                k = HEADS * g + HEADS - 1
                pool.wait_ge(S["probs_ready"], q * (G * HEADS) + (k + 1))
                pool.wait_ge(S["diagonal_clear"], q * G + (g + 1))
                settle(pool, "pool_settled")
                pool.tensor_tensor(probs[k % 4], probs[k % 4], groups[g], ALU.mult).then_inc(S["last_head_ready"], 1)

            load_nm(0, 0)
            load_nm(1, 1)

            def weigh_pair(qq, more):
                for i in range(2):
                    q = qq * 2 + i
                    for g in range(G):
                        if g == 2:
                            with pool.If(qq) if i == 0 else nullcontext():
                                pool.wait_ge(S["att_copied"], q + 2)
                                settle(pool, "pool_settled")
                                pool.dma_start(attT_d[:, bass.ds(q * CH, CH)], att_c).then_inc(S["att_stored"], 16)
                        weigh(q, g)
                    if more:
                        pool.wait_ge(S["nm_used"], q + 1)
                        settle(pool, "pool_settled")
                        load_nm(q + 2, i)

            with pool.Fori(0, Q // 2 - 1) as qq:
                weigh_pair(qq, True)
            with pool.Fori(Q // 2 - 1, Q // 2) as qq:
                weigh_pair(qq, False)
            pool.wait_ge(S["nm_used"], Q)
            pool.wait_ge(S["hT_stored"], 16)
            pieces = [slice(2 * i * CH, 2 * (i + 1) * CH) for i in range(Q // 2)]
            for i in range(3):
                pool.dma_start(HT[:, pieces[i]], hT_d[:, pieces[i]]).then_inc(cells_loaded[i], 16)
            pool.wait_ge(S["att_copied"], Q + 2)
            pool.dma_start(attT_d[:, Q * CH:], att_c).then_inc(S["att_stored"], 16)
            pool.wait_ge(S["support_stored"], 16 * Q)
            for i in range(Q // 2):
                pool.dma_start(supT[:, pieces[i]], sup_d[:, CH + 2 * i * CH:CH + 2 * (i + 1) * CH]).then_inc(cells_loaded[i], 16)
                if i == 0:
                    pool.wait_ge(S["att_stored"], 16 * Q)
                    pool.dma_start(HT[:, pieces[3]], hT_d[:, pieces[3]]).then_inc(cells_loaded[3], 16)
                pool.dma_start(attT[:, pieces[i]], attT_d[:, CH + 2 * i * CH:CH + 2 * (i + 1) * CH]).then_inc(cells_loaded[i], 16)
            for q in range(Q):
                pool.wait_ge(S["gru_scaled"], q + 1)
                x4, scaled4 = X[:, B * q:B * q + B, :], x_add.rearrange("p (b c) -> p b c", b=B)
                pool.tensor_tensor(x4, x4, scaled4, ALU.add).then_inc(S["x_added"], 1)

            pool.wait_ge(S["gat_rows_ready"], 1)
            pool.dma_start(gat_d[0:T, :], rows[0:T, :]).then_inc(S["gat_rows_stored"], 16)
            pool.wait_ge(S["gat_rows_stored"], 16)
            for half, signal in enumerate(("src_broadcast", "src_second_broadcast")):
                pool.dma_start(src_bc[:, half * HALF:(half + 1) * HALF],
                               gat_d[half * (T // 2):(half + 1) * (T // 2), :].rearrange("t p -> (t p)").partition_broadcast(P))\
                    .then_inc(S[signal], 16)
            pool.wait_ge(S["gat_rows_ready"], 2)
            pool.dma_start(gat_d[T:3 * T, :], rows[0:2 * T, :]).then_inc(S["gat_rows_stored"], 16)
            pool.wait_ge(S["gat_rows_stored"], 32)
            dst_v = gat_d[T:3 * T, :].rearrange("(h t) p -> h (t p)", h=2)
            for piece, signal in ((slice(0, CH), "first_dst_loaded"), (slice(CH, N), "dst_loaded")):
                for h in range(2):
                    pool.dma_start(dst_all[h][:, piece], dst_v[h, piece].partition_broadcast(P)).then_inc(S[signal], 16)
            def sum_weights(q, first):
                for g in range(1, G):
                    pool.wait_ge(S["gat_w_ready"], q * G + (g + 1))
                    if g > 1:
                        pool.wait_ge(S["gat_summed"], q * (G - 1) + (g - 1))
                    elif not first:
                        pool.wait_ge(S["den_summed"], q)
                    settle(pool, "pool_settled")
                    pool.tensor_tensor(w_sum, gat_p[0] if g == 1 else w_sum, gat_p[g % 4], ALU.add)\
                        .then_inc(S["gat_summed"], 1)

            sum_weights(0, True)
            with pool.Fori(1, Q) as q:
                sum_weights(q, False)
            with pool.Fori(0, Q) as q:
                pool.wait_ge(S["ready_to_store"], q + 1)
                settle(pool, "pool_settled")
                pool.dma_start(out_v[:, bass.ds(q * B, B), :], X[:, bass.ds(q * B, B), :]).then_inc(S["out_stored"], 16)
            pool.wait_ge(S["out_stored"], 16 * Q)

        @block.tensor
        def _(pe):
            pe.wait_ge(S["first_loaded"], 64)
            pe.wait_ge(S["ones_ready"], 1)
            turned = [0]

            def turn(l):
                for k in range(G):
                    pe.wait_ge(S["h_ready"], G * l + k + 1)
                    if turned[0] >= 2:
                        pe.wait_ge(S["turn_copied"], turned[0] - 1)
                    for b in range(B):
                        last = pe.transpose(banks[turned[0] % 2][:, b * P:(b + 1) * P], H[:, B * k + b, :], ident[:])
                    last.then_inc(S["tiles_turned"], 1)
                    turned[0] += 1
                    yield k

            def project(k, w):
                pe.wait_ge(S["turn_copied"], G + k + 1)
                if k >= 2:
                    pe.wait_ge(S["mx_copied"], k - 1)
                for b in range(B):
                    t = B * k + b
                    last = pe.matmul(banks[2 + k % 2][:, b * P:(b + 1) * P], HT[:, t * P:(t + 1) * P], w,
                                     start=True, stop=True)
                last.then_inc(S["mx_done"], 1)

            def product(p, u, stationary, grows=None):
                def product_chunk(q, grows):
                    for g in range(G):
                        pe.wait_ge(loaded[g], q * 16 + 16 * (used[p] + 1))
                        if grows:
                            pe.wait_ge(grows[0], grows[1] + g + 1)
                        for b in range(B):
                            last = pe.matmul(banks[0][:], stationary[:, B * g + b, :], groups[g][:, b, :],
                                             start=(g == 0 and b == 0), stop=(g == G - 1 and b == B - 1))
                        last.then_inc(freed[g], 1)
                    turn_chunk(q, u)

                if grows:
                    product_chunk(0, grows)
                with pe.Fori(1 if grows else 0, Q) as q:
                    product_chunk(q, None)

            def turn_chunk(q, u):
                pe.wait_ge(S["chunk_evacuated"], q + (8 * u + 1))
                for b in range(B):
                    last = pe.transpose(banks[1][:, b * P:(b + 1) * P], chunk[:, b * P:(b + 1) * P], ident[:])
                last.then_inc(S["chunk_turned"], 1)

            for h in range(HEADS):
                last = pe.matmul(banks[4][:, 2 * h:2 * h + 2], gwT[:, h * C:(h + 1) * C], ga[:, 2 * h:2 * h + 2],
                                 start=True, stop=True)
            last.then_inc(S["u_ready"], 1)
            pe.wait_ge(S["u_ready"], 2)

            def edge_values(k):
                pe.wait_ge(S["turn_copied"], k + 1)
                for t in range(B * k, B * k + B):
                    last = pe.matmul(banks[5][:, 6 * t:6 * t + 6], HT[:, t * P:(t + 1) * P], U[:], start=True, stop=True)
                last.then_inc(S["v_ready"], 1)

            for k in turn(0):
                if k:
                    edge_values(k - 1)
            edge_values(G - 1)
            pe.wait_ge(S["v19_ready"], 1)

            pe.wait_ge(S["const_loaded"], 16 * N_LOADS)
            with pe.Fori(0, Q) as q:
                for g in range(G):
                    pe.wait_ge(S["masks_ready"], q * (2 * G) + 2 * (g + 1))
                    for b in range(B):
                        t = B * g + b
                        first, end = t == 0, t == T - 1
                        pe.matmul(banks[3][0:VC, :], V19[:, t, :], mask_pos[g % 2][:, b, :], start=first, stop=end)
                        last = pe.matmul(banks[4][NEG0:NEG0 + VC, :], V19[:, t, :], mask_neg[g % 2][:, b, :],
                                         start=first, stop=end)
                    last.then_inc(freed[g], 1)
                pe.wait_ge(S["sums_copied"], q * 2 + 2)
            def add_parts(q, i):
                part = sums[:, bass.ds(q * CH, CH)]
                pe.matmul(banks[2 * i][0:4, :], sel[:, 0:4], part, start=True, stop=True)
                pe.matmul(banks[2 * i + 1][0:3, :], sel[:, 4:7], part, start=True, stop=True).then_inc(S["edges_summed"], 1)

            add_parts(0, 0)
            for q in range(Q):
                if q + 1 < Q:
                    if q:
                        pe.wait_ge(S["edges_ready"], q)
                    add_parts(q + 1, (q + 1) % 2)
                pe.wait_ge(S["edges_ready"], q + 1)
                if q >= 2:
                    pe.wait_ge(S["edge_cols_copied"], q - 1)
                for b in range(B):
                    cols = slice(q * CH + b * P, q * CH + (b + 1) * P)
                    pe.transpose(banks[6 + q % 2][:, 8 * b:8 * b + 4], ep[0:4, cols], ident[0:4, 0:4])
                    last = pe.transpose(banks[6 + q % 2][:, 8 * b + 4:8 * b + 7], dd[0:3, cols], ident[0:3, 0:3])
                last.then_inc(S["edge_cols_turned"], 1)

            pe.sem_inc(S["support_copied"], 1)
            with pe.Fori(0, Q) as q:
                pe.wait_ge(S["support_copied"], q + 1)
                for g in range(G):
                    pe.wait_ge(S["support_group_ready"], q * G + (g + 1))
                    for b in range(B):
                        t = B * g + b
                        last = pe.matmul(banks[2][:], H[:, t, :], groups[4 + g % 4][:, b, :], start=(t == 0), stop=(t == T - 1))
                    last.then_inc(freed[4 + g % 4], 1)

            pe.wait_ge(S["den_ready"], 2)
            pe.transpose(banks[0][0:HEADS * T, 0:P], nmf[:, 2, :], ident[:]).then_inc(S["nm_turned"], 1)
            pe.wait_ge(S["support_copied"], Q + 1)

            def turn_group(k):
                if k >= 2:
                    pe.wait_ge(S["hw_turn_copied"], k - 1)
                for b in range(B):
                    last = pe.transpose(banks[3 + k % 2][:, b * P:(b + 1) * P], H[:, B * k + b, :], ident[:])
                last.then_inc(S["hw_turned"], 1)

            turn_group(0)
            turn_group(1)
            for k in range(G):
                pe.wait_ge(S["hw_turn_copied"], k + 1)
                for t in range(B * k, B * k + B):
                    if t >= 2:
                        pe.wait_ge(S["hw_copied"], t - 1)
                    pe.matmul(banks[1 + t % 2][:, 0:HEADS * C], hT_pair[k % 2][:, (t - B * k) * P:(t - B * k + 1) * P], gw,
                              start=True, stop=True).then_inc(S["hw_ready"], 1)
                if k + 2 < G:
                    turn_group(k + 2)
            pe.wait_ge(S["hw_copied"], T)

            for _ in range(2):
                pe.sem_inc(S["att_copied"], 1)
            with pe.Fori(0, Q // 2) as qq:
                for i in range(2):
                    q = qq * 2 + i
                    pe.wait_ge(S["att_copied"], q + 1)
                    for k in range(G * HEADS):
                        g, h = k // HEADS, k % HEADS
                        if h < HEADS - 1:
                            pe.wait_ge(S["heads_ready"], q * (G * (HEADS - 1)) + ((HEADS - 1) * g + h + 1))
                        else:
                            pe.wait_ge(S["last_head_ready"], q * G + (g + 1))
                        for b in range(B):
                            last = pe.matmul(banks[i][:], hW[:, B * g + b, h * C:(h + 1) * C], probs[k % 4][:, b, :],
                                             start=(k == 0 and b == 0), stop=(k == G * HEADS - 1 and b == B - 1))
                        last.then_inc(S["probs_free"], 1)

            def gates(q, cell):
                n = 2 * q + cell
                if q:
                    pe.wait_ge(S["gru_out"], n - 1)
                    if cell == 0 and q >= 2:
                        pe.wait_ge(S["gru_scaled"], q - 1)
                bank, chunk_q = banks[4 * cell:4 * cell + 4], slice(q * CH, (q + 1) * CH)
                xin = (supT, attT)[cell][:, chunk_q]
                for gate in range(2):
                    pe.matmul(bank[gate][:], wx[cell][:, gate * C:(gate + 1) * C], xin, start=True, stop=False)
                    pe.matmul(bank[gate][:], wh[cell][:, gate * C:(gate + 1) * C], HT[:, chunk_q], start=False, stop=True)
                pe.matmul(bank[2][:], wx[cell][:, 2 * C:], xin, start=True, stop=True)
                pe.matmul(bank[3][:], wh[cell][:, 2 * C:], HT[:, chunk_q], start=True, stop=True).then_inc(S["gates_done"], 1)

            def turn_gru(q):
                pe.wait_ge(S["gru_out"], min(2 * q + 3, 2 * Q))
                for b in range(B):
                    last = pe.transpose(banks[3][:, b * P:(b + 1) * P], so[q % 2][:, b * P:(b + 1) * P], ident[:])
                last.then_inc(S["gru_turned"], 1)

            for q in range(Q):
                if q % 2 == 0:
                    pe.wait_ge(cells_loaded[q // 2], 48)
                gates(q, 0)
                gates(q, 1)
                if q:
                    turn_gru(q - 1)
            turn_gru(Q - 1)

            for k in turn(1):
                if k:
                    project(k - 1, w1s[:])
            project(G - 1, w1s[:])

            def turn_normalised(q):
                pe.wait_ge(S["h_ready"], q + (2 * G + 1))
                for b in range(B):
                    last = pe.transpose(banks[5][:, b * P:(b + 1) * P], h4[:, b, :], ident[:])
                last.then_inc(S["tiles_turned"], 1)

            def project_chunk(q):
                pe.wait_ge(S["turn_copied"], q + (2 * G + 1))
                for b in range(B):
                    last = pe.matmul(banks[6][:, b * P:(b + 1) * P], hT4[:, b * P:(b + 1) * P], w2s[:], start=True, stop=True)
                last.then_inc(S["mx_done"], 1)

            def hyperbolic(q, first):
                if not first:
                    pe.wait_ge(S["chunk_evacuated"], q)
                for g in range(G):
                    if first:
                        pe.wait_ge(S["tangent_ready"], g + 1)
                    elif g == 6:
                        turn_normalised(q - 1)
                    elif g == 7:
                        project_chunk(q - 1)
                    pe.wait_ge(loaded[g], q * 16 + 16 * (used[PASS_HYP] + 1))
                    for b in range(B):
                        last = pe.matmul(banks[0][:], M1[:, B * g + b, :], groups[g][:, b, :],
                                         start=(g == 0 and b == 0), stop=(g == G - 1 and b == B - 1))
                    last.then_inc(freed[g], 1)
                turn_chunk(q, 0)

            hyperbolic(0, True)
            with pe.Fori(1, Q) as q:
                hyperbolic(q, False)
            turn_normalised(Q - 1)
            project_chunk(Q - 1)

            pe.wait_ge(S["gat_cols_turned"], 1)
            pe.transpose(banks[2][0:T, 0:P], s[:, 9, :], ident[:]).then_inc(S["gat_cols_turned"], 1)
            pe.wait_ge(S["gat_max_done"], 1)
            pe.transpose(banks[2][0:2 * T, 0:P], s[:, 4:6, :].rearrange("p a t -> p (a t)"), ident[:])\
                .then_inc(S["gat_cols_turned"], 1)

            def attend(q, first):
                if not first:
                    pe.wait_ge(S["chunk_evacuated"], q + 8)
                for g in range(G):
                    pe.wait_ge(S["gat_w_ready"], q * G + (g + 1))
                    if g == 3 and not first:
                        finish(q - 1)
                    for b in range(B):
                        last = pe.matmul(banks[0][:], M2[:, B * g + b, :], gat_p[g % 4][:, b, :],
                                         start=(g == 0 and b == 0), stop=(g == G - 1 and b == B - 1))
                    last.then_inc(S["gat_w_free"], 1)
                if not first:
                    pe.wait_ge(S["den_out"], q)
                pe.wait_ge(S["gat_summed"], q * (G - 1) + (G - 1))
                for b in range(B):
                    last = pe.matmul(banks[3][0:1, :], ones[:], w_sum[:, b, :], start=(b == 0), stop=(b == B - 1))
                last.then_inc(S["den_summed"], 1)

            def finish(q):
                turn_chunk(q, 1)
                pe.wait_ge(S["den_out"], q + 1)
                settle(pe, "pe_settled")
                for b in range(B):
                    last = pe.transpose(banks[4][:, b:b + 1], den_c[0:1, b * P:(b + 1) * P], ident[0:1, 0:1])
                last.then_inc(S["den_turned"], 1)

            attend(0, True)
            with pe.Fori(1, Q) as q:
                attend(q, False)
            finish(Q - 1)

            product(PASS_SPEC, 2, H, (S["h_ready"], 3 * G))
            pe.wait_ge(S["chunk_stored"], 3 * Q)
            product(PASS_BACK, 3, M1)

        @block.scalar
        def _(act):
            def root(l, q):
                act.wait_ge(S["ln_var"], q + (G * l + 1))
                act.activation(ln[:, 1, :], ln[:, 0, :], ACT.Sqrt).then_inc(S["ln_sd"], 1)

            def turn_copy(l, k):
                act.wait_ge(S["tiles_turned"], G * l + k + 1)
                act.activation(HT[:, k * CH:(k + 1) * CH], banks[(G * l + k) % 2][:], ACT.Copy)\
                    .then_inc(S["turn_copied"], 1)

            def evacuate(q, p, u):
                act.wait_ge(freed[G - 1], q + (used[p] + 2))
                act.activation(chunk, banks[0][:], ACT.Copy).then_inc(S["chunk_evacuated"], 1)
                act.wait_ge(S["chunk_turned"], q + (8 * u + 1))

            for q in range(Q):
                root(0, q)
                if q == 0:
                    act.wait_ge(S["u_ready"], 1)
                    act.activation(U[:], banks[4][:, 0:6], ACT.Copy).then_inc(S["u_ready"], 1)
                else:
                    turn_copy(0, q - 1)
            turn_copy(0, Q - 1)
            act.wait_ge(S["v_ready"], G)
            act.activation(V.rearrange("p t v -> p (t v)"), banks[5][:, 0:6 * T], ACT.Copy).then_inc(S["v_copied"], 1)

            act.wait_ge(S["sums_cleared"], 1)
            with act.Fori(0, Q) as q:
                act.wait_ge(freed[G - 1], q + 2)
                act.activation(sums[0:VC, bass.ds(q * CH, CH)], banks[3][0:VC, :], ACT.Copy).then_inc(S["sums_copied"], 1)
                act.activation(sums[NEG0:NEG0 + VC, bass.ds(q * CH, CH)], banks[4][NEG0:NEG0 + VC, :], ACT.Copy)\
                    .then_inc(S["sums_copied"], 1)

            for q in range(Q):
                act.wait_ge(S["edges_summed"], q + 1)
                if q >= 2:
                    act.wait_ge(S["edges_ready"], q - 1)
                act.activation(slope_p[q % 2][0:4, :], banks[2 * (q % 2)][0:4, :], ACT.Copy, scale=SLOPE)\
                    .then_inc(S["edges_sloped"], 1)
                act.activation(slope_m[q % 2][0:3, :], banks[2 * (q % 2) + 1][0:3, :], ACT.Copy, scale=SLOPE)\
                    .then_inc(S["edges_sloped"], 1)

            roots, tanhs, logs = Count(), Count(), Count()

            def row_root(s_, a, b_):
                act.wait_ge(S["norms_ready"], roots())
                act.activation(s_[:, b_, :], s_[:, a, :], ACT.Sqrt).then_inc(S["norms_rooted"], 1)

            def row_tanh(s_, a, b_):
                act.wait_ge(S["tanh_in"], tanhs())
                act.activation(s_[:, b_, :], s_[:, a, :], ACT.Tanh).then_inc(S["tanh_out"], 1)

            def row_log(s_):
                act.wait_ge(S["log_in"], logs())
                act.activation(s_[:, 11, :], s_[:, 11, :], ACT.Ln).then_inc(S["log_out"], 1)

            row_root(s, 13, 13)
            row_tanh(s, 14, 14)

            for part in range(4):
                with act.Fori(0, 2) as i:
                    for g in range(G):
                        if g % 2 == 0:
                            slot = (g + 1) % 4
                            act.wait_ge(loaded[slot], i * 32 + 16 * (used[PASS_MAX] + 4 * part + (g + 1) // 4 + 1))
                            if part in (0, 3):
                                act.wait_ge(S["blocks_cleared"], i * G + (2 * G * (part // 3) + g + 2))
                            settle(act, "act_settled")
                            act.activation(not_positive_edge, ring[slot], ACT.Relu, bias=ones[:], scale=-STEEP)\
                                .then_inc(S["no_edge_ready"], 1)
                        for h in range(HEADS):
                            k = HEADS * g + h
                            act.wait_ge(S["logits_ready"], i * (G * HEADS) + (2 * part * G * HEADS + k + 1))
                            col = DEN.rearrange("p a n -> p (a n)")[:, bass.ds(i * (G * HEADS) + (2 * part * G * HEADS + k), 1)]
                            act.activation(logits[k % 3], logits[k % 3], ACT.Exp, bias=nmx[:, k:k + 1], scale=-1.0,
                                           accum_out=col).then_inc(S["logits_used"], 1)
                        if g in (1, 6):
                            with act.If(i) if part == 0 else nullcontext():
                                if g == 1:
                                    act.wait_ge(freed[G - 1], i * 2 + (used[PASS_MAX] + 4 * part + 1))
                                    act.activation(sup_c, banks[2][:], ACT.Copy).then_inc(S["support_copied"], 1)
                                else:
                                    act.wait_ge(S["support_stored"], i * 16 + 2 * part * 16)
                                    settle(act, "act_settled")
            act.wait_ge(freed[G - 1], used[PASS_HEADS] + 1)
            act.activation(sup_c, banks[2][:], ACT.Copy).then_inc(S["support_copied"], 1)
            act.wait_ge(S["row_max_final"], 1)
            act.activation(s_flat(s, 0), s_flat(s, 0), ACT.Exp).then_inc(S["den_scaled"], 1)
            act.activation(s_flat(s, 1), s_flat(s, 1), ACT.Exp).then_inc(S["den_scaled"], 1)
            act.wait_ge(S["den_ready"], 1)
            act.activation(nmf[:, 1, :], nmf[:, 1, :], ACT.Ln).then_inc(S["den_scaled"], 1)
            act.wait_ge(S["nm_turned"], 1)
            act.activation(rows[:], banks[0][0:HEADS * T, 0:P], ACT.Copy).then_inc(S["nm_rows_ready"], 1)
            for t in range(T):
                act.wait_ge(S["hw_ready"], t + 1)
                act.activation(hW[:, t, :], banks[1 + t % 2][:, 0:HEADS * C], ACT.Copy).then_inc(S["hw_copied"], 1)

            with act.Fori(0, Q // 2) as qq:
                for i in range(2):
                    q = qq * 2 + i
                    for k in range(G * HEADS):
                        act.wait_ge(S["exponents_ready"], q * (G * HEADS * B) + B * (k + 1))
                        flat = probs[k % 4].rearrange("p b i -> p (b i)")
                        act.activation(flat, flat, ACT.Exp).then_inc(S["probs_ready"], 1)
                        if k == 4:
                            with act.If(qq) if i == 0 else nullcontext():
                                act.wait_ge(S["probs_free"], q * (G * HEADS) + 4)
                                act.activation(att_c, banks[1 - i][:], ACT.Copy, scale=1.0 / HEADS)\
                                    .then_inc(S["att_copied"], 1)
                        if k == 16:
                            with act.If(qq) if i == 0 else nullcontext():
                                act.wait_ge(S["att_stored"], q * 16)
                                settle(act, "act_settled")
            act.wait_ge(S["probs_free"], Q * G * HEADS + 4)
            act.activation(att_c, banks[1][:], ACT.Copy, scale=1.0 / HEADS).then_inc(S["att_copied"], 1)

            def scale_chunk(q):
                act.wait_ge(S["gru_turned"], q + 1)
                if q:
                    act.wait_ge(S["x_added"], q)
                for b in range(B):
                    last = act.activation(x_add[:, b * C:(b + 1) * C], banks[3][:, b * C:(b + 1) * C], ACT.Copy,
                                          scale=dg[:, B * q + b:B * q + b + 1])
                last.then_inc(S["gru_scaled"], 1)

            def relu_chunk(q):
                act.wait_ge(S["ln_factors"], q + 1)
                for b in range(B):
                    t = B * q + b
                    last = act.activation(H[:, t, :], X[:, t, :], ACT.Relu, bias=ln[:, 2, b:b + 1], scale=ln[:, 1, b:b + 1])
                last.then_inc(S["h_ready"], 1)
                act.wait_ge(S["h_ready"], G + q + 1)

            squared = Count()

            def row_squares(i, rows_of, q):
                n = squared()
                if n > 1:
                    act.wait_ge(S["squares_ready"], n - 1)
                for b in range(B):
                    t = B * q + b
                    last = act.activation(junk[:, b, :], rows_of[:, t, :], ACT.Square, accum_out=s[:, i, t:t + 1])
                last.then_inc(S["squares_ready"], 1)

            for q in range(Q):
                for cell in range(2):
                    n, bank = 2 * q + cell, banks[4 * cell:4 * cell + 4]
                    act.wait_ge(S["gates_done"], n + 1)
                    if q:
                        act.wait_ge(S["gru_out"], n - 1)
                    act.activation(gr[cell], bank[0][:], ACT.Tanh, bias=bsum[:, cell, 0:1], scale=0.5).then_inc(S["gate_r"], 1)
                    act.activation(gz[cell], bank[1][:], ACT.Tanh, bias=bsum[:, cell, 1:2], scale=0.5).then_inc(S["gate_z"], 1)
                    if cell == 0 and q >= 2:
                        root(1, q - 2)
                    if cell == 1 and q >= 2:
                        relu_chunk(q - 2)
                    act.wait_ge(S["gate_n_in"], n + 1)
                    act.activation(gn[cell], gt[cell], ACT.Tanh, bias=bi[:, cell, 2:3]).then_inc(S["gate_n"], 1)
                    if cell == 0 and q:
                        scale_chunk(q - 1)
                    if cell == 1 and q >= 2:
                        row_squares(3, H, q - 2)
            root(1, Q - 2)
            scale_chunk(Q - 1)
            relu_chunk(Q - 2)
            row_squares(3, H, Q - 2)
            root(1, Q - 1)
            relu_chunk(Q - 1)
            row_squares(3, H, Q - 1)

            def project_copy(k):
                act.wait_ge(S["mx_done"], k + 1)
                act.activation(M1[:, B * k:B * k + B, :].rearrange("p b c -> p (b c)"), banks[2 + k % 2][:], ACT.Copy)\
                    .then_inc(S["mx_copied"], 1)
                act.wait_ge(S["mx_copied"], k + 1)
                row_squares(5, M1, k)

            for k in range(G):
                turn_copy(1, k)
                if k:
                    project_copy(k - 1)
            project_copy(G - 1)
            row_root(s, 3, 4)
            row_root(s, 5, 6)
            row_log(s)
            row_tanh(s, 8, 8)
            row_root(s, 3, 4)
            row_log(s)

            with act.Fori(0, Q) as q:
                for c, per in ((roots, 2), (tanhs, 2), (logs, 1)):
                    c.enter(q, per)
                evacuate(q, PASS_HYP, 0)
                act.activation(acc4.rearrange("p b c -> p (b c)"), banks[1][:], ACT.Copy).then_inc(S["chunk_stored"], 1)
                row_root(s4, 3, 4)
                row_root(s4, 5, 6)
                row_tanh(s4, 8, 8)
                row_log(s4)
                row_tanh(s4, 8, 8)
                root(2, q)
                act.wait_ge(S["tiles_turned"], q + (2 * G + 1))
                act.activation(hT4, banks[5][:], ACT.Copy).then_inc(S["turn_copied"], 1)
                act.wait_ge(S["mx_done"], q + (G + 1))
                act.activation(M2[:, bass.ds(q * B, B), :].rearrange("p b c -> p (b c)"), banks[6][:], ACT.Copy)\
                    .then_inc(S["mx_copied"], 1)
            for c in (roots, tanhs, logs):
                c.leave(Q)

            act.wait_ge(S["gat_cols_turned"], 2)
            act.activation(rows[0:T, :], banks[2][0:T, 0:P], ACT.Copy).then_inc(S["gat_rows_ready"], 1)
            for _ in range(2):
                act.sem_inc(S["signs_used"], 1)
            for half in range(2):
                with act.Fori(0, 4) as i:
                    for g in range(G):
                        act.wait_ge(loaded[g], i * 16 + 16 * (used[PASS_GATMAX] + 4 * half + 1))
                        act.wait_ge(S["signs_used"], i * G + (4 * G * half + g + 1))
                        settle(act, "act_settled")
                        act.activation(not_positive[g % 2], ring[g], ACT.Relu, bias=ones[:], scale=-STEEP)\
                            .then_inc(S["signs_ready"], 1)
                        act.wait_ge(S["signs_ready"], i * G + (4 * G * half + g + 1))
                        act.sem_inc(freed[g], 1)
            act.wait_ge(S["gat_cols_turned"], 3)
            act.wait_ge(S["gat_rows_stored"], 16)
            act.activation(rows[0:2 * T, :], banks[2][0:2 * T, 0:P], ACT.Copy).then_inc(S["gat_rows_ready"], 1)
            act.wait_ge(S["first_dst_loaded"], 32)

            def slopes(q, g, first):
                if g >= 4 or not first:
                    act.wait_ge(S["gat_w_free"], q * G + (g - 3))
                    act.wait_ge(S["gat_summed"], q * (G - 1) + (max(g - 4, 1) if g >= 4 else g - 3))
                    settle(act, "act_settled")
                for b in range(B):
                    act.activation(gat_p[g % 4][:, b, :], dst_all[1][:, bass.ds(q * CH, CH)], ACT.Identity, scale=1.0,
                                   bias=s[:, 8, B * g + b:B * g + b + 1]).then_inc(S["gat_slope_ready"], 1)

            def copy_chunk(q):
                act.wait_ge(S["gat_w_free"], q * G + G)
                act.activation(chunk, banks[0][:], ACT.Copy).then_inc(S["chunk_evacuated"], 1)

            def copy_denominators(q):
                act.wait_ge(S["den_summed"], q + 1)
                act.activation(den_c, banks[3][0:1, :], ACT.Copy).then_inc(S["den_out"], 1)

            def store_chunk(q):
                act.wait_ge(S["chunk_turned"], q + (8 + 1))
                act.activation(ACC[:, bass.ds(q * B, B), :].rearrange("p b c -> p (b c)"), banks[1][:], ACT.Copy)\
                    .then_inc(S["chunk_stored"], 1)
                act.wait_ge(S["den_turned"], q + 1)
                act.activation(s[:, 6, :][:, bass.ds(q * B, B)], banks[4][:, 0:B], ACT.Copy).then_inc(S["acc_used"], 1)

            def attention(q, first, more):
                for g in range(G):
                    if g < G - 1:
                        slopes(q, g + 1, first)
                    elif more:
                        if first:
                            act.wait_ge(S["dst_loaded"], 32)
                        slopes(q + 1, 0, False)
                    act.wait_ge(S["gat_logit_ready"], q * (G * B) + B * (g + 1))
                    flat = gat_p[g % 4].rearrange("p b i -> p (b i)")
                    act.activation(flat, flat, ACT.Exp).then_inc(S["gat_exp_ready"], 1)
                    if not first:
                        if g == 2:
                            copy_chunk(q - 1)
                        if g == 3:
                            copy_denominators(q - 1)
                        if g == 6:
                            store_chunk(q - 1)

            slopes(0, 0, True)
            attention(0, True, True)
            with act.Fori(1, Q - 1) as q:
                attention(q, False, True)
            attention(Q - 1, False, False)
            copy_chunk(Q - 1)
            copy_denominators(Q - 1)
            store_chunk(Q - 1)
            with act.Fori(0, Q // 2) as qq:
                for q in (qq * 2, qq * 2 + 1):
                    act.wait_ge(S["exp_in"], q + 1)
                    flat = TMP[:, bass.ds(q * B, B), :].rearrange("p b c -> p (b c)")
                    act.activation(flat, flat, ACT.Exp).then_inc(S["exp_out"], 1)
            with act.Fori(0, Q // 2) as qq:
                for q in (qq * 2, qq * 2 + 1):
                    root(3, q)
                    act.wait_ge(S["ln_factors"], q + (Q + 1))
                    for b in range(B):
                        x_row, h_row = (a[:, bass.ds(q * B + b, 1), :].rearrange("p b c -> p (b c)") for a in (X, H))
                        last = act.activation(h_row, x_row, ACT.Relu, bias=ln[:, 2, b:b + 1], scale=ln[:, 1, b:b + 1])
                    last.then_inc(S["h_ready"], 1)
                    act.wait_ge(S["h_ready"], q + (3 * G + 1))

            act.wait_ge(S["exp_in"], Q + 1)
            act.activation(s[:, 7, :], s[:, 7, :], ACT.Exp).then_inc(S["exp_out"], 1)
            act.wait_ge(S["exp_out"], Q + 1)
            with act.Fori(0, Q) as q:
                evacuate(q, PASS_SPEC, 2)
                for b in range(B):
                    last = act.activation(M1[:, bass.ds(q * B + b, 1), :].rearrange("p b c -> p (b c)"),
                                          banks[1][:, b * C:(b + 1) * C], ACT.Copy,
                                          scale=s[:, 7, :][:, bass.ds(q * B + b, 1)])
                last.then_inc(S["chunk_stored"], 1)
            with act.Fori(0, Q) as q:
                evacuate(q, PASS_BACK, 3)
                act.wait_ge(S["ready_to_store"], q + 1)
                settle(act, "act_settled")

        @block.vector
        def _(dve):
            ch = Chain(dve, S["dve_chain"])
            signed_chain, plain_chain = Chain(dve, S["signed_chain"]), Chain(dve, S["plain_chain"])
            v = nc.vector

            def sc(i):
                return s[:, i, :]

            def ts(o, a, s1, s2, op0, op1=ALU.bypass):
                ch(v.tensor_scalar(o, a, s1, s2, op0, op1) if s2 is not None else v.tensor_scalar(o, a, s1, None, op0))

            def tt(o, a, b_, op):
                ch(v.tensor_tensor(o, a, b_, op))

            def x_tile(q, b):
                return X[:, bass.ds(q * B + b, 1), :].rearrange("p b c -> p (b c)")

            def variances(l, q):
                settle(dve, "dve_settled")
                for b in range(B):
                    (ch if b == B - 1 else ch.also)(v.bn_stats(bn[:, b, :], x_tile(q, b)))
                settle(dve, "dve_settled")
                for b in range(B):
                    (ch if b == B - 1 else ch.also)(v.bn_aggr(mv[:, b, :], bn[:, b, :]))
                v.tensor_scalar(ln[:, 0, :], mv[:, :, 1], 1e-5, None, ALU.add).then_inc(S["ln_var"], 1)

            def factors(l, q, last=True):
                r, nb = ln[:, 1, :], ln[:, 2, :]
                dve.wait_ge(S["ln_sd"], q + (G * l + 1))
                if last:
                    dve.wait_ge(S["h_ready"], q + G * l)
                ch(v.reciprocal(r, r))
                tt(ln[:, 3, :], r, r, ALU.mult)
                ch(v.scalar_tensor_tensor(ln[:, 3, :], ln[:, 3, :], -0.5, ln[:, 0, :], ALU.mult, ALU.mult))
                ch(v.scalar_tensor_tensor(r, ln[:, 3, :], 1.5, r, ALU.add, ALU.mult))
                final = v.scalar_tensor_tensor(nb, mv[:, :, 0], -1.0, r, ALU.mult, ALU.mult)
                if last:
                    final.then_inc(S["ln_factors"], 1)
                    dve.wait_ge(S["ln_factors"], q + (1 if l == 1 else Q + 1))
                else:
                    ch(final)

            def normalise(l, q, h_of):
                r, nb = ln[:, 1, :], ln[:, 2, :]
                factors(l, q, last=False)
                for b in range(B):
                    (ch if b == B - 1 else ch.also)(v.tensor_scalar(h_of[:, b, :], x_tile(q, b), r[:, b:b + 1], nb[:, b:b + 1],
                                                                    ALU.mult, ALU.add))
                v.tensor_scalar(h_of, h_of, 0.0, None, ALU.max).then_inc(S["h_ready"], 1)
                dve.wait_ge(S["h_ready"], q + (G * l + 1))

            for q in range(Q):
                if q % 2 == 0:
                    dve.wait_ge(x_loaded[q // 2], 16)
                variances(0, q)
                normalise(0, q, H[:, B * q:B * q + B, :])
            ch(v.memset(V19, 1.0))
            v.memset(sums, 0.0).then_inc(S["sums_cleared"], 1)
            dve.wait_ge(S["v_copied"], 1)
            for part in range(3):
                src = V if part == 0 else VR
                dst = V19[:, :, 1 + 6 * part:7 + 6 * part]
                if part < 2:
                    ch(v.tensor_copy(dst, src))
                    tt(VR, src, dst, ALU.subtract)
                else:
                    v.tensor_copy(dst, src).then_inc(S["v19_ready"], 1)

            def clear_diagonal(q, g, link):
                diag_ap = diagonal_blocks(g)
                m = not_i[:, bass.ds(q * P + (7 - g) * P, P)].unsqueeze(1).broadcast_to([P, B, P])
                link(v.tensor_tensor(diag_ap, diag_ap, m, ALU.mult))

            dve.wait_ge(S["first_loaded"], 64)
            with dve.Fori(0, Q) as q:
                ch.enter(q, G)
                for g in range(G):
                    dve.wait_ge(loaded[g], q * 16 + 16)
                    clear_diagonal(q, g, ch)
                    if g >= 2:
                        dve.wait_ge(freed[g - 2], q + 2)
                    else:
                        dve.wait_ge(freed[g + 6], q + 1)
                    v.tensor_scalar(mask_pos[g % 2], groups[g], 0.0, None, ALU.is_gt).then_inc(S["masks_ready"], 1)
                    v.tensor_scalar(mask_neg[g % 2], groups[g], 0.0, None, ALU.is_lt)\
                        .then_inc(S["masks_ready"], 1)
            ch.leave(Q)
            dve.wait_ge(S["const_loaded"], 16 * N_LOADS)
            dve.wait_ge(freed[G - 1], Q + 1)

            def copy_cols(q):
                dve.wait_ge(S["edge_cols_turned"], q + 1)
                v.tensor_copy(ecol[:, B * q:B * q + B, 0:7],
                              banks[6 + q % 2][:, 0:8 * B].rearrange("p (b k) -> p b k", k=8)[:, :, 0:7])\
                    .then_inc(S["edge_cols_copied"], 1)

            for q in range(Q):
                cols, plus, minus = slice(q * CH, (q + 1) * CH), banks[2 * (q % 2)], banks[2 * (q % 2) + 1]
                dve.wait_ge(S["edges_summed"], q + 1)
                dve.wait_ge(S["edges_sloped"], 2 * q + 2)
                ch.also(v.tensor_tensor(ep[:, cols], slope_p[q % 2][0:4, :], plus[0:4, :], ALU.max))
                if q:
                    dve.wait_ge(S["edges_ready"], q)
                tt(em[0:3, :], slope_m[q % 2][0:3, :], minus[0:3, :], ALU.max)
                v.tensor_tensor(dd[:, cols], em[0:3, :], ep[0:3, cols], ALU.subtract).then_inc(S["edges_ready"], 1)
                if q:
                    copy_cols(q - 1)
            copy_cols(Q - 1)
            dve.wait_ge(S["edge_cols_copied"], Q)
            v.tensor_scalar(ep[0:3, :], ep[0:3, :], -NEAR_UNIT, None, ALU.mult).then_inc(S["edges_scaled"], 1)
            v.tensor_scalar(dd, dd, -NEAR_UNIT, None, ALU.mult).then_inc(S["edges_scaled"], 1)
            at_count = slice(NEG0, NEG0 + 1)
            ch(v.tensor_reduce(flag[at_count, :], sums[at_count, :], AX.X, ALU.max))
            v.tensor_copy(flag_i[at_count, :], flag[at_count, :]).then_inc(S["flag_ready"], 1)
            dve.wait_ge(S["flag_ready"], 1)
            any_negative = dve.value_load(flag_i[NEG0:NEG0 + 1, 0:1], min_val=0, max_val=N)

            roots, tanhs, logs = Count(), Count(), Count()

            def rooted(ins):
                ins.then_inc(S["norms_ready"], 1)
                dve.wait_ge(S["norms_rooted"], roots())

            def tanhed(ins):
                ins.then_inc(S["tanh_in"], 1)
                dve.wait_ge(S["tanh_out"], tanhs())

            def artanh(s_, a, o):
                x_, x2, lg, se = (s_[:, i, :] for i in (9, 10, 11, 12))
                ts(x_, s_[:, a, :], CLIP, None, ALU.min)
                ts(lg, x_, -1.0, 1.0, ALU.mult, ALU.add)
                ch(v.reciprocal(lg, lg))
                logs_at = logs()
                v.scalar_tensor_tensor(lg, x_, 1.0, lg, ALU.add, ALU.mult).then_inc(S["log_in"], 1)
                tt(x2, x_, x_, ALU.mult)
                ts(se, x2, 1.0 / 17, None, ALU.mult)
                for odd in (15, 13, 11, 9, 7, 5, 3):
                    ch(v.scalar_tensor_tensor(se, se, 1.0 / odd, x2, ALU.add, ALU.mult))
                ch(v.scalar_tensor_tensor(se, se, 1.0, x_, ALU.add, ALU.mult))
                ts(x2, x_, 0.25, None, ALU.is_lt)
                tt(se, se, x2, ALU.mult)
                ts(x2, x_, 0.25, 0.5, ALU.is_ge, ALU.mult)
                dve.wait_ge(S["log_out"], logs_at)
                tt(lg, lg, x2, ALU.mult)
                tt(s_[:, o, :], lg, se, ALU.add)

            def over(s_, o, a, b_):
                ch(v.reciprocal(s_[:, 12, :], s_[:, b_, :]))
                tt(s_[:, o, :], s_[:, a, :], s_[:, 12, :], ALU.mult)

            tt(bsum[:], bi[:], bh[:], ALU.add)
            ts(bsum[:], bsum[:], 0.5, None, ALU.mult)
            ch(v.tensor_tensor(avec[:, 3, :], avec[:, 0, :], avec[:, 0, :], ALU.mult))
            ch(v.memset(sc(13), 0.0))
            rooted(v.tensor_reduce(s[:, 13, 0:1], avec[:, 3, :], AX.X, ALU.add))
            ts(sc(13), sc(13), TINY, None, ALU.max)
            tanhed(v.tensor_copy(sc(14), sc(13)))
            ts(sc(14), sc(14), MAXNORM, None, ALU.min)
            over(s, 15, 14, 13)
            ch(v.tensor_scalar(avec[:, 3, :], avec[:, 0, :], s[:, 15, 0:1], None, ALU.mult))
            tt(s[:, 16, 0:1], s[:, 14, 0:1], s[:, 14, 0:1], ALU.mult)
            y2 = s[:, 16, 0:1]

            dve.wait_ge(S["hT_stored"], 16)
            dve.wait_ge(S["logits_used"], 3)
            def maxima_part(part, link, signed):
                half, on_diagonal = part // 2, part in (0, 3)
                if part % 2 == 0 and signed:
                    dve.wait_ge(S["e_broadcast"], 16 * HEADS * (half + 1))
                    dve.wait_ge(S["second_broadcast"], 16 * HEADS * (half + 1))
                elif part % 2 == 0:
                    dve.wait_ge(S["second_broadcast" if half else "e_broadcast"], 16 * HEADS)
                with dve.Fori(0, 2) as i:
                    link.enter(i, (G + 2 * G * HEADS if signed else G // 2) + 1)
                    for g in range(G):
                        half_rows = ring[g % 4]
                        dve.wait_ge(loaded[g % 4], i * 32 + 16 * (used[PASS_MAX] + 4 * part + g // 4 + 1))
                        if on_diagonal:
                            dve.wait_ge(S["blocks_cleared"], i * G + (2 * G * half + g + 1))
                        if g % 2:
                            dve.wait_ge(S["no_edge_ready"], i * (G // 2) + (G * part + (g + 1) // 2))
                        mask = not_positive_edge if g % 2 and not signed else no_edge
                        if mask is no_edge:
                            link(v.tensor_scalar(no_edge, half_rows, 0.0, None, ALU.is_equal))
                        for h in range(HEADS):
                            k = HEADS * g + h
                            e_row = e_bc[:, h if signed else half * HEADS + h, :]
                            if signed:
                                if h:
                                    dve.wait_ge(S["logits_ready"], i * (G * HEADS) + (2 * part * G * HEADS + k))
                                link(v.scalar_tensor_tensor(signed_e, half_rows, 0.0, e_bc[:, HEADS + h, :],
                                                            ALU.is_lt, ALU.mult))
                                link(v.tensor_tensor(signed_e, signed_e, e_row, ALU.add))
                                e_row = signed_e
                            dve.wait_ge(S["logits_used"], i * (G * HEADS) + (2 * part * G * HEADS + k + 1))
                            settle(dve, "dve_settled")
                            v.tensor_tensor_reduce(logits[k % 3], mask, e_row, FAR_UNIT, FAR,
                                                   ALU.add, ALU.min, nmx[:, k:k + 1]).then_inc(S["logits_ready"], 1)
                        dve.wait_ge(S["logits_ready"], i * (G * HEADS) + (2 * part * G * HEADS + HEADS * g + HEADS))
                        v.sem_inc(freed[g % 4], 1)
                    col = NM.rearrange("p a n -> p (a n)")[:, bass.ds(i * (G * HEADS) + 2 * part * G * HEADS, G * HEADS)]
                    link(v.tensor_copy(col, nmx[:]))
                link.leave(2)

            with dve.If(any_negative):
                for part in range(4):
                    maxima_part(part, signed_chain, True)
            with dve.Else():
                for part in range(4):
                    maxima_part(part, plain_chain, False)
            rt = "p (t h) -> p h t"
            by_head = nmf[:].rearrange("p a (h t) -> p a h t", h=HEADS)
            tt(by_head[:, 0], NM[:, 0, :].rearrange(rt, h=HEADS), NM[:, 1, :].rearrange(rt, h=HEADS), ALU.min)
            f0, f1 = s_flat(s, 0), s_flat(s, 1)
            tt(f0.rearrange("p (h t) -> p h t", h=HEADS), by_head[:, 0], NM[:, 0, :].rearrange(rt, h=HEADS), ALU.subtract)
            v.tensor_tensor(f1.rearrange("p (h t) -> p h t", h=HEADS), by_head[:, 0], NM[:, 1, :].rearrange(rt, h=HEADS),
                            ALU.subtract).then_inc(S["row_max_final"], 1)
            dve.wait_ge(S["den_scaled"], 2)
            tt(f0.rearrange("p (h t) -> p h t", h=HEADS), f0.rearrange("p (h t) -> p h t", h=HEADS),
               DEN[:, 0, :].rearrange(rt, h=HEADS), ALU.mult)
            tt(f1.rearrange("p (h t) -> p h t", h=HEADS), f1.rearrange("p (h t) -> p h t", h=HEADS),
               DEN[:, 1, :].rearrange(rt, h=HEADS), ALU.mult)
            v.tensor_tensor(nmf[:, 1, :], f0, f1, ALU.add).then_inc(S["den_ready"], 1)
            dve.wait_ge(S["den_scaled"], 3)
            v.tensor_tensor(nmf[:, 2, :], nmf[:, 0, :], nmf[:, 1, :], ALU.subtract).then_inc(S["den_ready"], 1)

            dve.wait_ge(S["logits_used"], 2 * T * HEADS + 3)
            for k in range(G):
                dve.wait_ge(S["hw_turned"], k + 1)
                if k >= 2:
                    dve.wait_ge(S["hw_ready"], B * (k - 1))
                v.tensor_copy(hT_pair[k % 2], banks[3 + k % 2][:]).then_inc(S["hw_turn_copied"], 1)
            dve.wait_ge(S["hw_ready"], T)

            dve.wait_ge(S["probs_free"], 4)

            LAST = G * HEADS

            def exponents(q, qq, i, k, link, signed):
                g, h = k // HEADS, k % HEADS
                nm, buf = nm_c[i], probs[k % 4]
                if k == 0:
                    dve.wait_ge(nm_loaded[i], qq * (16 * HEADS) + 16 * HEADS)
                if h == 0:
                    dve.wait_ge(loaded[g], q * 16 + 16 * (used[PASS_HEADS] + 1))
                    clear_diagonal(q, g, link)
                    v.sem_inc(S["diagonal_clear"], 1)
                dve.wait_ge(S["probs_free"], q * LAST + (k + 1))
                settle(dve, "dve_settled")
                if signed:
                    for b in range(B):
                        link(v.tensor_scalar(buf[:, b, :], groups[g][:, b, :], 0.0,
                                             ecol[:, B * g + b, 4 + h:5 + h], ALU.is_lt, ALU.mult))
                    link(v.tensor_tensor(buf, buf, nm[:, h, :].unsqueeze(1).broadcast_to([P, B, CH]), ALU.add))
                for b in range(B):
                    v.tensor_scalar(buf[:, b, :], buf[:, b, :] if signed else nm[:, h, :],
                                    ecol[:, B * g + b, h:h + 1], 0.0,
                                    ALU.add, ALU.min).then_inc(S["exponents_ready"], 1)
                if k == LAST - 1:
                    dve.wait_ge(S["exponents_ready"], q * (LAST * B) + LAST * B)
                    v.sem_inc(S["nm_used"], 1)

            def weigh(q, k):
                g, h = k // HEADS, k % HEADS
                if h < HEADS - 1:
                    dve.wait_ge(S["probs_ready"], q * LAST + (k + 1))
                    v.tensor_tensor(probs[k % 4], probs[k % 4], groups[g], ALU.mult).then_inc(S["heads_ready"], 1)
                elif g:
                    dve.wait_ge(S["heads_ready"], q * (G * (HEADS - 1)) + (HEADS - 1) * (g + 1))
                    dve.wait_ge(S["last_head_ready"], q * G + g)
                    v.sem_inc(freed[g - 1], 1)

            def free_last_group(q):
                dve.wait_ge(S["last_head_ready"], q * G + G)
                v.sem_inc(freed[G - 1], 1)

            def heads_pair(qq, link, signed, more):
                for i in range(2):
                    q = qq * 2 + i
                    for k in range(LAST):
                        weigh(q, k)
                        if k + 2 < LAST:
                            exponents(q, qq, i, k + 2, link, signed)
                        elif i == 0:
                            exponents(q + 1, qq, 1, k + 2 - LAST, link, signed)
                        elif more:
                            exponents(q + 1, qq + 1, 0, k + 2 - LAST, link, signed)
                    free_last_group(q)

            def heads_pass(link, signed):
                for k in range(2):
                    exponents(0, 0, 0, k, link, signed)
                per = 2 * G * (1 + signed * HEADS * (B + 1))
                with dve.Fori(0, Q // 2 - 1) as qq:
                    link.enter(qq, per)
                    heads_pair(qq, link, signed, True)
                link.leave(Q // 2 - 1)
                heads_pair(Q // 2 - 1, link, signed, False)

            with dve.If(any_negative):
                heads_pass(signed_chain, True)
            with dve.Else():
                heads_pass(plain_chain, False)

            for q in range(Q):
                for cell in range(2):
                    n, bank = 2 * q + cell, banks[4 * cell:4 * cell + 4]
                    r, z, t_, h_new = gr[cell], gz[cell], gt[cell], gn[cell]
                    dve.wait_ge(S["gate_r"], n + 1)
                    ts(r, r, 0.5, 0.5, ALU.mult, ALU.add)
                    ch(v.scalar_tensor_tensor(t_, bank[3][:], bh[:, cell, 2:3], r, ALU.add, ALU.mult))
                    v.tensor_tensor(t_, t_, bank[2][:], ALU.add).then_inc(S["gate_n_in"], 1)
                    dve.wait_ge(S["gate_z"], n + 1)
                    dve.wait_ge(S["gate_n"], n + 1)
                    tt(t_, HT[:, q * CH:(q + 1) * CH], h_new, ALU.subtract)
                    ch(v.scalar_tensor_tensor(t_, z, 1.0, t_, ALU.add, ALU.mult))
                    if cell == 0:
                        if q >= 2:
                            dve.wait_ge(S["gru_turned"], q - 1)
                        v.scalar_tensor_tensor(so[q % 2], t_, 0.5, h_new, ALU.mult, ALU.add).then_inc(S["gru_out"], 1)
                    else:
                        ch(v.scalar_tensor_tensor(t_, t_, 0.5, h_new, ALU.mult, ALU.add))
                        dve.wait_ge(S["gru_out"], n)
                        v.tensor_tensor(so[q % 2], so[q % 2], t_, ALU.add).then_inc(S["gru_out"], 1)
                    if cell == 0 and q:
                        if q >= 2:
                            factors(1, q - 2)
                    elif q:
                        dve.wait_ge(S["x_added"], q)
                        variances(1, q - 1)
            factors(1, Q - 2)
            dve.wait_ge(S["x_added"], Q)
            variances(1, Q - 1)
            factors(1, Q - 1)

            def squares(o, a, tmp):
                tt(tmp, a, a, ALU.mult)
                rooted(v.tensor_reduce(o, tmp, AX.X, ALU.add))

            for k in range(G):
                tiles = slice(B * k, B * k + B)
                dve.wait_ge(S["mx_copied"], k + 1)
                tt(TMP[:, tiles, :], M1[:, tiles, :], avec[:, 3, :].unsqueeze(1).broadcast_to([P, B, C]), ALU.mult)
                ch(v.tensor_reduce(sc(17)[:, tiles], TMP[:, tiles, :], AX.X, ALU.add))
            dve.wait_ge(S["squares_ready"], 2 * G)
            rooted(v.tensor_copy(sc(18), sc(3)))
            rooted(v.tensor_copy(sc(18), sc(5)))
            ts(sc(4), sc(4), TINY, None, ALU.max)
            ts(sc(6), sc(6), TINY, None, ALU.max)
            artanh(s, 4, 7)
            over(s, 8, 6, 4)
            tanhed(v.tensor_tensor(sc(8), sc(8), sc(7), ALU.mult))
            ts(sc(8), sc(8), MAXNORM, None, ALU.min)
            over(s, 7, 8, 6)
            tt(sc(9), sc(17), sc(7), ALU.mult)
            ts(sc(9), sc(9), 2.0, 1.0, ALU.mult, ALU.add)
            tt(sc(10), sc(8), sc(8), ALU.mult)
            ts(sc(11), sc(9), y2, None, ALU.add)
            tt(sc(11), sc(11), sc(7), ALU.mult)
            ts(sc(13), sc(10), y2, None, ALU.mult)
            tt(sc(13), sc(13), sc(9), ALU.add)
            ts(sc(13), sc(13), TINY, None, ALU.max)
            ts(sc(10), sc(10), -1.0, 1.0, ALU.mult, ALU.add)
            ch(v.reciprocal(sc(12), sc(13)))
            tt(sc(14), sc(11), sc(12), ALU.mult)
            tt(sc(15), sc(10), sc(12), ALU.mult)
            tt(sc(3), sc(14), sc(5), ALU.mult)
            tt(sc(9), sc(15), sc(17), ALU.mult)
            ch(v.scalar_tensor_tensor(sc(3), sc(9), 2.0, sc(3), ALU.mult, ALU.add))
            tt(sc(3), sc(3), sc(14), ALU.mult)
            tt(sc(9), sc(15), sc(15), ALU.mult)
            ch(v.scalar_tensor_tensor(sc(3), sc(9), y2, sc(3), ALU.mult, ALU.add))
            rooted(v.tensor_scalar(sc(3), sc(3), 0.0, None, ALU.max))
            ts(sc(4), sc(4), TINY, None, ALU.max)
            ts(sc(5), sc(4), MAXNORM, None, ALU.min)
            artanh(s, 5, 7)
            over(s, 7, 7, 4)
            tt(sc(14), sc(14), sc(7), ALU.mult)
            tt(sc(15), sc(15), sc(7), ALU.mult)
            for g in range(G):
                tiles = slice(B * g, B * g + B)

                def factor(i):
                    return sc(i)[:, tiles].unsqueeze(2).broadcast_to([P, B, C])

                ch.also(v.tensor_tensor(M1[:, tiles, :], M1[:, tiles, :], factor(14), ALU.mult))
                tt(TMP[:, tiles, :], avec[:, 3, :].unsqueeze(1).broadcast_to([P, B, C]), factor(15), ALU.mult)
                v.tensor_tensor(M1[:, tiles, :], M1[:, tiles, :], TMP[:, tiles, :], ALU.add).then_inc(S["tangent_ready"], 1)
            dve.wait_ge(S["tangent_ready"], G)

            def c4(i):
                return s4[:, i, :]

            def wide4(col):
                return col.unsqueeze(2).broadcast_to([P, B, C])

            with dve.Fori(0, Q) as q:
                ch.enter(q, LINKS_3)
                for c, per in ((roots, 2), (tanhs, 2), (logs, 1)):
                    c.enter(q, per)
                dve.wait_ge(S["chunk_stored"], q + 1)
                squares(c4(3), acc4, tmp4)
                ts(acc4, acc4, 0.0, None, ALU.max)
                squares(c4(5), acc4, tmp4)
                ts(c4(4), c4(4), TINY, None, ALU.max)
                tanhed(v.tensor_copy(c4(8), c4(4)))
                ts(c4(8), c4(8), MAXNORM, TINY, ALU.min, ALU.max)
                artanh(s4, 8, 7)
                over(s4, 7, 7, 4)
                tt(c4(5), c4(7), c4(6), ALU.mult)
                ts(c4(5), c4(5), TINY, None, ALU.max)
                tanhed(v.tensor_copy(c4(8), c4(5)))
                ts(c4(8), c4(8), MAXNORM, None, ALU.min)
                over(s4, 8, 8, 5)
                tt(c4(8), c4(8), c4(7), ALU.mult)
                tt(acc4, acc4, wide4(c4(8)), ALU.mult)
                x4 = X[:, bass.ds(q * B, B), :]
                tt(x4, x4, acc4, ALU.add)
                variances(2, q)
                normalise(2, q, h4)
                dve.wait_ge(S["mx_copied"], q + (G + 1))
                m4 = M2[:, bass.ds(q * B, B), :]
                for i in range(2):
                    tt(tmp4, m4, avec[:, 1 + i, :].unsqueeze(1).broadcast_to([P, B, C]), ALU.mult)
                    ch(v.tensor_reduce(s[:, i, :][:, bass.ds(q * B, B)], tmp4, AX.X, ALU.add))
            ch.leave(Q)
            for c in (roots, tanhs, logs):
                c.leave(Q)

            ts(sc(9), sc(0), -NEAR_UNIT, None, ALU.mult)
            v.tensor_scalar(sc(8), sc(0), SLOPE, None, ALU.mult).then_inc(S["gat_cols_turned"], 1)
            dve.wait_ge(S["src_broadcast"], 16)
            for half in range(2):
                if half:
                    dve.wait_ge(S["src_second_broadcast"], 16)
                with dve.Fori(0, 4) as i:
                    ch.enter(i, G + 1)
                    for g in range(G):
                        dve.wait_ge(S["signs_ready"], i * G + (4 * G * half + g + 1))
                        settle(dve, "dve_settled")
                        ch(v.tensor_tensor_reduce(masked_src, not_positive[g % 2], src_bc[:, half * HALF:(half + 1) * HALF],
                                                  FAR_UNIT, FAR, ALU.add, ALU.min, nmx[:, g:g + 1]))
                        v.sem_inc(S["signs_used"], 1)
                    ch(v.tensor_copy(s[:, 2 + half, :][:, bass.ds(i * G, G)], nmx[:, 0:G]))
                ch.leave(4)
            tt(sc(2), sc(2), sc(3), ALU.min)
            tt(sc(2), sc(1), sc(2), ALU.subtract)
            ts(sc(3), sc(2), SLOPE, None, ALU.mult)
            tt(sc(2), sc(2), sc(3), ALU.max)
            ts(sc(3), dg[:], 0.0, None, ALU.is_gt)
            tt(sc(3), sc(3), ecol[:, :, 3], ALU.add)
            ts(sc(3), sc(3), float(N) - 0.5, -BIG, ALU.is_gt, ALU.mult)
            tt(sc(2), sc(2), sc(3), ALU.max)
            tt(sc(4), sc(1), sc(2), ALU.subtract)
            ts(sc(5), sc(1), SLOPE, None, ALU.mult)
            v.tensor_tensor(sc(5), sc(5), sc(2), ALU.subtract).then_inc(S["gat_max_done"], 1)
            dve.wait_ge(S["first_dst_loaded"], 32)

            def scores(q, g):
                buf = gat_p[g % 4]
                for b in range(B):
                    dve.wait_ge(S["gat_slope_ready"], q * (G * B) + (B * g + b + 1))
                    v.scalar_tensor_tensor(buf[:, b, :], dst_all[0][:, bass.ds(q * CH, CH)], s[:, 0, B * g + b:B * g + b + 1],
                                           buf[:, b, :], ALU.add, ALU.max).then_inc(S["gat_logit_ready"], 1)

            def weights(q, g):
                dve.wait_ge(loaded[g], q * 16 + 16 * (used[PASS_GAT] + 1))
                dve.wait_ge(S["gat_exp_ready"], q * G + (g + 1))
                settle(dve, "dve_settled")
                v.scalar_tensor_tensor(gat_p[g % 4], groups[g], 0.0, gat_p[g % 4], ALU.is_gt, ALU.min)\
                    .then_inc(S["gat_w_ready"], 1)
                if g:
                    dve.wait_ge(S["gat_w_ready"], q * G + g)
                    v.sem_inc(freed[g - 1], 1)

            def attention(q, more, first=False):
                for g in range(G):
                    if g < G - 1:
                        scores(q, g + 1)
                    elif more:
                        if first:
                            dve.wait_ge(S["dst_loaded"], 32)
                        scores(q + 1, 0)
                    weights(q, g)
                dve.wait_ge(S["gat_w_ready"], q * G + G)
                v.sem_inc(freed[G - 1], 1)

            scores(0, 0)
            attention(0, True, True)
            with dve.Fori(1, Q - 1) as q:
                attention(q, True)
            attention(Q - 1, False)
            with dve.Fori(0, Q // 2) as qq:
                ch.enter(qq, 8)
                for q in (qq * 2, qq * 2 + 1):
                    tiles = bass.ds(q * B, B)
                    dve.wait_ge(S["chunk_stored"], q + (Q + 1))
                    dve.wait_ge(S["acc_used"], q + 1)
                    ts(c4(6), sc(6)[:, tiles], 1e-8, None, ALU.add)
                    ch(v.reciprocal(c4(6), c4(6)))
                    tt(ACC[:, tiles, :], ACC[:, tiles, :], wide4(c4(6)), ALU.mult)
                    v.tensor_scalar(TMP[:, tiles, :], ACC[:, tiles, :], 0.0, None, ALU.min).then_inc(S["exp_in"], 1)
                    ch(v.scalar_tensor_tensor(X[:, tiles, :], ACC[:, tiles, :], 0.0, X[:, tiles, :], ALU.max, ALU.add))
            ch.leave(Q // 2)
            with dve.Fori(0, Q // 2) as qq:
                ch.enter(qq, 2 * LINKS_5)
                for q in (qq * 2, qq * 2 + 1):
                    tiles = bass.ds(q * B, B)
                    dve.wait_ge(S["exp_out"], q + 1)
                    ch(v.scalar_tensor_tensor(X[:, tiles, :], TMP[:, tiles, :], -1.0, X[:, tiles, :], ALU.add, ALU.add))
                    variances(3, q)
                    factors(3, q)
            ch.leave(Q // 2)

            ts(tv[:], tv[:], 1e-8, -1.0, ALU.max, ALU.mult)
            v.tensor_scalar(sc(7), ev[:], tv[:, 0:1], None, ALU.mult).then_inc(S["exp_in"], 1)
            with dve.Fori(0, Q) as q:
                dve.wait_ge(S["chunk_turned"], q + (3 * Q + 1))
                settle(dve, "dve_settled")
                x4 = X[:, bass.ds(q * B, B), :]
                v.tensor_tensor(x4, x4, banks[1][:].rearrange("p (b c) -> p b c", b=B), ALU.add).then_inc(S["ready_to_store"], 1)


def kernel(**inputs):
    import numpy as np
    import ml_dtypes
    import concourse.bacc as bacc
    from concourse.bass_utils import run_bass_kernel_spmd as run

    f = {k: np.asarray(v) for k, v in inputs.items()}

    def cols(a, n):
        return np.ascontiguousarray(a.reshape(n, P).T)

    def row(a):
        return np.ascontiguousarray(np.broadcast_to(a.reshape(1, C), (P, C)))

    not_i = np.ones((P, 15 * P), ml_dtypes.bfloat16)
    not_i[:, 7 * P:8 * P] = 1 - np.eye(P)
    sel = np.zeros((P, 8), np.float32)
    sel[0, 3] = 1
    for part in range(3):
        for h in range(HEADS):
            a1, a2 = 1 + 6 * part + 2 * h, 2 + 6 * part + 2 * h
            sel[a1, h] = sel[a2, 4 + h] = 1
            sel[NEG0 + a2, h] = sel[NEG0 + a1, 4 + h] = 1
    e, n = "L0_gnn_edge_", "L0_gnn_node_"
    arrays = {
        "x": f["x"], "adj": f["adj"], "adjT": np.ascontiguousarray(f["adj"].T),
        "diag": cols(np.diagonal(f["adj"]), T),
        "gatW": np.ascontiguousarray(f["L0_gnn_gat_W"].transpose(1, 0, 2)).reshape(C, HEADS * C),
        "gatWT": np.ascontiguousarray(f["L0_gnn_gat_W"].transpose(2, 0, 1)).reshape(C, HEADS * C),
        "gata": np.ascontiguousarray(f["L0_gnn_gat_a"].reshape(HEADS, 2, C).transpose(2, 0, 1)).reshape(C, 2 * HEADS),
        "wih": np.stack([f[e + "Wih"].T, f[n + "Wih"].T]), "whh": np.stack([f[e + "Whh"].T, f[n + "Whh"].T]),
        "bih": np.stack([cols(f[e + "bih"], 3), cols(f[n + "bih"], 3)]),
        "bhh": np.stack([cols(f[e + "bhh"], 3), cols(f[n + "bhh"], 3)]),
        "w1": np.ascontiguousarray(f["L1_gnn_weight"].T), "bias1": row(f["L1_gnn_bias"]),
        "w2": np.ascontiguousarray(f["L2_gnn_W"].T), "att_s": row(f["L2_gnn_attn_src"]),
        "att_d": row(f["L2_gnn_attn_dst"]),
        "evals": cols(f["L3_gnn_evals"], T), "t_in": np.ascontiguousarray(np.broadcast_to(f["L3_gnn_t"].reshape(1, 1), (P, 1))),
        "ident": np.eye(P, dtype=np.float32), "not_i": not_i, "sel": sel,
    }
    nc = bacc.Bacc("TRN2", target_bir_lowering=False, num_devices=1)
    aps = [nc.dram_tensor(f"in_{k}", a.shape, mybir.dt.from_np(a.dtype), kind="ExternalInput").ap() for k, a in arrays.items()]
    out = nc.dram_tensor("out_x", (N, C), F32, kind="ExternalOutput").ap()
    build(nc, *aps, out)
    r = run(nc, [{f"in_{k}": a for k, a in arrays.items()}], core_ids=[0])
    return r.results[0]["out_x"]
```
